# Optimizing a Trainium2 kernel written in Bass

```python
import numpy as np
import jax
import jax.numpy as jnp

def _softmax(x, axis=-1):
    return jax.nn.softmax(x, axis=axis)

def _gelu(x):
    return jax.nn.gelu(x, approximate=True)

def _silu(x):
    return jax.nn.silu(x)

def _sigmoid(x):
    return jax.nn.sigmoid(x)

def _layernorm(x, axis=-1, eps=1e-05):
    m = jnp.mean(x, axis=axis, keepdims=True)
    v = jnp.var(x, axis=axis, keepdims=True)
    return (x - m) / jnp.sqrt(v + eps)

def _scatter_add(tgt, idx, src, axis=0):
    return tgt.at[idx].add(src)

def _segment_sum(src, seg, n):
    return jax.ops.segment_sum(src, seg, n)
kernel_name = 'mk_seq_postln_d1_jaxref_r4_ee6250'

def setup_inputs(seed: int=0):
    np.random.seed(seed)
    _w = jnp.asarray

    def _L0_attn_setup():
        import jax, jax.numpy as jnp
        import numpy as np
        H = 256
        D = 64
        CHUNK = 128
        LR = 0.1
        GRAD_SCALE = 0.1
        MAX_GRAD_NORM = 1.0
        EPS = 1e-06
        P = 2 * D * D

        def _xavier(k, shape, gain=0.1):
            fan_out, fan_in = shape
            a = gain * np.sqrt(6.0 / (fan_in + fan_out))
            return jax.random.uniform(k, shape, jnp.float32, -a, a)

        def _causal_dwconv(x, w, b):
            T = x.shape[1]
            xp = jnp.pad(x, ((0, 0), (3, 0), (0, 0)))
            y = b
            for j in range(4):
                y = y + xp[:, j:j + T, :] * w[:, j]
            return y

        def _mem_loss(p, k_t, v_t):
            W1 = p[:D * D].reshape(D, D)
            W2 = p[D * D:].reshape(D, D)
            pred = jax.nn.silu(k_t @ W1.T) @ W2.T
            return jnp.sum((pred - v_t) ** 2)
        _grad_fn = jax.vmap(jax.vmap(jax.grad(_mem_loss), in_axes=(None, 0, 0)), in_axes=(0, 0, 0))

        def _forward(hidden, Wk, Wv, Wq, Wo, ckw, ckb, cvw, cvb, cqw, cqb, mW1, mW2, aW, ab, eW, eb, tW, tb, norm_g, gW, gb):
            B, S, _ = hidden.shape
            k = _causal_dwconv(hidden @ Wk.T, ckw, ckb)
            v = _causal_dwconv(hidden @ Wv.T, cvw, cvb)
            q = _causal_dwconv(hidden @ Wq.T, cqw, cqb)
            alpha = (jax.nn.sigmoid(hidden @ aW.T + ab) * 0.1).mean(-1)
            eta = (jax.nn.sigmoid(hidden @ eW.T + eb) * 0.9 + 0.05).mean(-1)
            theta = (jax.nn.softplus(hidden @ tW.T + tb) * LR).mean(-1)
            W_state = jnp.tile(jnp.concatenate([mW1.ravel(), mW2.ravel()])[None], (B, 1))
            S_state = jnp.zeros_like(W_state)

            def step(carry, xs):
                Sm, Wm = carry
                gt, et, tt, at = xs
                Sm = et[:, None] * Sm - tt[:, None] * gt
                Wm = (1.0 - at[:, None]) * Wm + Sm
                return ((Sm, Wm), Wm)
            outs = []
            for c0 in range(0, S, CHUNK):
                sl = slice(c0, c0 + CHUNK)
                g = _grad_fn(W_state, k[:, sl], v[:, sl]) * GRAD_SCALE
                gn = jnp.maximum(jnp.linalg.norm(g, axis=-1, keepdims=True), EPS)
                g = g * jnp.minimum(MAX_GRAD_NORM / gn, 1.0)
                g = jax.lax.stop_gradient(g)
                xs = (jnp.swapaxes(g, 0, 1), eta[:, sl].T, theta[:, sl].T, alpha[:, sl].T)
                (S_state, W_state), Wtraj = jax.lax.scan(step, (S_state, W_state), xs)
                Wtraj = jnp.swapaxes(Wtraj, 0, 1)
                T = Wtraj.shape[1]
                W1t = Wtraj[..., :D * D].reshape(B, T, D, D)
                W2t = Wtraj[..., D * D:].reshape(B, T, D, D)
                h = jax.nn.silu(jnp.einsum('btd,btod->bto', q[:, sl], W1t))
                outs.append(jnp.einsum('bto,btpo->btp', h, W2t))
            retrieved = jnp.concatenate(outs, axis=1)
            out = retrieved @ Wo.T
            out = out * jax.lax.rsqrt(jnp.mean(out * out, -1, keepdims=True) + EPS) * norm_g
            gate = hidden @ gW.T + gb
            return out * gate
        key = jax.random.key(seed)
        ks = jax.random.split(key, 24)
        B, S = (1, 256)
        return {'hidden': jax.random.normal(ks[0], (B, S, H), jnp.float32), 'Wk': _xavier(ks[1], (D, H)), 'Wv': _xavier(ks[2], (D, H)), 'Wq': _xavier(ks[3], (D, H)), 'Wo': _xavier(ks[4], (H, D)), 'ckw': jax.random.normal(ks[5], (D, 4), jnp.float32) * 0.05, 'ckb': jnp.zeros((D,), jnp.float32), 'cvw': jax.random.normal(ks[6], (D, 4), jnp.float32) * 0.05, 'cvb': jnp.zeros((D,), jnp.float32), 'cqw': jax.random.normal(ks[7], (D, 4), jnp.float32) * 0.05, 'cqb': jnp.zeros((D,), jnp.float32), 'mW1': _xavier(ks[8], (D, D)), 'mW2': _xavier(ks[9], (D, D)), 'aW': jax.random.normal(ks[10], (D, H), jnp.float32) * 0.02, 'ab': jnp.zeros((D,), jnp.float32), 'eW': jax.random.normal(ks[11], (D, H), jnp.float32) * 0.02, 'eb': jnp.zeros((D,), jnp.float32), 'tW': jax.random.normal(ks[12], (D, H), jnp.float32) * 0.02, 'tb': jnp.zeros((D,), jnp.float32), 'norm_g': jnp.ones((H,), jnp.float32), 'gW': jnp.zeros((H, H), jnp.float32), 'gb': jnp.ones((H,), jnp.float32)}
    _L0_attn_in = _L0_attn_setup()

    def _L0_ffn_setup():
        import jax, jax.numpy as jnp
        import numpy as np
        B, S, H, E = (2, 2048, 256, 8)
        SCALE = 0.5
        key = jax.random.key(seed)
        k1, k2 = jax.random.split(key)
        x = jax.random.normal(k1, (B, S, H), dtype=jnp.float32)
        gate_w = jax.random.normal(k2, (E, H), dtype=jnp.float32) * 0.02
        coeff = SCALE * (1.0 + 0.05 * jnp.arange(E, dtype=jnp.float32))
        expert_w = coeff[:, None, None] * jnp.eye(H, dtype=jnp.float32)
        return {'x': x, 'gate_w': gate_w, 'expert_w': expert_w}
    _L0_ffn_in = _L0_ffn_setup()
    _d = {'L0_attn_hidden': _L0_attn_in['hidden'], 'L0_attn_Wk': _L0_attn_in['Wk'], 'L0_attn_Wv': _L0_attn_in['Wv'], 'L0_attn_Wq': _L0_attn_in['Wq'], 'L0_attn_Wo': _L0_attn_in['Wo'], 'L0_attn_ckw': _L0_attn_in['ckw'], 'L0_attn_ckb': _L0_attn_in['ckb'], 'L0_attn_cvw': _L0_attn_in['cvw'], 'L0_attn_cvb': _L0_attn_in['cvb'], 'L0_attn_cqw': _L0_attn_in['cqw'], 'L0_attn_cqb': _L0_attn_in['cqb'], 'L0_attn_mW1': _L0_attn_in['mW1'], 'L0_attn_mW2': _L0_attn_in['mW2'], 'L0_attn_aW': _L0_attn_in['aW'], 'L0_attn_ab': _L0_attn_in['ab'], 'L0_attn_eW': _L0_attn_in['eW'], 'L0_attn_eb': _L0_attn_in['eb'], 'L0_attn_tW': _L0_attn_in['tW'], 'L0_attn_tb': _L0_attn_in['tb'], 'L0_attn_norm_g': _L0_attn_in['norm_g'], 'L0_attn_gW': _L0_attn_in['gW'], 'L0_attn_gb': _L0_attn_in['gb'], 'L0_ffn_gate_w': _L0_ffn_in['gate_w'], 'L0_ffn_expert_w': _L0_ffn_in['expert_w']}
    _x0 = _d['L0_attn_hidden']
    _d['L0_attn_hidden'] = jax.random.normal(jax.random.fold_in(jax.random.key(seed), 1), (16, 512, 256), dtype=_x0.dtype)
    del _x0
    return _d

def reference(L0_attn_hidden, L0_attn_Wk, L0_attn_Wv, L0_attn_Wq, L0_attn_Wo, L0_attn_ckw, L0_attn_ckb, L0_attn_cvw, L0_attn_cvb, L0_attn_cqw, L0_attn_cqb, L0_attn_mW1, L0_attn_mW2, L0_attn_aW, L0_attn_ab, L0_attn_eW, L0_attn_eb, L0_attn_tW, L0_attn_tb, L0_attn_norm_g, L0_attn_gW, L0_attn_gb, L0_ffn_gate_w, L0_ffn_expert_w):

    def _L0_attn_ref(hidden, Wk, Wv, Wq, Wo, ckw, ckb, cvw, cvb, cqw, cqb, mW1, mW2, aW, ab, eW, eb, tW, tb, norm_g, gW, gb):
        import jax, jax.numpy as jnp
        import numpy as np
        H = 256
        D = 64
        CHUNK = 128
        LR = 0.1
        GRAD_SCALE = 0.1
        MAX_GRAD_NORM = 1.0
        EPS = 1e-06
        P = 2 * D * D

        def _xavier(k, shape, gain=0.1):
            fan_out, fan_in = shape
            a = gain * np.sqrt(6.0 / (fan_in + fan_out))
            return jax.random.uniform(k, shape, jnp.float32, -a, a)

        def _causal_dwconv(x, w, b):
            T = x.shape[1]
            xp = jnp.pad(x, ((0, 0), (3, 0), (0, 0)))
            y = b
            for j in range(4):
                y = y + xp[:, j:j + T, :] * w[:, j]
            return y

        def _mem_loss(p, k_t, v_t):
            W1 = p[:D * D].reshape(D, D)
            W2 = p[D * D:].reshape(D, D)
            pred = jax.nn.silu(k_t @ W1.T) @ W2.T
            return jnp.sum((pred - v_t) ** 2)
        _grad_fn = jax.vmap(jax.vmap(jax.grad(_mem_loss), in_axes=(None, 0, 0)), in_axes=(0, 0, 0))

        def _forward(hidden, Wk, Wv, Wq, Wo, ckw, ckb, cvw, cvb, cqw, cqb, mW1, mW2, aW, ab, eW, eb, tW, tb, norm_g, gW, gb):
            B, S, _ = hidden.shape
            k = _causal_dwconv(hidden @ Wk.T, ckw, ckb)
            v = _causal_dwconv(hidden @ Wv.T, cvw, cvb)
            q = _causal_dwconv(hidden @ Wq.T, cqw, cqb)
            alpha = (jax.nn.sigmoid(hidden @ aW.T + ab) * 0.1).mean(-1)
            eta = (jax.nn.sigmoid(hidden @ eW.T + eb) * 0.9 + 0.05).mean(-1)
            theta = (jax.nn.softplus(hidden @ tW.T + tb) * LR).mean(-1)
            W_state = jnp.tile(jnp.concatenate([mW1.ravel(), mW2.ravel()])[None], (B, 1))
            S_state = jnp.zeros_like(W_state)

            def step(carry, xs):
                Sm, Wm = carry
                gt, et, tt, at = xs
                Sm = et[:, None] * Sm - tt[:, None] * gt
                Wm = (1.0 - at[:, None]) * Wm + Sm
                return ((Sm, Wm), Wm)
            outs = []
            for c0 in range(0, S, CHUNK):
                sl = slice(c0, c0 + CHUNK)
                g = _grad_fn(W_state, k[:, sl], v[:, sl]) * GRAD_SCALE
                gn = jnp.maximum(jnp.linalg.norm(g, axis=-1, keepdims=True), EPS)
                g = g * jnp.minimum(MAX_GRAD_NORM / gn, 1.0)
                g = jax.lax.stop_gradient(g)
                xs = (jnp.swapaxes(g, 0, 1), eta[:, sl].T, theta[:, sl].T, alpha[:, sl].T)
                (S_state, W_state), Wtraj = jax.lax.scan(step, (S_state, W_state), xs)
                Wtraj = jnp.swapaxes(Wtraj, 0, 1)
                T = Wtraj.shape[1]
                W1t = Wtraj[..., :D * D].reshape(B, T, D, D)
                W2t = Wtraj[..., D * D:].reshape(B, T, D, D)
                h = jax.nn.silu(jnp.einsum('btd,btod->bto', q[:, sl], W1t))
                outs.append(jnp.einsum('bto,btpo->btp', h, W2t))
            retrieved = jnp.concatenate(outs, axis=1)
            out = retrieved @ Wo.T
            out = out * jax.lax.rsqrt(jnp.mean(out * out, -1, keepdims=True) + EPS) * norm_g
            gate = hidden @ gW.T + gb
            return out * gate
        return _forward(hidden, Wk, Wv, Wq, Wo, ckw, ckb, cvw, cvb, cqw, cqb, mW1, mW2, aW, ab, eW, eb, tW, tb, norm_g, gW, gb)

    def _L0_ffn_ref(x, gate_w, expert_w):
        import jax, jax.numpy as jnp
        import numpy as np
        B, S, H, E = (2, 2048, 256, 8)
        SCALE = 0.5
        scores = jnp.einsum('bsh,eh->bse', x, gate_w)
        chosen = jnp.argmax(scores, axis=-1)
        onehot = jax.nn.one_hot(chosen, gate_w.shape[0], dtype=x.dtype)
        expert_out = jnp.einsum('bsh,efh->bsef', x, expert_w)
        return x + jnp.einsum('bsef,bse->bsf', expert_out, onehot)
    x = L0_attn_hidden
    x = _layernorm(x + _L0_attn_ref(x, L0_attn_Wk, L0_attn_Wv, L0_attn_Wq, L0_attn_Wo, L0_attn_ckw, L0_attn_ckb, L0_attn_cvw, L0_attn_cvb, L0_attn_cqw, L0_attn_cqb, L0_attn_mW1, L0_attn_mW2, L0_attn_aW, L0_attn_ab, L0_attn_eW, L0_attn_eb, L0_attn_tW, L0_attn_tb, L0_attn_norm_g, L0_attn_gW, L0_attn_gb), axis=-1)
    x = _layernorm(x + _L0_ffn_ref(x, L0_ffn_gate_w, L0_ffn_expert_w), axis=-1)
    return x

_drawn_inputs = setup_inputs


def setup_inputs(seed=0):
    import zlib

    import numpy as np

    out = dict(_drawn_inputs(seed))
    spreads = {'L0_attn_ckb': (0.0, 0.8),
     'L0_attn_cvb': (0.0, 0.8),
     'L0_attn_cqb': (0.0, 0.8),
     'L0_attn_ab': (0.0, 2.0),
     'L0_attn_eb': (0.0, 2.0),
     'L0_attn_tb': (0.0, 0.8),
     'L0_attn_norm_g': (1.0, 0.6),
     'L0_attn_gW': (0.0, 0.8),
     'L0_attn_gb': (1.0, 0.6)}
    factors = {'L0_attn_Wk': 8.0,
     'L0_attn_Wv': 8.0,
     'L0_attn_Wq': 8.0,
     'L0_attn_Wo': 8.0,
     'L0_attn_ckw': 8.0,
     'L0_attn_cvw': 8.0,
     'L0_attn_cqw': 8.0,
     'L0_attn_mW1': 8.0,
     'L0_attn_mW2': 7.912,
     'L0_attn_aW': 8.0,
     'L0_attn_eW': 8.0,
     'L0_attn_tW': 8.0,
     'L0_ffn_gate_w': 64.0}
    for name, (base, spread) in spreads.items():
        noise = np.random.default_rng([zlib.crc32(name.encode()), seed]).standard_normal(out[name].shape)
        drawn = base * np.exp(spread * noise) if base else spread * noise
        out[name] = jnp.asarray(drawn.astype(out[name].dtype))
    for name, factor in factors.items():
        out[name] = (out[name] * factor).astype(out[name].dtype)
    return out
```

```python
import concourse.bass as bass
from concourse import mybir
from contextlib import ExitStack

F32 = mybir.dt.float32
BF16 = mybir.dt.bfloat16
I32 = mybir.dt.int32
ALU = mybir.AluOpType
ACT = mybir.ActivationFunctionType
AX = mybir.AxisListType

P = 128
B = 16
S = 512
H = 256
KH = H // P
D = 64
NC = S // P
G = 4
NB = B // G
TOK = B * S
NE = 8
REGION = TOK + P
NT = TOK // P + NE
ROW = H + 4
UNROLL = 4
NO_TOKEN = 2.0 * TOK
EPS_RMS = 1e-6
EPS_LN = 1e-5
GRAD_SCALE = 0.1
LR = 0.1


def spread(ap, axis, n):
    shape = list(ap.shape)
    shape[axis] = n
    return ap.broadcast_to(shape)


class Marks:

    def __init__(self, nc, ctx, prefix, plan):
        self.nc = nc
        self.engines = dict(pe=nc.tensor, act=nc.scalar, dve=nc.vector, pool=nc.gpsimd, sp=nc.sync)
        self.sem = {e: ctx.enter_context(nc.semaphore(f"{prefix}_{e}")) for e in ("pe", "act", "dve", "pool")}
        self.plan = plan
        self.count = {e: 0 for e in self.sem}
        self.at = {}
        self.lap = None
        self.passed = ctx.enter_context(nc.semaphore(f"{prefix}_passed"))

    def start_loop(self):
        for e, s in self.sem.items():
            self.engines[e].sem_inc(s, self.per_lap(e))

    def per_lap(self, e):
        return self.plan["count"][e] if self.plan else 1

    def mark(self, e, name, instruction):
        instruction.then_inc(self.sem[e], 1)
        self.count[e] += 1
        assert name not in self.at, name
        self.at[name] = (e, self.count[e])

    def wait(self, e, *names):
        need = {}
        for name in names:
            if name in self.at:
                who, n = self.at[name]
                n += self.per_lap(who)
            else:
                who, n = self.plan["at"][name] if self.plan else ("pe", 1)
            need[who] = max(need.get(who, 0), n)
        for who, n in need.items():
            self.engines[e].wait_ge(self.sem[who], self.lap * self.per_lap(who) + n)

    def apart(self, e):
        self.engines[e].sem_inc(self.passed, 1)

    def finish(self):
        return dict(count=dict(self.count), at=dict(self.at))


class Slots:

    def __init__(self, name, buffers, plan):
        self.name, self.buffers, self.n = name, buffers, 0
        self.last = dict(plan["slots"][name]) if plan else {i: None for i in range(len(buffers))}
        self.plan = plan

    def take(self):
        i = self.n % len(self.buffers)
        self.n += 1
        return i, self.buffers[i], self.last[i]

    def freed_by(self, i, name):
        self.last[i] = name


def build(nc, dram, plan):
    plans = {}
    out = dram["out"]
    with ExitStack() as ctx:
        def sb(name, shape, dt=F32):
            return ctx.enter_context(nc.sbuf_tensor(name, shape, dt))

        def sem(name):
            return ctx.enter_context(nc.semaphore(name))

        sorted_rows = nc.dram_tensor("sorted_rows", [NE * REGION + P, ROW], F32).ap()

        w_kv = sb("w_kv", [P, KH, P])
        w_q = sb("w_q", [P, KH, P])
        w_ae = sb("w_ae", [P, KH, P])
        NG = H + D
        w_gt = sb("w_gt", [P, KH, NG])
        bias_gt = sb("bias_gt", [P, NG])
        norm_g = sb("norm_g", [P, H])
        w_o = sb("w_o", [D, H])
        conv_w = sb("conv_w", [P, 2, 4])
        conv_b = sb("conv_b", [P, 2])
        bias_ae = sb("bias_ae", [P, 1])
        w_route = sb("w_route", [P, KH, NE])
        w_expert = sb("w_expert", [P, KH, NE, H])
        ident = sb("ident", [P, P])
        ident_nb = sb("ident_nb", [P, NB, P])
        ident_g = sb("ident_g", [P, 2, D])
        ones_a = sb("ones_a", [P, P])
        ones_e = sb("ones_e", [P, P])
        ones_bf = sb("ones_bf", [P, P], BF16)
        before = sb("before", [P, P], BF16)
        rank = sb("rank", [P, NE])
        region0 = sb("region0", [P, NE])
        token = sb("token", [P, G * NB])
        minus_half = sb("minus_half", [P, 8])
        tile_no = sb("tile_no", [P, NT])
        pad_row = sb("pad_row", [P, ROW])

        state = [sb(f"state{g}", [P, NB, 3, D]) for g in range(G)]
        w2 = [sb(f"w2_{g}", [D, NB, D]) for g in range(G)]
        raw = [sb(f"raw{g}", [P, 2, NB, P + 3]) for g in range(G)]
        routed = sb("routed", [P, NE], BF16)

        banks = [ctx.enter_context(nc.psum_tensor(f"bank{i}", [P, 512], F32)) for i in range(8)]

        s_load = sem("s_load")
        loads = [
            (w_kv[:, :, :], dram["w_kv"].rearrange("(k p) m -> p k m", p=P)),
            (w_q[:, :, :], dram["w_q"].rearrange("(k p) m -> p k m", p=P)),
            (w_ae[:, :, :], dram["w_ae"].rearrange("(k p) m -> p k m", p=P)),
            (w_gt[:, :, :], dram["w_gt"].rearrange("(k p) m -> p k m", p=P)),
            (bias_gt[:, :], dram["bias_gt"]),
            (norm_g[:, :], dram["norm_g"]),
            (w_o[:, :], dram["w_o"]),
            (conv_w[:, :, :], dram["conv_w"]),
            (conv_b[:, :], dram["conv_b"]),
            (bias_ae[:, :], dram["bias_ae"]),
            (w_route[:, :, :], dram["w_route"].rearrange("(k p) m -> p k m", p=P)),
        ]
        for g in range(G):
            loads += [(state[g][0:D, :, :, :], dram["state0"]), (w2[g][:, :, :], dram["w2_0"])]
        loads += [(w_expert[:, k, :, :], dram["w_expert"][:, k * P:(k + 1) * P, :].rearrange("e p f -> p e f"))
                  for k in range(KH)]
        for dst, src in loads:
            nc.scalar.dma_start(dst, src).then_inc(s_load, 16)

        s_const = sem("s_const")
        n_const = 0

        def pool_const(instruction):
            nonlocal n_const
            n_const += 1
            instruction.then_inc(s_const, 1)
            nc.gpsimd.wait_ge(s_const, n_const)

        pool = nc.gpsimd
        pool_const(pool.memset(ident[:, :], 0.0))
        pool_const(pool.affine_select(out=ident[:, :], in_=ident[:, :], compare_op=ALU.not_equal, fill=1.0,
                                      base=0, pattern=[[-1, P]], channel_multiplier=1))
        pool_const(pool.memset(ident_nb[:, :, :], 0.0))
        pool_const(pool.affine_select(out=ident_nb[:, :, :], in_=ident_nb[:, :, :], compare_op=ALU.not_equal,
                                      fill=1.0, base=0, pattern=[[0, NB], [-1, P]], channel_multiplier=1))
        pool_const(pool.memset(ident_g[:, :, :], 0.0))
        pool_const(pool.affine_select(out=ident_g[:, 0, :], in_=ident_g[:, 0, :], compare_op=ALU.not_equal,
                                      fill=1.0, base=0, pattern=[[-1, D]], channel_multiplier=1))
        pool_const(pool.affine_select(out=ident_g[:, :, :], in_=ident_g[:, :, :], compare_op=ALU.not_equal,
                                      fill=1.0, base=-D, pattern=[[0, 2], [-1, D]], channel_multiplier=1))
        pool_const(pool.memset(ones_a[:, :], 0.0))
        pool_const(pool.memset(ones_a[0:D, :], 1.0))
        pool_const(pool.memset(ones_e[:, :], 0.0))
        pool_const(pool.memset(ones_e[D:P, :], 1.0))
        pool_const(pool.memset(ones_bf[:, :], 1.0))
        pool_const(pool.affine_select(out=before[:, :], in_=ones_bf[:, :], compare_op=ALU.is_gt, fill=0.0,
                                      base=0, pattern=[[1, P]], channel_multiplier=-1))
        pool_const(pool.iota(rank[:, :], pattern=[[-1, NE]], base=NE, channel_multiplier=0,
                             allow_small_or_imprecise_dtypes=True))
        pool_const(pool.iota(region0[:, :], pattern=[[REGION, NE]], base=0, channel_multiplier=0,
                             allow_small_or_imprecise_dtypes=True))
        pool_const(pool.iota(token[:, :], pattern=[[S, G * NB]], base=0, channel_multiplier=1,
                             allow_small_or_imprecise_dtypes=True))
        pool_const(pool.iota(tile_no[:, :], pattern=[[1, NT]], base=0, channel_multiplier=0,
                             allow_small_or_imprecise_dtypes=True))
        pool_const(pool.memset(minus_half[:, :], -0.5))
        pool_const(pool.memset(pad_row[:, :], 0.0))
        pool_const(pool.memset(pad_row[:, H:H + 1], NO_TOKEN))
        pool_const(pool.memset(routed[:, :], 0.0))
        for g in range(G):
            pool_const(pool.memset(state[g][D:P, :, :, :], 0.0))
            pool_const(pool.memset(raw[g][:, :, :, :], 0.0))

        NBUF = 2
        t_first = [sb(f"t_first{i}", [P, NB, P]) for i in range(NBUF)]
        for i in range(NBUF):
            pool_const(pool.memset(t_first[i][:, :, :], 0.0))

        s_prep = sem("s_prep")
        nc.vector.wait_ge(s_load, 16 * len(loads))
        for k in range(KH):
            nc.vector.tensor_tensor(w_gt[:, k, 0:H], w_gt[:, k, 0:H], norm_g[:, :], ALU.mult).then_inc(s_prep, 1)
        nc.vector.tensor_tensor(bias_gt[:, 0:H], bias_gt[:, 0:H], norm_g[:, :], ALU.mult).then_inc(s_prep, 1)
        nc.vector.tensor_scalar(bias_ae[:, :], bias_ae[:, :], 0.5, None, ALU.mult).then_inc(s_prep, 1)
        n_prep = KH + 2
        for e in (nc.tensor, nc.scalar, nc.vector, nc.gpsimd, nc.sync):
            e.wait_ge(s_load, 16 * len(loads))
            e.wait_ge(s_const, n_const)
            e.wait_ge(s_prep, n_prep)

        with ExitStack() as inner:
            sb1 = lambda name, shape, dt=F32: inner.enter_context(nc.sbuf_tensor(name, shape, dt))
            loop1(nc, ctx, sb1, sem, dict(locals()), plan and plan["loop1"], plans)
        tiles(nc, ctx, sb, sem, dict(locals()))
        loop2(nc, ctx, sb, sem, dict(locals()), plan and plan["loop2"], plans)
    return plans


def loop1(nc, ctx, sb, sem, v, plan, plans):
    dram, banks = v["dram"], v["banks"]
    w_kv, w_q, w_ae, w_gt, bias_gt, w_o = (v[n] for n in ("w_kv", "w_q", "w_ae", "w_gt", "bias_gt", "w_o"))
    conv_w, conv_b, bias_ae, w_route = (v[n] for n in ("conv_w", "conv_b", "bias_ae", "w_route"))
    ident, ident_nb, ident_g, ones_a, ones_e = (v[n] for n in ("ident", "ident_nb", "ident_g", "ones_a", "ones_e"))
    ones_bf, before, rank, region0, token = (v[n] for n in ("ones_bf", "before", "rank", "region0", "token"))
    minus_half, state, w2, raw, routed = (v[n] for n in ("minus_half", "state", "w2", "raw", "routed"))
    t_first, sorted_rows = v["t_first"], v["sorted_rows"]
    NG = H + D

    pe, act, dve, pool, sp = nc.tensor, nc.scalar, nc.vector, nc.gpsimd, nc.sync
    M = Marks(nc, ctx, "l1", plan)
    mark, wait = M.mark, M.wait

    def two(name, shape, dt=F32):
        return [sb(f"{name}{i}", shape, dt) for i in range(2)]

    NX = 4
    x = [sb(f"x{i}", [P, NB, H]) for i in range(NX)]
    s_x = [sem(f"s_x{i}") for i in range(NX)]
    xt = sb("xt", [P, KH, NB * P])
    kv = two("kv", [P, NB, P])
    q = two("q", [P, NB, P])
    tanh_ae = sb("tanh_ae", [P, NB * P])
    decay = sb("decay", [P, 3, NB, P])
    resp = two("resp", [P, 2, NB, P])
    carry = two("carry", [P, 2, NB, P])
    gt = two("gt", [P, NB, NG])
    soft = sb("soft", [P, 3, NB, D])
    theta = two("theta", [P, NB])
    kv_n = two("kv_n", [P, 2, NB, D])
    kq = two("kq", [P, NB, P])
    ab_q = two("ab_q", [P, NB, P])
    g_dec = two("g_dec", [P, NB, 2, D])
    ck = two("ck", [P, NB, 2, D])
    sq_k = two("sq_k", [P, NB, D])
    norms = two("norms", [P, 4, NB])
    t_z = sb("t_z", [P, NB, D])
    sig = sb("sig", [P, NB, D])
    h = sb("h", [P, NB, D])
    h_t = sb("h_t", [D, NB, P])
    grad = sb("grad", [P, 2, NB, D])
    dz_w = sb("dz_w", [P, NB, 2, D])
    e_w = sb("e_w", [P, NB, D])
    e_t = sb("e_t", [D, NB, P])
    ds = sb("ds", [P, 2, NB, D])
    sq = sb("sq", [P, 3, NB, D])
    ch = sb("ch", [P, NB, 2, D])
    small = sb("small", [P, 8, NB])
    t_q = sb("t_q", [P, NB, P])
    hq = sb("hq", [P, NB, P])
    hh = sb("hh", [P, NB, P])
    ab_h = sb("ab_h", [P, NB, P])
    ret = two("ret", [D, NB, P])
    junk = sb("junk", [P, H])
    ssq = sb("ssq", [P, NB])
    rms = sb("rms", [P, 2, NB])
    y = two("y", [P, NB, H])
    stats = sb("stats", [P, NB, 6])
    mv = sb("mv", [P, NB, 2])
    rstd = sb("rstd", [P, 2, NB])
    rows = two("rows", [P, NB, ROW])
    rows_t = sb("rows_t", [P, KH, NB * P])
    best = sb("best", [P, 2, NB])
    pick = sb("pick", [P, 3, NB, NE])
    onehot = sb("onehot", [P, NB, NE], BF16)
    total = sb("total", [P, NE])
    where = sb("where", [P, 2, NB, NE])
    where_f = sb("where_f", [P, NB])
    index = two("index", [P, NB], I32)
    s_scatter = [sem(f"s_scatter{i}") for i in range(2)]

    pro = Slots("pro", banks[0:3], plan)
    core = Slots("core", banks[3:6], plan)
    epi = Slots("epi", banks[6:8], plan)

    def grab(slots, engine="pe"):
        i, bank, last = slots.take()
        if last or plan is None:
            wait(engine, last)
        return i, bank

    hidden = dram["hidden"].rearrange("b (c s) h -> c s b h", s=P)

    def prologue(c, g):
        n = lambda name, g_=g: f"{name}.{g_}"
        before_ = lambda name: f"{name}.{(g - 2) % G}"
        i2 = g % 2
        X, KV, Q = x[g % NX], kv[i2], q[i2]
        wait("sp", n("res"))
        sp.dma_start(X[:, :, :], hidden[c][:, g * NB:(g + 1) * NB, :]).then_inc(s_x[g % NX], 16)
        pe.wait_ge(s_x[g % NX], c * 16 + 16)
        for k in range(KH):
            i, bank = grab(pro)
            for b in range(NB):
                ins = pe.transpose(bank[:, b * P:(b + 1) * P], X[:, b, k * P:(k + 1) * P], ident[:, :])
            mark("pe", n(f"xt_ps{k}"), ins)
            wait("act", n(f"xt_ps{k}"))
            wait("act", f"gt_ps{NB - 1}.{(g - 1) % G}", f"ae_ps.{(g - 1) % G}")
            mark("act", n(f"xt{k}"), act.activation(xt[:, k, :], bank[:, :], ACT.Copy))
            pro.freed_by(i, n(f"xt{k}"))
            yield
        wait("dve", n("conv_kv"), n("conv_q"))
        mark("dve", n("halo"), dve.tensor_copy(raw[g][:, :, :, 0:3], raw[g][:, :, :, P:P + 3]))
        wait("pe", n("xt0"), n("xt1"))
        for j, (name, w) in enumerate((("kv", w_kv), ("q", w_q))):
            i, bank = grab(pro)
            for k in range(KH):
                ins = pe.matmul(bank[:, :], w[:, k, :], xt[:, k, :], start=k == 0, stop=k == KH - 1)
            mark("pe", n(f"{name}_ps"), ins)
            wait("act", n(f"{name}_ps"), n("halo"))
            mark("act", n(f"{name}_raw"),
                 act.activation(raw[g][:, j, :, 3:P + 3], bank[:, :].rearrange("p (b t) -> p b t", b=NB), ACT.Copy))
            pro.freed_by(i, n(f"{name}_raw"))
            yield
        i, bank = grab(pro)
        for k in range(KH):
            ins = pe.matmul(bank[:, :], w_ae[:, k, :], xt[:, k, :], start=k == 0, stop=k == KH - 1)
        mark("pe", n("ae_ps"), ins)
        wait("act", n("ae_ps"))
        wait("act", f"sum_e.{(g - 1) % G}")
        mark("act", n("tanh_ae"), act.activation(tanh_ae[:, :], bank[:, :], ACT.Tanh, bias=bias_ae[:, 0:1], scale=0.5))
        pro.freed_by(i, n("tanh_ae"))
        yield
        for j, (name, dst) in enumerate((("kv", KV), ("q", Q))):
            wait("dve", n(f"{name}_raw"), n("halo"))
            if name == "kv":
                wait("dve", before_("kq_ps"), before_("kv_n_ps"), before_("z_ps"))
            else:
                wait("dve", before_("kq_ps"), before_("ab_q"))
            mark("dve", n(f"conv_{name}0"),
                 dve.tensor_scalar(dst[:, :, :], raw[g][:, j, :, 0:P], conv_w[:, j, 0:1], conv_b[:, j:j + 1], ALU.mult, ALU.add))
            for tap in range(1, 4):
                wait("dve", n(f"conv_{name}{tap - 1}"))
                mark("dve", n(f"conv_{name}{tap}" if tap < 3 else f"conv_{name}"),
                     dve.scalar_tensor_tensor(dst[:, :, :], raw[g][:, j, :, tap:tap + P], conv_w[:, j, tap:tap + 1],
                                              dst[:, :, :], ALU.mult, ALU.add))
            yield
        sums = []
        wait("pe", n("tanh_ae"))
        for name, ones in (("sum_a", ones_a), ("sum_e", ones_e)):
            i, bank = grab(pro)
            mark("pe", n(name), pe.matmul(bank[:, :], ones[:, :], tanh_ae[:, :], start=True, stop=True))
            sums.append((i, bank))
        scale_a, shift_a = -0.5 * 0.1 / D, 1 - 0.5 * 0.1
        scale_e, shift_e = 0.5 * 0.9 / D, 0.5 * 0.9 + 0.05
        (ia, bank_a), (ie, bank_e) = sums
        va, ve = (bk[:, :].rearrange("p (b t) -> p b t", b=NB) for bk in (bank_a, bank_e))
        wait("act", n("sum_a"), f"scan_b.{(g - 1) % G}", f"scan_c.{(g - 1) % G}", f"scan_f.{(g - 1) % G}", f"scan_e.{(g - 1) % G}",
             f"clear.{(g - 1) % G}")
        act.activation(decay[:, 0, :, :], va, ACT.Copy, bias=shift_a, scale=scale_a)
        mark("act", n("dec_a"), act.activation(decay[0:D, 2, :, :], va[0:D], ACT.Copy, bias=shift_a, scale=scale_a))
        pro.freed_by(ia, n("dec_a"))
        wait("act", n("sum_e"))
        act.activation(decay[:, 1, :, :], ve, ACT.Copy, bias=shift_e, scale=scale_e)
        mark("act", n("dec_e"), act.activation(decay[D:P, 2, :, :], ve[D:P], ACT.Copy, bias=shift_e, scale=scale_e))
        pro.freed_by(ie, n("dec_e"))
        yield
        for b in range(NB):
            i, bank = grab(pro)
            for k in range(KH):
                ins = pe.matmul(bank[:, 0:NG], xt[:, k, b * P:(b + 1) * P], w_gt[:, k, :], start=k == 0, stop=k == KH - 1)
            mark("pe", n(f"gt_ps{b}"), ins)
            wait("dve", n(f"gt_ps{b}"), before_(f"gated{b}"), before_("soft"))
            mark("dve", n(f"gt{b}"), dve.tensor_tensor(gt[i2][:, b, :], bank[:, 0:NG], bias_gt[:, :], ALU.add))
            pro.freed_by(i, n(f"gt{b}"))
            if b % 2:
                yield
        u = gt[i2][:, :, H:NG]
        wait("act", *[n(f"gt{b}") for b in range(NB)])
        wait("act", f"soft.{(g - 1) % G}")
        mark("act", n("abs_u"), act.activation(soft[:, 0, :, :], u, ACT.Abs))
        wait("act", n("abs_u"))
        mark("act", n("exp_u"), act.activation(soft[:, 1, :, :], soft[:, 0, :, :], ACT.Exp, scale=-1.0))
        wait("act", n("exp_u"))
        mark("act", n("ln_u"), act.activation(soft[:, 2, :, :], soft[:, 1, :, :], ACT.Ln, bias=1.0))
        wait("dve", n("ln_u"))
        mark("dve", n("soft"), dve.scalar_tensor_tensor(soft[:, 0, :, :], u, 0.0, soft[:, 2, :, :], ALU.max, ALU.add))
        wait("dve", n("soft"), before_("weight"))
        mark("dve", n("theta0"), dve.tensor_reduce(theta[i2][:, :], soft[:, 0, :, :], AX.X, ALU.add))
        wait("dve", n("theta0"))
        mark("dve", n("theta"), dve.tensor_scalar(theta[i2][:, :], theta[i2][:, :], -GRAD_SCALE * LR / D, None, ALU.mult))
        yield
        wait("dve", n("dec_a"), n("dec_e"), before_("scan_f"))
        mark("dve", n("first"), dve.tensor_copy(t_first[i2][:, :, 0:1], decay[:, 2, :, 0:1]))
        wait("dve", n("first"))
        mark("dve", n("clear"), dve.memset(decay[:, :, :, 0:1], 0.0))
        flat = lambda a: a.rearrange("p b t -> p (b t)")
        C, E_, AB, AF = (flat(a) for a in (resp[i2][:, 0], resp[i2][:, 1], carry[i2][:, 0], carry[i2][:, 1]))
        dec_a, dec_e, dec_ae = (flat(decay[:, j]) for j in range(3))
        wait("dve", n("clear"), before_("ck"), before_("ch"), before_("p2"), before_("kq"))
        mark("dve", n("scan_e"), dve.tensor_tensor_scan(E_, dec_e, ident_nb[:, :, :].rearrange("p b t -> p (b t)"), 0.0, ALU.mult, ALU.add))
        wait("dve", n("scan_e"))
        mark("dve", n("scan_c"), dve.tensor_tensor_scan(C, dec_a, E_, 0.0, ALU.mult, ALU.add))
        wait("dve", before_("g_dec"), before_("ab_h"), before_("ab_q"))
        mark("dve", n("scan_f"), dve.tensor_tensor_scan(AF, dec_ae, flat(t_first[i2][:, :, :]), 0.0, ALU.mult, ALU.add))
        wait("dve", n("scan_f"))
        mark("dve", n("scan_b"), dve.tensor_tensor_scan(AB[D:P], dec_a[D:P], AF[D:P], 0.0, ALU.mult, ALU.add))
        wait("pool", n("scan_f"), before_("ab_h"), before_("g_dec"))
        M.apart("pool")
        mark("pool", n("copy_a"), pool.tensor_copy(AB[0:D], AF[0:D]))
        yield
        i, bank = grab(pro)
        wait("pe", n("conv_kv"))
        for b in range(NB):
            ins = pe.transpose(bank[:, b * P:(b + 1) * P], KV[:, b, :], ident[:, :])
        mark("pe", n("kv_n_ps"), ins)
        vb = bank[:, :].rearrange("p (b two d) -> p two b d", b=NB, two=2)
        wait("act", n("kv_n_ps"), before_("ck"), before_("e2"), before_("sq_k"))
        act.activation(kv_n[i2][:, 0], vb[:, 0], ACT.Copy)
        mark("act", n("kv_n"), act.activation(kv_n[i2][:, 1], vb[:, 1], ACT.Copy, scale=2.0))
        pro.freed_by(i, n("kv_n"))
        yield
        i, bank = grab(pro)
        wait("pe", n("conv_q"))
        for b in range(NB):
            ins = pe.matmul(bank[:, b * P:(b + 1) * P], KV[0:D, b, :], Q[0:D, b, :], start=True, stop=True)
        mark("pe", n("kq_ps"), ins)
        wait("dve", n("kq_ps"), n("scan_c"), before_("zq_ps"))
        mark("dve", n("kq"), dve.tensor_tensor(flat(kq[i2][:, :, :]), bank[:, :], C, ALU.mult))
        pro.freed_by(i, n("kq"))
        yield
        wait("pool", n("conv_q"), n("copy_a"), n("scan_b"), before_("zq_ps"))
        mark("pool", n("ab_q"), pool.tensor_tensor(ab_q[i2][:, :, :], q[i2][:, :, :], carry[i2][:, 0], ALU.mult))
        last = spread(carry[i2][:, :, :, P - 1:P].rearrange("p w b o -> p b w o"), 3, D)
        wait("dve", n("scan_b"), n("copy_a"), before_("upd_ps"))
        mark("dve", n("g_dec"), dve.tensor_tensor(g_dec[i2][:, :, :, :], spread(ident_g[:, :, :].unsqueeze(1), 1, NB), last, ALU.mult))
        last_r = spread(resp[i2][:, :, :, P - 1:P].rearrange("p w b o -> p b w o"), 3, D)
        wait("pool", n("kv_n"), n("scan_c"), before_("upd_ps"))
        mark("pool", n("ck"), pool.tensor_tensor(ck[i2][:, :, :, :], spread(kv_n[i2][:, 0].unsqueeze(2), 2, 2), last_r, ALU.mult))
        wait("pool", n("kv_n"), before_("norm_k"))
        mark("pool", n("sq_k"), pool.tensor_tensor(sq_k[i2][:, :, :], kv_n[i2][:, 0], kv_n[i2][:, 0], ALU.mult))
        wait("dve", n("sq_k"), before_("norm_p"))
        mark("dve", n("norm_k"), dve.tensor_reduce(norms[i2][:, 0, :], sq_k[i2][:, :, :], AX.X, ALU.add))
        yield

    def memory(c, g):
        n = lambda name: f"{name}.{g}"
        o = lambda name: f"{name}.{(g - 1) % G}"
        o2 = lambda name: f"{name}.{(g - 2) % G}"
        i2 = g % 2
        KV, C = kv[i2], resp[i2][:, 0]
        ST, W2 = state[g], w2[g]
        i, zb = grab(core)
        z = zb[:, 0:NB * D].rearrange("p (b d) -> p b d", b=NB)
        wait("pe", n("conv_kv"), n("state"))
        for b in range(NB):
            ins = pe.matmul(z[:, b, :], KV[0:D, b, :], ST[0:D, b, 0, :], start=True, stop=True)
        mark("pe", n("z_ps"), ins)
        wait("act", n("z_ps"), o("sig"))
        mark("act", n("t_z"), act.activation(t_z[:, :, :], z, ACT.Tanh, scale=0.5))
        wait("dve", n("t_z"), o("d_silu"), o("dz"))
        mark("dve", n("sig"), dve.tensor_scalar(sig[:, :, :], t_z[:, :, :], 0.5, 0.5, ALU.mult, ALU.add))
        wait("dve", n("sig"), o("ch"), o("h_ps"), o("sq_h"))
        mark("dve", n("h"), dve.tensor_tensor(h[:, :, :], z, sig[:, :, :], ALU.mult))
        core.freed_by(i, n("h"))
        yield
        i, bank = grab(core)
        wait("pe", n("h"))
        M.apart("pe")
        for b in range(NB):
            ins = pe.transpose(bank[0:D, b * P:(b + 1) * P], h[:, b, :], ident[:, :])
        mark("pe", n("h_ps"), ins)
        wait("act", n("h_ps"), o("hh_ps"))
        mark("act", n("h_t"), act.activation(h_t[:, :, :].rearrange("p b t -> p (b t)"), bank[0:D, :], ACT.Copy))
        core.freed_by(i, n("h_t"))
        wait("dve", n("h"))
        mark("dve", n("r"), dve.scalar_tensor_tensor(ds[:, 0], sig[:, :, :], 1.0, h[:, :, :], ALU.subtract, ALU.mult))
        wait("dve", n("r"))
        mark("dve", n("d_silu"), dve.tensor_tensor(ds[:, 1], sig[:, :, :], ds[:, 0], ALU.subtract))
        last_r = spread(resp[i2][:, :, :, P - 1:P].rearrange("p w b o -> p b w o"), 3, D)
        wait("pool", n("h"), o("upd_ps"))
        mark("pool", n("ch"), pool.tensor_tensor(ch[:, :, :, :], spread(h[:, :, :].unsqueeze(2), 2, 2), last_r, ALU.mult))
        yield
        i, bank = grab(core)
        pred = bank[:, 0:NB * D].rearrange("p (b d) -> p b d", b=NB)
        wait("pe", n("h_t"))
        for b in range(NB):
            ins = pe.matmul(pred[:, b, :], h_t[:, b, :], ST[0:D, b, 2, :], start=True, stop=True)
        mark("pe", n("pred_ps"), ins)
        wait("dve", n("pred_ps"), n("kv_n"), o("grad_w"), o("e_ps"), o("sq_e"))
        mark("dve", n("e2"), dve.scalar_tensor_tensor(grad[:, 1], pred, 2.0, kv_n[i2][:, 1], ALU.mult, ALU.subtract))
        core.freed_by(i, n("e2"))
        yield
        i, bank = grab(core)
        wait("pe", n("e2"))
        M.apart("pe")
        for b in range(NB):
            ins = pe.transpose(bank[0:D, b * P:(b + 1) * P], grad[:, 1, b, :], ident[:, :])
        mark("pe", n("e_ps"), ins)
        wait("act", n("e_ps"), o("dh_ps"))
        mark("act", n("e_t"), act.activation(e_t[:, :, :].rearrange("p b t -> p (b t)"), bank[0:D, :], ACT.Copy))
        core.freed_by(i, n("e_t"))
        wait("act", n("h"), o("norm_h"))
        mark("act", n("sq_h"), act.activation(sq[:, 0], h[:, :, :], ACT.Square))
        wait("act", n("e2"))
        mark("act", n("sq_e"), act.activation(sq[:, 2], grad[:, 1], ACT.Square))
        yield
        i, bank = grab(core)
        dh = bank[:, 0:NB * D].rearrange("p (b d) -> p b d", b=NB)
        wait("pe", n("e_t"), n("w2"))
        for b in range(NB):
            ins = pe.matmul(dh[:, b, :], e_t[:, b, :], W2[:, b, :], start=True, stop=True)
        mark("pe", n("dh_ps"), ins)
        wait("dve", n("dh_ps"), n("d_silu"), o("sq_z"))
        mark("dve", n("dz"), dve.tensor_tensor(grad[:, 0], dh, ds[:, 1], ALU.mult))
        core.freed_by(i, n("dz"))
        wait("act", n("dz"))
        mark("act", n("sq_z"), act.activation(sq[:, 1], grad[:, 0], ACT.Square))
        wait("dve", n("sq_z"), n("sq_h"), n("sq_e"), n("norm_k"))
        mark("dve", n("norm_h"), dve.tensor_reduce(norms[i2][:, 1:4, :], sq[:, :, :, :], AX.X, ALU.add))
        yield
        wait("dve", n("norm_h"))
        mark("dve", n("norm_p"), dve.tensor_tensor(small[:, 0:2, :], norms[i2][:, 0:2, :], norms[i2][:, 2:4, :], ALU.mult))
        wait("dve", n("norm_p"))
        mark("dve", n("norm_s"), dve.tensor_tensor(small[:, 2, :], small[:, 0, :], small[:, 1, :], ALU.add))
        wait("dve", n("norm_s"))
        mark("dve", n("norm_g"), dve.tensor_scalar(small[:, 3, :], small[:, 2, :], GRAD_SCALE ** 2, 1e-12, ALU.mult, ALU.max))
        wait("pool", n("norm_g"))
        mark("pool", n("inv_g"), pool.tensor_tensor(small[:, 4, :], small[:, 3, :], minus_half[:, 0:NB], ALU.pow))
        wait("dve", n("inv_g"), n("theta"))
        mark("dve", n("weight"), dve.scalar_tensor_tensor(small[:, 5, :], small[:, 4, :], 1.0, theta[i2][:, :], ALU.min, ALU.mult))
        wait("dve", n("weight"), o("upd_ps"), o("out_ps"), o("zq_ps"))
        wgt = small[:, 5, :].unsqueeze(2)
        mark("dve", n("dz_w"), dve.tensor_tensor(dz_w[:, :, :, :], spread(grad[:, 0].unsqueeze(2), 2, 2),
                                                 spread(spread(wgt, 2, 2).unsqueeze(3), 3, D), ALU.mult))
        mark("dve", n("grad_w"), dve.tensor_tensor(e_w[:, :, :], grad[:, 1], spread(wgt, 2, D), ALU.mult))
        yield
        i, bank = grab(core)
        wait("pe", n("grad_w"), n("kq"), n("ab_q"))
        for b in range(NB):
            zq = bank[:, b * P:(b + 1) * P]
            pe.matmul(zq, ST[:, b, 0:2, :].rearrange("p w d -> p (w d)"), ab_q[i2][:, b, :], start=True, stop=False)
            ins = pe.matmul(zq, dz_w[:, b].rearrange("p w d -> p (w d)"), kq[i2][:, b, :], start=False, stop=True)
        mark("pe", n("zq_ps"), ins)
        wait("act", n("zq_ps"), o("hq"))
        mark("act", n("t_q"), act.activation(t_q[:, :, :].rearrange("p b t -> p (b t)"), bank[:, :], ACT.Tanh, scale=0.5))
        wait("dve", n("t_q"), o("hh_ps"), o("ab_h"))
        mark("dve", n("hq"), dve.scalar_tensor_tensor(hq[:, :, :].rearrange("p b t -> p (b t)"), t_q[:, :, :].rearrange("p b t -> p (b t)"),
                                                      1.0, bank[:, :], ALU.add, ALU.mult))
        core.freed_by(i, n("hq"))
        wait("pool", n("hq"), n("copy_a"), n("scan_b"), o("out_ps"))
        mark("pool", n("ab_h"), pool.tensor_tensor(ab_h[:, :, :], hq[:, :, :], carry[i2][:, 0], ALU.mult))
        yield
        iu, upd = grab(core)
        wait("pe", n("g_dec"), n("ck"), n("ch"))
        for b in range(NB):
            ub = upd[:, b * P:(b + 1) * P]
            pe.matmul(ub, g_dec[i2][:, b].rearrange("p w d -> p (w d)"), ST[:, b, 1:3].rearrange("p w d -> p (w d)"), start=True, stop=False)
            pe.matmul(ub[:, 0:D], ck[i2][:, b].rearrange("p w d -> p (w d)"), dz_w[:, b, 0, :], start=False, stop=False)
            ins = pe.matmul(ub[:, D:P], ch[:, b].rearrange("p w d -> p (w d)"), e_w[:, b, :], start=False, stop=True)
        mark("pe", n("upd_ps"), ins)
        i, bank = grab(core)
        wait("pe", n("hq"))
        for b in range(NB):
            ins = pe.matmul(bank[:, b * P:(b + 1) * P], h_t[:, b, :], hq[0:D, b, :], start=True, stop=True)
        mark("pe", n("hh_ps"), ins)
        wait("dve", n("hh_ps"), o("out_ps"))
        mark("dve", n("p2"), dve.tensor_tensor(hh[:, :, :].rearrange("p b t -> p (b t)"), bank[:, :], C.rearrange("p b t -> p (b t)"), ALU.mult))
        core.freed_by(i, n("p2"))
        yield
        i, bank = grab(core)
        wait("pe", n("p2"), n("ab_h"))
        for b in range(NB):
            ob = bank[0:D, b * P:(b + 1) * P]
            pe.matmul(ob, ST[:, b, 2, :], ab_h[:, b, :], start=True, stop=False)
            ins = pe.matmul(ob, e_w[:, b, :], hh[:, b, :], start=False, stop=True)
        mark("pe", n("out_ps"), ins)
        wait("act", n("out_ps"), o2(f"wo_ps1"))
        mark("act", n("ret"), act.activation(ret[i2][:, :, :].rearrange("p b t -> p (b t)"), bank[0:D, :], ACT.Copy, scale=0.5))
        core.freed_by(i, n("ret"))
        wait("act", n("upd_ps"))
        u4 = upd[:, :].rearrange("p (b w d) -> p b w d", b=NB, w=2)
        act.activation(ST[:, :, 0:2, :], spread(u4[:, :, 0:1, :], 2, 2), ACT.Copy)
        mark("act", n("state"), act.activation(ST[:, :, 2, :], u4[:, :, 1, :], ACT.Copy))
        core.freed_by(iu, n("state"))
        yield
        i, bank = grab(core)
        wait("pe", n("state"))
        M.apart("pe")
        for b in range(NB):
            ins = pe.transpose(bank[0:D, b * P:(b + 1) * P], ST[:, b, 2, :], ident[:, :])
        mark("pe", n("w2_ps"), ins)
        wait("act", n("w2_ps"), n("dh_ps"))
        mark("act", n("w2"), act.activation(W2[:, :, :], bank[0:D, :].rearrange("p (b d) -> p b d", b=NB)[:, :, 0:D], ACT.Copy))
        core.freed_by(i, n("w2"))
        yield

    def epilogue(c, g):
        n = lambda name: f"{name}.{g}"
        o = lambda name: f"{name}.{(g - 1) % G}"
        o2 = lambda name: f"{name}.{(g - 2) % G}"
        i2 = g % 2
        X, Y, R = x[g % NX], y[i2], rows[i2]
        held = []
        for j in range(2):
            i, bank = grab(epi)
            held.append((i, bank))
            wait("pe", n("ret"))
            for b in (2 * j, 2 * j + 1):
                ins = pe.matmul(bank[:, (b % 2) * H:(b % 2 + 1) * H], ret[i2][:, b, :], w_o[:, :], start=True, stop=True)
            mark("pe", n(f"wo_ps{j}"), ins)
            wait("act", n(f"wo_ps{j}"), o("ms"))
            for b in (2 * j, 2 * j + 1):
                if g or j or b:
                    pass
                prev = n(f"ssq{b - 1}") if b else o(f"ssq{NB - 1}")
                wait("act", prev)
                mark("act", n(f"ssq{b}"), act.activation(junk[:, :], bank[:, (b % 2) * H:(b % 2 + 1) * H], ACT.Square, accum_out=ssq[:, b:b + 1]))
        yield
        wait("dve", *[n(f"ssq{b}") for b in range(NB)])
        wait("dve", o("rms"))
        mark("dve", n("ms"), dve.tensor_scalar(rms[:, 0, :], ssq[:, :], 1.0 / H, EPS_RMS, ALU.mult, ALU.add))
        wait("pool", n("ms"), o(f"gated{NB - 1}"))
        mark("pool", n("rms"), pool.tensor_tensor(rms[:, 1, :], rms[:, 0, :], minus_half[:, 0:NB], ALU.pow))
        yield
        for b in range(NB):
            i, bank = held[b // 2]
            wait("dve", n("rms"), n(f"gt{b}"), o2("norm3"))
            mark("dve", n(f"gated{b}"), dve.scalar_tensor_tensor(Y[:, b, :], bank[:, (b % 2) * H:(b % 2 + 1) * H], rms[:, 1, b:b + 1],
                                                                 gt[i2][:, b, 0:H], ALU.mult, ALU.mult))
            if b % 2:
                epi.freed_by(i, n(f"gated{b}"))
        yield
        wait("pool", *[n(f"gated{b}") for b in range(NB)])
        pool.wait_ge(s_x[g % NX], c * 16 + 16)
        mark("pool", n("res"), pool.tensor_tensor(Y[:, :, :], Y[:, :, :], X[:, :, :], ALU.add))
        yield
        wait("dve", n("res"), o("mv3"))
        for b in range(NB):
            mark("dve", n(f"stats{b}"), dve.bn_stats(stats[:, b, :], Y[:, b, :]))
        wait("dve", o("norm3"), o("var"))
        for b in range(NB):
            wait("dve", n(f"stats{b}"))
            M.apart("dve")
            mark("dve", n(f"mv{b}"), dve.bn_aggr(mv[:, b, :], stats[:, b, :]))
        wait("dve", n("mv3"), o("rstd"))
        mark("dve", n("var"), dve.tensor_scalar(rstd[:, 0, :], mv[:, :, 1], EPS_LN, None, ALU.add))
        wait("pool", n("var"))
        mark("pool", n("rstd"), pool.tensor_tensor(rstd[:, 1, :], rstd[:, 0, :], minus_half[:, 0:NB], ALU.pow))
        yield
        wait("dve", n("rstd"), o2("sent"))
        for b in range(NB):
            mark("dve", n(f"norm{b}"), dve.tensor_scalar(R[:, b, 0:H], Y[:, b, :], mv[:, b, 0:1], rstd[:, 1, b:b + 1], ALU.subtract, ALU.mult))
        mark("dve", n("token"), dve.tensor_copy(R[:, :, H:H + 1], token[:, g * NB:(g + 1) * NB].unsqueeze(2)))
        wait("dve", n("token"))
        mark("dve", n("next_token"), dve.tensor_scalar(token[:, g * NB:(g + 1) * NB], token[:, g * NB:(g + 1) * NB], float(P), None, ALU.add))
        yield
        for k in range(KH):
            i, bank = grab(epi)
            wait("pe", n("norm3"))
            for b in range(NB):
                ins = pe.transpose(bank[:, b * P:(b + 1) * P], R[:, b, k * P:(k + 1) * P], ident[:, :])
            mark("pe", n(f"rt_ps{k}"), ins)
            wait("act", n(f"rt_ps{k}"), o("score_ps"))
            mark("act", n(f"rt{k}"), act.activation(rows_t[:, k, :], bank[:, :], ACT.Copy))
            epi.freed_by(i, n(f"rt{k}"))
        yield
        i, bank = grab(epi)
        score = bank[:, 0:NB * NE].rearrange("p (b e) -> p b e", b=NB)
        wait("pe", n("rt0"), n("rt1"))
        for b in range(NB):
            for k in range(KH):
                ins = pe.matmul(score[:, b, :], rows_t[:, k, b * P:(b + 1) * P], w_route[:, k, :], start=k == 0, stop=k == KH - 1)
        mark("pe", n("score_ps"), ins)
        wait("dve", n("score_ps"))
        mark("dve", n("best"), dve.tensor_reduce(best[:, 0, :], score, AX.X, ALU.max))
        wait("dve", n("best"))
        mark("dve", n("is_best"), dve.tensor_tensor(pick[:, 0], score, spread(best[:, 0, :].unsqueeze(2), 2, NE), ALU.is_ge))
        epi.freed_by(i, n("is_best"))
        wait("dve", n("is_best"))
        mark("dve", n("ranked"), dve.tensor_tensor(pick[:, 1], pick[:, 0], spread(rank[:, :].unsqueeze(1), 1, NB), ALU.mult))
        wait("dve", n("ranked"))
        mark("dve", n("top"), dve.tensor_reduce(best[:, 1, :], pick[:, 1], AX.X, ALU.max))
        wait("dve", n("top"), o("pos_ps"))
        mark("dve", n("onehot"), dve.tensor_tensor(onehot[:, :, :], spread(rank[:, :].unsqueeze(1), 1, NB),
                                                   spread(best[:, 1, :].unsqueeze(2), 2, NE), ALU.is_equal))
        yield
        i, bank = grab(epi)
        pos = bank[:, 0:NB * NE].rearrange("p (b e) -> p b e", b=NB)
        wait("pe", n("onehot"), o("routed"))
        pe.matmul(pos, before[:, :], onehot[:, :, :], start=True, stop=False)
        for b in range(NB - 1):
            pe.matmul(pos[:, b + 1:NB, :], ones_bf[:, :], spread(onehot[:, b:b + 1, :], 1, NB - 1 - b), start=False, stop=False)
        ins = pe.matmul(pos, ones_bf[:, :], spread(routed[:, :].unsqueeze(1), 1, NB), start=False, stop=True)
        mark("pe", n("pos_ps"), ins)
        wait("dve", n("onehot"))
        mark("dve", n("total"), dve.tensor_reduce(total[:, :], onehot[:, :, :].rearrange("p b e -> p e b"), AX.X, ALU.add))
        wait("dve", n("total"), n("pos_ps"))
        mark("dve", n("routed"), dve.tensor_tensor(routed[:, :], routed[:, :], total[:, :], ALU.add))
        mark("dve", n("where0"), dve.tensor_tensor(where[:, 0], pos, spread(region0[:, :].unsqueeze(1), 1, NB), ALU.add))
        epi.freed_by(i, n("where0"))
        wait("dve", n("where0"))
        mark("dve", n("where1"), dve.tensor_tensor(where[:, 1], where[:, 0], onehot[:, :, :], ALU.mult))
        wait("dve", n("where1"))
        mark("dve", n("where_f"), dve.tensor_reduce(where_f[:, :], where[:, 1], AX.X, ALU.add))
        wait("dve", n("where_f"), o2("sent"))
        mark("dve", n("index"), dve.tensor_copy(index[i2][:, :], where_f[:, :]))
        yield
        wait("pool", n("index"), n("norm3"), n("token"))
        M.apart("pool")
        for b in range(NB):
            pool.indirect_dma_start(sorted_rows[:, :], bass.IndirectOffsetOnAxis(index[i2][:, b:b + 1], 0), R[:, b, :], None,
                                    bounds_check=NE * REGION - 1, oob_is_err=False).then_inc(s_scatter[i2], 16)
        pool.wait_ge(s_scatter[i2], c * (2 * NB * 16) + (g // 2 + 1) * NB * 16)
        M.apart("pool")
        mark("pool", n("sent"), pool.memset(junk_pool[:, :], 0.0))
        yield

    junk_pool = sb("junk_pool", [P, 1])

    def run(*stages):
        live = list(stages)
        while live:
            for s in list(live):
                if next(s, "done") == "done":
                    live.remove(s)

    s_blank = sem("s_blank")
    for r in rows:
        pool.memset(r[:, :, H:ROW], 0.0).then_inc(s_blank, 1)
    dve.wait_ge(s_blank, 2)
    M.start_loop()
    with nc.Fori(0, NC) as c:
        M.lap = c
        run(prologue(c, 0))
        for g in range(G):
            stages = [memory(c, g)]
            if g + 1 < G:
                stages.append(prologue(c, g + 1))
            if g:
                stages.append(epilogue(c, g - 1))
            run(*stages)
        run(epilogue(c, G - 1))
    result = M.finish()
    result["slots"] = {s.name: dict(s.last) for s in (pro, core, epi)}
    plans["loop1"] = result
    per = plan["count"] if plan else {e: 1 for e in M.sem}
    for e in (pe, act, dve, pool, sp):
        for who, s in M.sem.items():
            e.wait_ge(s, per[who] * (NC + 1))
        for s in s_scatter:
            e.wait_ge(s, NC * 2 * NB * 16)


def tiles(nc, ctx, sb, sem, v):
    routed, ones_bf, region0, tile_no, pad_row = (v[n] for n in ("routed", "ones_bf", "region0", "tile_no", "pad_row"))
    banks, sorted_rows = v["banks"], v["sorted_rows"]
    pe, dve, pool = nc.tensor, nc.vector, nc.gpsimd
    s_cnt, s_d, s_pad, s_io = sem("s_cnt"), sem("s_tiles"), sem("s_pad"), sem("s_iota")
    lane = sb("lane", [P, 1])
    n_tok = sb("n_tok", [P, NE])
    pad_f = sb("pad_f", [P, NE])
    pad_i = sb("pad_i", [P, NE], I32)
    nt_i = sb("nt_i", [P, 2, NE], I32)
    nt = sb("nt", [P, NE])
    cum = sb("cum", [P, NE])
    one = sb("one", [P, NE])
    past = sb("past", [P, NT, NE])
    first = sb("first", [P, NT, NE])
    e_of = sb("e_of", [P, 2, NT])
    f_of = sb("f_of", [P, 4, NT])
    tile_row = sb("tile_row", [P, NT], I32)
    tile_expert = sb("tile_expert", [P, NT], I32)
    made = [0]

    def step(instruction):
        made[0] += 1
        instruction.then_inc(s_d, 1)
        dve.wait_ge(s_d, made[0])

    pool.iota(lane[:, :], pattern=[[0, 1]], base=0, channel_multiplier=1, allow_small_or_imprecise_dtypes=True).then_inc(s_io, 1)
    pe.matmul(banks[0][:, 0:NE], ones_bf[:, :], routed[:, :], start=True, stop=True).then_inc(s_cnt, 1)
    dve.wait_ge(s_cnt, 1)
    dve.wait_ge(s_io, 1)
    step(dve.tensor_copy(n_tok[:, :], banks[0][:, 0:NE]))
    step(dve.tensor_tensor(pad_f[:, :], n_tok[:, :], region0[:, :], ALU.add))
    step(dve.tensor_scalar(pad_f[:, :], pad_f[:, :], lane[:, 0:1], None, ALU.add))
    step(dve.tensor_copy(pad_i[:, :], pad_f[:, :]))
    pad_ready = made[0]
    step(dve.tensor_scalar(n_tok[:, :], n_tok[:, :], float(P - 1), None, ALU.add))
    step(dve.tensor_copy(nt_i[:, 0, :], n_tok[:, :]))
    step(dve.tensor_scalar(nt_i[:, 1, :], nt_i[:, 0, :], 7, None, ALU.arith_shift_right))
    step(dve.tensor_copy(nt[:, :], nt_i[:, 1, :]))
    step(dve.memset(one[:, :], 1.0))
    step(dve.tensor_tensor_scan(cum[:, :], one[:, :], nt[:, :], 0.0, ALU.mult, ALU.add))
    step(dve.tensor_tensor(past[:, :, :], spread(tile_no[:, :].unsqueeze(2), 2, NE), spread(cum[:, :].unsqueeze(1), 1, NT), ALU.is_ge))
    step(dve.tensor_reduce(e_of[:, 0, :], past[:, :, :], AX.X, ALU.add))
    step(dve.tensor_tensor(first[:, :, :], past[:, :, :], spread(nt[:, :].unsqueeze(1), 1, NT), ALU.mult))
    step(dve.tensor_reduce(f_of[:, 0, :], first[:, :, :], AX.X, ALU.add))
    step(dve.tensor_tensor(f_of[:, 1, :], tile_no[:, :], f_of[:, 0, :], ALU.subtract))
    step(dve.tensor_scalar(f_of[:, 2, :], f_of[:, 1, :], float(P), None, ALU.mult))
    step(dve.scalar_tensor_tensor(f_of[:, 3, :], e_of[:, 0, :], float(REGION), f_of[:, 2, :], ALU.mult, ALU.add))
    step(dve.tensor_scalar(f_of[:, 3, :], f_of[:, 3, :], float(NE * REGION), None, ALU.min))
    step(dve.tensor_copy(tile_row[:, :], f_of[:, 3, :]))
    step(dve.tensor_scalar(e_of[:, 1, :], e_of[:, 0, :], float(NE - 1), None, ALU.min))
    step(dve.tensor_copy(tile_expert[:, :], e_of[:, 1, :]))
    pool.wait_ge(s_d, pad_ready)
    for e in range(NE):
        pool.indirect_dma_start(sorted_rows[:, :], bass.IndirectOffsetOnAxis(pad_i[:, e:e + 1], 0), pad_row[:, :], None,
                                bounds_check=NE * REGION - 1, oob_is_err=False).then_inc(s_pad, 16)
    pool.dma_start(sorted_rows[NE * REGION:NE * REGION + P, :], pad_row[:, :]).then_inc(s_pad, 16)
    for e in (nc.tensor, nc.scalar, nc.vector, nc.gpsimd, nc.sync):
        e.wait_ge(s_d, made[0])
        e.wait_ge(s_pad, 16 * (NE + 1))
    v["tile_row"], v["tile_expert"] = tile_row, tile_expert
    TILE_LIST.update(row=tile_row, expert=tile_expert)


TILE_LIST = {}


def loop2(nc, ctx, sb, sem, v, plan, plans):
    banks, sorted_rows, out, ident, w_expert, minus_half = (
        v[n] for n in ("banks", "sorted_rows", "out", "ident", "w_expert", "minus_half"))
    tile_row, tile_expert = TILE_LIST["row"], TILE_LIST["expert"]
    pe, act, dve, pool, sp = nc.tensor, nc.scalar, nc.vector, nc.gpsimd, nc.sync
    M = Marks(nc, ctx, "l2", plan)
    mark, wait = M.mark, M.wait
    U = UNROLL
    xs = [sb(f"xs{u}", [P, ROW]) for u in range(U)]
    xs_t = [sb(f"xs_t{u}", [P, KH, P]) for u in range(U)]
    ys = [sb(f"ys{u}", [P, H]) for u in range(U)]
    os_ = [sb(f"os{u}", [P, H]) for u in range(U)]
    st = [sb(f"st{u}", [P, 6]) for u in range(U)]
    mvs = [sb(f"mvs{u}", [P, 2]) for u in range(U)]
    rs = [sb(f"rs{u}", [P, 3]) for u in range(U)]
    tok = [sb(f"tok{u}", [P, 1], I32) for u in range(U)]
    s_row = [sem(f"s_row{u}") for u in range(U)]
    s_out = [sem(f"s_out{u}") for u in range(U)]

    for u in range(U):
        pool.dma_start(os_[u][:, :], sorted_rows[NE * REGION:NE * REGION + P, 0:H]).then_inc(s_out[u], 16)
    M.start_loop()
    with nc.Fori(0, NT // U) as it:
        M.lap = it
        for u in range(U):
            n = lambda name, u_=u: f"{name}.{u_}"
            wait("sp", n("ys"), n("tok"))
            M.apart("sp")
            r0 = sp.value_load(tile_row[0:1, bass.ds(it * U + u, 1)], min_val=0, max_val=NE * REGION)
            sp.dma_start(xs[u][:, :], sorted_rows[bass.ds(r0, P), :]).then_inc(s_row[u], 16)

        def front(u):
            n = lambda name: f"{name}.{u}"
            bt = banks[u]
            pe.wait_ge(s_row[u], it * 16 + 16)
            wait("pe", n("xt"))
            for k in range(KH):
                ins = pe.transpose(bt[:, k * P:(k + 1) * P], xs[u][:, k * P:(k + 1) * P], ident[:, :])
            mark("pe", n("tr"), ins)
            wait("act", n("tr"), n("mm"))
            mark("act", n("xt"), act.activation(xs_t[u][:, :, :].rearrange("p k t -> p (k t)"), bt[:, 0:H], ACT.Copy))

        def middle(u):
            n = lambda name: f"{name}.{u}"
            bank = banks[4 + u]
            e = pe.value_load(tile_expert[0:1, bass.ds(it * U + u, 1)], min_val=0, max_val=NE - 1)
            wait("pe", n("xt"), n("ys"))
            for k in range(KH):
                ins = pe.matmul(bank[:, 0:H], xs_t[u][:, k, :], w_expert[:, k, bass.ds(e, 1), :], start=k == 0, stop=k == KH - 1)
            mark("pe", n("mm"), ins)
            dve.wait_ge(s_row[u], it * 16 + 16)
            wait("dve", n("mm"), n("os"))
            mark("dve", n("ys"), dve.scalar_tensor_tensor(ys[u][:, :], xs[u][:, 0:H], 2.0, bank[:, 0:H], ALU.mult, ALU.add))
            dve.wait_ge(s_out[u], it * 16 + 16)
            mark("dve", n("tok"), dve.tensor_copy(tok[u][:, :], xs[u][:, H:H + 1]))
            wait("dve", n("ys"))
            mark("dve", n("st"), dve.bn_stats(st[u][:, :], ys[u][:, :]))
            wait("dve", n("st"), n("os"))
            M.apart("dve")
            mark("dve", n("mv"), dve.bn_aggr(mvs[u][:, :], st[u][:, :]))
            wait("dve", n("mv"), n("rs"))
            mark("dve", n("var"), dve.tensor_scalar(rs[u][:, 0:1], mvs[u][:, 1:2], EPS_LN, None, ALU.add))
            wait("pool", n("var"), n("os"))
            mark("pool", n("rs"), pool.tensor_tensor(rs[u][:, 1:2], rs[u][:, 0:1], minus_half[:, 0:1], ALU.pow))

        def back(u):
            n = lambda name: f"{name}.{u}"
            dve.wait_ge(s_out[u], it * 16 + 16)
            wait("dve", n("rs"))
            mark("dve", n("os"), dve.tensor_scalar(os_[u][:, :], ys[u][:, :], mvs[u][:, 0:1], rs[u][:, 1:2], ALU.subtract, ALU.mult))
            wait("pool", n("os"), n("tok"))
            M.apart("pool")
            pool.indirect_dma_start(out[:, :], bass.IndirectOffsetOnAxis(tok[u][:, :], 0), os_[u][:, :], None,
                                    bounds_check=TOK - 1, oob_is_err=False).then_inc(s_out[u], 16)

        for u in range(U + 2):
            if u < U:
                front(u)
            if 0 <= u - 1 < U:
                middle(u - 1)
            if 0 <= u - 2 < U:
                back(u - 2)
    plans["loop2"] = M.finish() | dict(slots={})
    for s in s_out:
        sp.wait_ge(s, 16 * (NT // U) + 16)


INPUTS = dict(hidden=[B, S, H], w_kv=[H, P], w_q=[H, P], w_ae=[H, P], w_gt=[H, H + D], bias_gt=[P, H + D],
              norm_g=[P, H], w_o=[D, H], conv_w=[P, 2, 4], conv_b=[P, 2], bias_ae=[P, 1], w_route=[H, NE],
              state0=[D, NB, 3, D], w2_0=[D, NB, D], w_expert=[NE, H, H])


def program(nc, plan):
    dram = {n: nc.dram_tensor(f"in_{n}", s, F32, kind="ExternalInput").ap() for n, s in INPUTS.items()}
    dram["out"] = nc.dram_tensor("out_0", [TOK, H], F32, kind="ExternalOutput").ap()
    return build(nc, dram, plan)


def kernel(**inputs):
    import numpy as np
    import concourse.bacc as bacc
    from concourse.bass_utils import run_bass_kernel_spmd

    a = {k.split("_", 2)[2]: np.asarray(w) for k, w in inputs.items()}
    rows = lambda w: np.broadcast_to(w[None, :], (P, w.shape[0]))
    arrays = dict(
        hidden=a["hidden"],
        w_kv=np.concatenate([a["Wk"], a["Wv"]]).T,
        w_q=np.concatenate([a["Wq"], a["Wq"]]).T,
        w_ae=np.concatenate([a["aW"], a["eW"]]).T,
        w_gt=np.concatenate([a["gW"], a["tW"]]).T,
        bias_gt=rows(np.concatenate([a["gb"], a["tb"]])),
        norm_g=rows(a["norm_g"]),
        w_o=a["Wo"].T,
        conv_w=np.stack([np.concatenate([a["ckw"], a["cvw"]]), np.concatenate([a["cqw"], a["cqw"]])], 1),
        conv_b=np.stack([np.concatenate([a["ckb"], a["cvb"]]), np.concatenate([a["cqb"], a["cqb"]])], 1),
        bias_ae=np.concatenate([a["ab"], a["eb"]])[:, None],
        w_route=a["gate_w"].T,
        state0=np.broadcast_to(np.stack([a["mW1"].T, a["mW1"].T, a["mW2"].T], 1)[:, None], (D, NB, 3, D)),
        w2_0=np.broadcast_to(a["mW2"][:, None], (D, NB, D)),
        w_expert=a["expert_w"].transpose(0, 2, 1),
    )
    plan = program(bacc.Bacc("TRN2", target_bir_lowering=False, num_devices=1), None)
    nc = bacc.Bacc("TRN2", target_bir_lowering=False, num_devices=1)
    program(nc, plan)
    feed = {f"in_{n}": np.ascontiguousarray(w) for n, w in arrays.items()}
    r = run_bass_kernel_spmd(nc, [feed], core_ids=[0])
    return r.results[0]["out_0"].reshape(B, S, H)
```

```python
import concourse.bass as bass
from concourse import mybir
from contextlib import ExitStack

F32 = mybir.dt.float32
BF16 = mybir.dt.bfloat16
I32 = mybir.dt.int32
ALU = mybir.AluOpType
ACT = mybir.ActivationFunctionType
AX = mybir.AxisListType

P = 128
B = 16
S = 512
H = 256
KH = H // P
D = 64
NC = S // P
G = 4
NB = B // G
TOK = B * S
NE = 8
REGION = TOK + P
NT = TOK // P + NE
ROW = H + 4
UNROLL = 4
NO_TOKEN = 2.0 * TOK
EPS_RMS = 1e-6
EPS_LN = 1e-5
GRAD_SCALE = 0.1
LR = 0.1


def spread(ap, axis, n):
    shape = list(ap.shape)
    shape[axis] = n
    return ap.broadcast_to(shape)


class Marks:

    def __init__(self, nc, ctx, prefix, plan):
        self.engines = dict(pe=nc.tensor, act=nc.scalar, dve=nc.vector, pool=nc.gpsimd, sp=nc.sync)
        self.sem = {e: ctx.enter_context(nc.semaphore(f"{prefix}_{e}")) for e in ("pe", "act", "dve", "pool")}
        self.passed = ctx.enter_context(nc.semaphore(f"{prefix}_passed"))
        self.plan = plan
        self.per_lap = plan["count"] if plan else {e: 1 for e in self.sem}

    def begin(self, lap, first=False):
        self.lap, self.first = lap, first
        self.count = {e: 0 for e in self.sem}
        self.at = {}

    def mark(self, e, name, instruction):
        instruction.then_inc(self.sem[e], 1)
        self.count[e] += 1
        assert name not in self.at, name
        self.at[name] = (e, self.count[e])

    def wait(self, e, *names):
        need = {}
        for name in names:
            if name is None:
                continue
            if name in self.at:
                who, n = self.at[name]
            elif self.first:
                continue
            elif self.plan:
                who, n = self.plan["at"][name]
                n -= self.per_lap[who]
            else:
                who, n = "pe", 1
            need[who] = max(need.get(who, n), n)
        for who, n in need.items():
            self.engines[e].wait_ge(self.sem[who], self.lap * self.per_lap[who] + n)

    def apart(self, e):
        self.engines[e].sem_inc(self.passed, 1)

    def fill(self):
        for e, s in self.sem.items():
            missing = self.per_lap[e] - self.count[e]
            if self.plan and missing:
                self.engines[e].wait_ge(s, self.count[e])
                self.engines[e].sem_inc(s, missing)
        if self.plan:
            assert all(self.plan["at"][name][1] >= n for name, (_, n) in self.at.items())


class Slots:

    def __init__(self, name, banks, plan):
        self.name, self.banks = name, banks
        self.place = plan["slots"][name][1] if plan else {}
        self.end = plan["slots"][name][0] if plan else None
        self.last = {}
        self.held = set()

    def begin(self):
        if self.end:
            self.last = dict(self.end)
        else:
            self.place = {}

    def take(self, use):
        i = self.place.setdefault(use, len(self.place) % len(self.banks))
        assert i not in self.held, use
        self.held.add(i)
        return i, self.banks[i], self.last.get(i)

    def freed_by(self, i, name):
        self.held.remove(i)
        self.last[i] = name


def build(nc, dram, plan):
    plans = {}
    out = dram["out"]
    with ExitStack() as ctx:
        def sb(name, shape, dt=F32):
            return ctx.enter_context(nc.sbuf_tensor(name, shape, dt))

        def sem(name):
            return ctx.enter_context(nc.semaphore(name))

        sorted_rows = nc.dram_tensor("sorted_rows", [NE * REGION + P, ROW], F32).ap()

        w_kv = sb("w_kv", [P, KH, P])
        w_q = sb("w_q", [P, KH, P])
        w_ae = sb("w_ae", [P, KH, P])
        NG = H + D
        w_gt = sb("w_gt", [P, KH, NG])
        bias_gt = sb("bias_gt", [P, NG])
        norm_g = sb("norm_g", [P, H])
        w_o = sb("w_o", [D, H])
        conv_w = sb("conv_w", [P, 2, 4])
        conv_b = sb("conv_b", [P, 2])
        bias_ae = sb("bias_ae", [P, 1])
        w_route = sb("w_route", [P, KH, NE])
        ident = sb("ident", [P, P])
        ident_nb = sb("ident_nb", [P, NB, P])
        ident_g = sb("ident_g", [P, 2, D])
        ones_a = sb("ones_a", [P, P])
        ones_e = sb("ones_e", [P, P])
        ones_bf = sb("ones_bf", [P, P], BF16)
        before = sb("before", [P, P], BF16)
        rank = sb("rank", [P, NE])
        region0 = sb("region0", [P, NE])
        token = sb("token", [P, G * NB])
        minus_half = sb("minus_half", [P, 8])
        tile_no = sb("tile_no", [P, NT])
        pad_row = sb("pad_row", [P, ROW])

        state = [sb(f"state{g}", [P, NB, 3, D]) for g in range(G)]
        w2 = [sb(f"w2_{g}", [D, NB, D]) for g in range(G)]
        n_raw = 2 * NB * (P + 3)
        shared = sb("shared", [P, G * n_raw])
        raw = [shared[:, g * n_raw:(g + 1) * n_raw].rearrange("p (j b t) -> p j b t", j=2, b=NB) for g in range(G)]
        w_expert = shared[:, 0:KH * NE * H].rearrange("p (k e f) -> p k e f", k=KH, e=NE)
        routed = sb("routed", [P, NE], BF16)

        banks = [ctx.enter_context(nc.psum_tensor(f"bank{i}", [P, 512], F32)) for i in range(8)]

        s_load = sem("s_load")
        s_expert = sem("s_expert")
        loads = [
            (w_kv[:, :, :], dram["w_kv"].rearrange("(k p) m -> p k m", p=P)),
            (w_q[:, :, :], dram["w_q"].rearrange("(k p) m -> p k m", p=P)),
            (w_ae[:, :, :], dram["w_ae"].rearrange("(k p) m -> p k m", p=P)),
            (w_gt[:, :, :], dram["w_gt"].rearrange("(k p) m -> p k m", p=P)),
            (bias_gt[:, :], dram["bias_gt"]),
            (norm_g[:, :], dram["norm_g"]),
            (w_o[:, :], dram["w_o"]),
            (conv_w[:, :, :], dram["conv_w"]),
            (conv_b[:, :], dram["conv_b"]),
            (bias_ae[:, :], dram["bias_ae"]),
            (w_route[:, :, :], dram["w_route"].rearrange("(k p) m -> p k m", p=P)),
        ]
        for g in range(G):
            loads += [(state[g][0:D, :, :, :], dram["state0"]), (w2[g][:, :, :], dram["w2_0"])]
        for dst, src in loads:
            nc.scalar.dma_start(dst, src).then_inc(s_load, 16)

        s_const = sem("s_const")
        n_const = 0

        def pool_const(instruction):
            nonlocal n_const
            n_const += 1
            instruction.then_inc(s_const, 1)
            nc.gpsimd.wait_ge(s_const, n_const)

        pool = nc.gpsimd
        pool_const(pool.memset(ident[:, :], 0.0))
        pool_const(pool.affine_select(out=ident[:, :], in_=ident[:, :], compare_op=ALU.not_equal, fill=1.0,
                                      base=0, pattern=[[-1, P]], channel_multiplier=1))
        pool_const(pool.memset(ident_nb[:, :, :], 0.0))
        pool_const(pool.affine_select(out=ident_nb[:, :, :], in_=ident_nb[:, :, :], compare_op=ALU.not_equal,
                                      fill=1.0, base=0, pattern=[[0, NB], [-1, P]], channel_multiplier=1))
        pool_const(pool.memset(ident_g[:, :, :], 0.0))
        pool_const(pool.affine_select(out=ident_g[:, 0, :], in_=ident_g[:, 0, :], compare_op=ALU.not_equal,
                                      fill=1.0, base=0, pattern=[[-1, D]], channel_multiplier=1))
        pool_const(pool.affine_select(out=ident_g[:, :, :], in_=ident_g[:, :, :], compare_op=ALU.not_equal,
                                      fill=1.0, base=-D, pattern=[[0, 2], [-1, D]], channel_multiplier=1))
        pool_const(pool.memset(ones_a[:, :], 0.0))
        pool_const(pool.memset(ones_a[0:D, :], 1.0))
        pool_const(pool.memset(ones_e[:, :], 0.0))
        pool_const(pool.memset(ones_e[D:P, :], 1.0))
        pool_const(pool.memset(ones_bf[:, :], 1.0))
        pool_const(pool.affine_select(out=before[:, :], in_=ones_bf[:, :], compare_op=ALU.is_gt, fill=0.0,
                                      base=0, pattern=[[1, P]], channel_multiplier=-1))
        pool_const(pool.iota(rank[:, :], pattern=[[-1, NE]], base=NE, channel_multiplier=0,
                             allow_small_or_imprecise_dtypes=True))
        pool_const(pool.iota(region0[:, :], pattern=[[REGION, NE]], base=0, channel_multiplier=0,
                             allow_small_or_imprecise_dtypes=True))
        pool_const(pool.iota(token[:, :], pattern=[[S, G * NB]], base=0, channel_multiplier=1,
                             allow_small_or_imprecise_dtypes=True))
        pool_const(pool.iota(tile_no[:, :], pattern=[[1, NT]], base=0, channel_multiplier=0,
                             allow_small_or_imprecise_dtypes=True))
        pool_const(pool.memset(minus_half[:, :], -0.5))
        pool_const(pool.memset(pad_row[:, :], 0.0))
        pool_const(pool.memset(pad_row[:, H:H + 1], NO_TOKEN))
        pool_const(pool.memset(routed[:, :], 0.0))
        for g in range(G):
            pool_const(pool.memset(state[g][D:P, :, :, :], 0.0))
            pool_const(pool.memset(raw[g][:, :, :, :], 0.0))

        t_first = sb("t_first", [P, NB, P])
        pool_const(pool.memset(t_first[:, :, :], 0.0))

        s_prep = sem("s_prep")
        nc.vector.wait_ge(s_load, 16 * len(loads))
        for k in range(KH):
            nc.vector.tensor_tensor(w_gt[:, k, 0:H], w_gt[:, k, 0:H], norm_g[:, :], ALU.mult).then_inc(s_prep, 1)
        nc.vector.tensor_tensor(bias_gt[:, 0:H], bias_gt[:, 0:H], norm_g[:, :], ALU.mult).then_inc(s_prep, 1)
        nc.vector.tensor_scalar(bias_ae[:, :], bias_ae[:, :], 0.5, None, ALU.mult).then_inc(s_prep, 1)
        n_prep = KH + 2
        for e in (nc.tensor, nc.scalar, nc.vector, nc.gpsimd, nc.sync):
            e.wait_ge(s_load, 16 * len(loads))
            e.wait_ge(s_const, n_const)
            e.wait_ge(s_prep, n_prep)

        with ExitStack() as inner:
            sb1 = lambda name, shape, dt=F32: inner.enter_context(nc.sbuf_tensor(name, shape, dt))
            loop1(nc, ctx, sb1, sem, dict(locals()), plan and plan["loop1"], plans)
        tiles(nc, ctx, sb, sem, dict(locals()))
        loop2(nc, ctx, sb, sem, dict(locals()), plan and plan["loop2"], plans)
    return plans


def loop1(nc, ctx, sb, sem, v, plan, plans):
    dram, banks = v["dram"], v["banks"]
    w_kv, w_q, w_ae, w_gt, bias_gt, w_o = (v[n] for n in ("w_kv", "w_q", "w_ae", "w_gt", "bias_gt", "w_o"))
    conv_w, conv_b, bias_ae, w_route = (v[n] for n in ("conv_w", "conv_b", "bias_ae", "w_route"))
    ident, ident_nb, ident_g, ones_a, ones_e = (v[n] for n in ("ident", "ident_nb", "ident_g", "ones_a", "ones_e"))
    ones_bf, before, rank, region0, token = (v[n] for n in ("ones_bf", "before", "rank", "region0", "token"))
    minus_half, state, w2, raw, routed = (v[n] for n in ("minus_half", "state", "w2", "raw", "routed"))
    t_first, sorted_rows = v["t_first"], v["sorted_rows"]
    NG = H + D

    pe, act, dve, pool, sp = nc.tensor, nc.scalar, nc.vector, nc.gpsimd, nc.sync
    M = Marks(nc, ctx, "l1", plan)
    mark, wait = M.mark, M.wait

    def two(name, shape, dt=F32):
        return [sb(f"{name}{i}", shape, dt) for i in range(2)]

    x = [sb(f"x{g}", [P, NB, H]) for g in range(G)]
    s_x = [sem(f"s_x{g}") for g in range(G)]
    gt = [sb(f"gt{g}", [P, NB, NG]) for g in range(G)]
    xt = sb("xt", [P, KH, NB * P])
    kv = two("kv", [P, NB, P])
    q = two("q", [P, NB, P])
    tanh_ae = sb("tanh_ae", [P, NB * P])
    decay = two("decay", [P, 3, NB, P])
    soft = sb("soft", [P, 3, NB, D])
    theta = two("theta", [P, NB])
    resp_c = two("resp_c", [P, NB, P])
    resp_e = sb("resp_e", [P, NB, P])
    ends = two("ends", [P, NB, 2])
    carry = two("carry", [P, NB, P])
    carry_f = sb("carry_f", [P, NB, P])
    kv_n = two("kv_n", [P, 2, NB, D])
    kq = two("kq", [P, NB, P])
    ab_q = two("ab_q", [P, NB, P])
    g_dec = two("g_dec", [P, NB, 2, D])
    ck = two("ck", [P, NB, 2, D])
    sq_k = sb("sq_k", [P, NB, D])
    norms = two("norms", [P, 4, NB])
    t_z = sb("t_z", [P, NB, D])
    sig = sb("sig", [P, NB, D])
    h = sb("h", [P, NB, D])
    h_t = two("h_t", [D, NB, P])
    grad = sb("grad", [P, 2, NB, D])
    dz_w = two("dz_w", [P, NB, 2, D])
    e_w = two("e_w", [P, NB, D])
    e_t = sb("e_t", [D, NB, P])
    ds = sb("ds", [P, 2, NB, D])
    sq = sb("sq", [P, 3, NB, D])
    ch = two("ch", [P, NB, 2, D])
    small = sb("small", [P, 8, NB])
    t_q = sb("t_q", [P, NB, P])
    hq = sb("hq", [P, NB, P])
    hh = sb("hh", [P, NB, P])
    ab_h = sb("ab_h", [P, NB, P])
    ret = two("ret", [D, NB, P])
    junk = sb("junk", [P, H])
    ssq = sb("ssq", [P, NB])
    rms = sb("rms", [P, 2, NB])
    y = sb("y", [P, NB, H])
    stats = sb("stats", [P, NB, 6])
    mv = sb("mv", [P, NB, 2])
    rstd = sb("rstd", [P, 2, NB])
    rows = two("rows", [P, NB, ROW])
    rows_t = sb("rows_t", [P, KH, NB * P])
    best = sb("best", [P, 2, NB])
    pick = sb("pick", [P, 3, NB, NE])
    onehot = sb("onehot", [P, NB, NE], BF16)
    total = sb("total", [P, NE])
    where = sb("where", [P, 2, NB, NE])
    where_f = sb("where_f", [P, NB])
    index = two("index", [P, NB], I32)
    s_scatter = [sem(f"s_scatter{i}") for i in range(2)]

    pro = Slots("pro", banks[0:3], plan)
    lrn = Slots("lrn", banks[3:4], plan)
    rtv = Slots("rtv", banks[4:5], plan)
    new = Slots("new", banks[5:6], plan)
    epi = Slots("epi", banks[6:8], plan)
    rings = (pro, lrn, rtv, new, epi)

    def grab(slots, use):
        i, bank, last = slots.take(use)
        wait("pe", last)
        return i, bank

    hidden = dram["hidden"].rearrange("b (c s) h -> c s b h", s=P)
    flat = lambda a: a.rearrange("p b t -> p (b t)")

    def names(g):
        return tuple((lambda name, g_=(g - k) % G: f"{name}.{g_}") for k in range(3))

    def project(c, g):
        n, o, o2 = names(g)
        i2 = g % 2
        X, KV, Q = x[g], kv[i2], q[i2]
        wait("sp", n("res"))
        sp.dma_start(X[:, :, :], hidden[c][:, g * NB:(g + 1) * NB, :]).then_inc(s_x[g], 16)
        pe.wait_ge(s_x[g], c * 16 + 16)
        for k in range(KH):
            i, bank = grab(pro, n(f"xt{k}"))
            for b in range(NB):
                ins = pe.transpose(bank[:, b * P:(b + 1) * P], X[:, b, k * P:(k + 1) * P], ident[:, :])
            mark("pe", n(f"xt_ps{k}"), ins)
            wait("act", n(f"xt_ps{k}"), o(f"gt_ps{NB - 1}"), o("ae_ps"))
            mark("act", n(f"xt{k}"), act.activation(xt[:, k, :], bank[:, :], ACT.Copy))
            pro.freed_by(i, n(f"xt{k}"))
            yield
        wait("dve", n("conv_kv"), n("conv_q"))
        mark("dve", n("halo"), dve.tensor_copy(raw[g][:, :, :, 0:3], raw[g][:, :, :, P:P + 3]))
        wait("pe", n("xt0"), n("xt1"))
        for j, (name, w) in enumerate((("kv", w_kv), ("q", w_q))):
            i, bank = grab(pro, n(name))
            for k in range(KH):
                ins = pe.matmul(bank[:, :], w[:, k, :], xt[:, k, :], start=k == 0, stop=k == KH - 1)
            mark("pe", n(f"{name}_ps"), ins)
            wait("act", n(f"{name}_ps"), n("halo"))
            mark("act", n(f"{name}_raw"),
                 act.activation(raw[g][:, j, :, 3:P + 3], bank[:, :].rearrange("p (b t) -> p b t", b=NB), ACT.Copy))
            pro.freed_by(i, n(f"{name}_raw"))
            yield
        i, bank = grab(pro, n("ae"))
        for k in range(KH):
            ins = pe.matmul(bank[:, :], w_ae[:, k, :], xt[:, k, :], start=k == 0, stop=k == KH - 1)
        mark("pe", n("ae_ps"), ins)
        wait("act", n("ae_ps"), o("sum_e"))
        mark("act", n("tanh_ae"), act.activation(tanh_ae[:, :], bank[:, :], ACT.Tanh, bias=bias_ae[:, 0:1], scale=0.5))
        pro.freed_by(i, n("tanh_ae"))
        yield
        for j, (name, dst) in enumerate((("kv", KV), ("q", Q))):
            last = (o2("kq_ps"), o2("kv_n_ps"), o2("z_ps")) if name == "kv" else (o2("kq_ps"), o2("ab_q"))
            wait("act", n(f"{name}_raw"), n("halo"), *last)
            mark("act", n(f"conv_{name}0"),
                 act.activation(dst[:, :, :], raw[g][:, j, :, 0:P], ACT.Identity, bias=conv_b[:, j:j + 1], scale=conv_w[:, j, 0:1]))
            for tap in range(1, 4):
                wait("dve", n(f"conv_{name}{tap - 1}"))
                mark("dve", n(f"conv_{name}{tap}" if tap < 3 else f"conv_{name}"),
                     dve.scalar_tensor_tensor(dst[:, :, :], raw[g][:, j, :, tap:tap + P], conv_w[:, j, tap:tap + 1],
                                              dst[:, :, :], ALU.mult, ALU.add))
            yield
        wait("pe", n("tanh_ae"))
        scale_a, shift_a = -0.5 * 0.1 / D, 1 - 0.5 * 0.1
        scale_e, shift_e = 0.5 * 0.9 / D, 0.5 * 0.9 + 0.05
        for name, ones, w, rows_, scale, shift in (("a", ones_a, 0, slice(0, D), scale_a, shift_a),
                                                   ("e", ones_e, 1, slice(D, P), scale_e, shift_e)):
            i, bank = grab(pro, n(f"sum_{name}"))
            mark("pe", n(f"sum_{name}"), pe.matmul(bank[:, :], ones[:, :], tanh_ae[:, :], start=True, stop=True))
            v4 = bank[:, :].rearrange("p (b t) -> p b t", b=NB)
            wait("act", n(f"sum_{name}"), o2("scan_b"))
            act.activation(decay[i2][:, w, :, :], v4, ACT.Copy, bias=shift, scale=scale)
            mark("act", n(f"dec_{name}"), act.activation(decay[i2][rows_, 2, :, :], v4[rows_], ACT.Copy, bias=shift, scale=scale))
            pro.freed_by(i, n(f"dec_{name}"))
            yield
        for b in range(NB):
            i, bank = grab(pro, n(f"gt{b}"))
            for k in range(KH):
                ins = pe.matmul(bank[:, 0:NG], xt[:, k, b * P:(b + 1) * P], w_gt[:, k, :], start=k == 0, stop=k == KH - 1)
            mark("pe", n(f"gt_ps{b}"), ins)
            wait("dve", n(f"gt_ps{b}"), n(f"gated{b}"), n("soft"))
            mark("dve", n(f"gt{b}"), dve.tensor_tensor(gt[g][:, b, :], bank[:, 0:NG], bias_gt[:, :], ALU.add))
            pro.freed_by(i, n(f"gt{b}"))
            yield
        u = gt[g][:, :, H:NG]
        wait("act", n(f"gt{NB - 1}"), o("theta0"))
        mark("act", n("abs_u"), act.activation(soft[:, 0, :, :], u, ACT.Abs))
        wait("act", n("abs_u"))
        mark("act", n("exp_u"), act.activation(soft[:, 1, :, :], soft[:, 0, :, :], ACT.Exp, scale=-1.0))
        wait("act", n("exp_u"))
        mark("act", n("ln_u"), act.activation(soft[:, 2, :, :], soft[:, 1, :, :], ACT.Ln, bias=1.0))
        yield
        wait("dve", n("ln_u"))
        mark("dve", n("soft"), dve.scalar_tensor_tensor(soft[:, 0, :, :], u, 0.0, soft[:, 2, :, :], ALU.max, ALU.add))
        wait("dve", n("soft"), o2("weight"))
        mark("dve", n("theta0"), dve.tensor_reduce(theta[i2][:, :], soft[:, 0, :, :], AX.X, ALU.add))
        wait("dve", n("theta0"))
        mark("dve", n("theta"), dve.tensor_scalar(theta[i2][:, :], theta[i2][:, :], -GRAD_SCALE * LR / D, None, ALU.mult))
        yield

    def respond(c, g):
        n, o, o2 = names(g)
        i2 = g % 2
        KV, Q = kv[i2], q[i2]
        i, bank = grab(pro, n("kv_n"))
        wait("pe", n("conv_kv"))
        for b in range(NB):
            ins = pe.transpose(bank[:, b * P:(b + 1) * P], KV[:, b, :], ident[:, :])
        mark("pe", n("kv_n_ps"), ins)
        vb = bank[:, :].rearrange("p (b two d) -> p two b d", b=NB, two=2)
        wait("act", n("kv_n_ps"), o2("ck"), o2("e2"), o2("sq_k"))
        act.activation(kv_n[i2][:, 0], vb[:, 0], ACT.Copy)
        mark("act", n("kv_n"), act.activation(kv_n[i2][:, 1], vb[:, 1], ACT.Copy, scale=2.0))
        pro.freed_by(i, n("kv_n"))
        wait("dve", n("dec_a"), n("dec_e"), o("scan_f"))
        mark("dve", n("first"), dve.tensor_copy(t_first[:, :, 0:1], decay[i2][:, 2, :, 0:1]))
        wait("dve", n("first"))
        mark("dve", n("clear"), dve.memset(decay[i2][:, :, :, 0:1], 0.0))
        C, E_, AB, AF = (flat(a[:, :, :]) for a in (resp_c[i2], resp_e, carry[i2], carry_f))
        dec_a, dec_e, dec_ae = (flat(decay[i2][:, j]) for j in range(3))
        wait("pool", n("kv_n"), o("norm_k"))
        mark("pool", n("sq_k"), pool.tensor_tensor(sq_k[:, :, :], kv_n[i2][:, 0], kv_n[i2][:, 0], ALU.mult))
        yield
        wait("dve", n("clear"), o("end_e"))
        mark("dve", n("scan_e"), dve.tensor_tensor_scan(E_, dec_e, flat(ident_nb[:, :, :]), 0.0, ALU.mult, ALU.add))
        wait("dve", n("first"), o("g_dec_s"), o("copy_a"))
        mark("dve", n("scan_f"), dve.tensor_tensor_scan(AF, dec_ae, flat(t_first[:, :, :]), 0.0, ALU.mult, ALU.add))
        wait("act", n("scan_f"), o2("ab_h"), o2("g_dec"))
        mark("act", n("copy_a"), act.activation(AB[0:D], AF[0:D], ACT.Copy))
        yield
        wait("dve", n("scan_e"), o2("p2"))
        mark("dve", n("scan_c"), dve.tensor_tensor_scan(C, dec_a, E_, 0.0, ALU.mult, ALU.add))
        wait("dve", n("scan_f"), o2("ab_h"))
        mark("dve", n("scan_b"), dve.tensor_tensor_scan(AB[D:P], dec_a[D:P], AF[D:P], 0.0, ALU.mult, ALU.add))
        wait("dve", n("scan_c"), o2("ck"), o2("ch"))
        mark("dve", n("end_e"), dve.tensor_copy(ends[i2][:, :, 1:2], resp_e[:, :, P - 1:P]))
        mark("dve", n("ends"), dve.tensor_copy(ends[i2][:, :, 0:1], resp_c[i2][:, :, P - 1:P]))
        yield
        i, bank = grab(pro, n("kq"))
        wait("pe", n("conv_q"))
        for b in range(NB):
            ins = pe.matmul(bank[:, b * P:(b + 1) * P], KV[0:D, b, :], Q[0:D, b, :], start=True, stop=True)
        mark("pe", n("kq_ps"), ins)
        wait("dve", n("kq_ps"), n("scan_c"), o2("zq_ps"))
        mark("dve", n("kq"), dve.tensor_tensor(flat(kq[i2][:, :, :]), bank[:, :], C, ALU.mult))
        pro.freed_by(i, n("kq"))
        wait("pool", n("conv_q"), n("copy_a"), n("scan_b"), o2("zq_ps"))
        mark("pool", n("ab_q"), pool.tensor_tensor(ab_q[i2][:, :, :], q[i2][:, :, :], carry[i2][:, :, :], ALU.mult))
        wait("dve", n("sq_k"), o2("norm_p"))
        mark("dve", n("norm_k"), dve.tensor_reduce(norms[i2][:, 0, :], sq_k[:, :, :], AX.X, ALU.add))
        yield
        wait("dve", n("scan_b"), n("copy_a"), o2("upd_ps"))
        for w, (name, src) in enumerate((("g_dec", carry[i2]), ("g_dec_s", carry_f))):
            mark("dve", n(name), dve.tensor_tensor(g_dec[i2][:, :, w, :], spread(ident_g[:, w:w + 1, :], 1, NB),
                                                   spread(src[:, :, P - 1:P], 2, D), ALU.mult))
        wait("pool", n("kv_n"), n("ends"), o2("upd_ps"))
        mark("pool", n("ck"), pool.tensor_tensor(ck[i2][:, :, :, :], spread(kv_n[i2][:, 0].unsqueeze(2), 2, 2), at_end(i2), ALU.mult))
        yield

    def at_end(i2):
        return spread(ends[i2][:, :, :].unsqueeze(3), 3, D)

    def learn(c, g):
        n, o, o2 = names(g)
        i2 = g % 2
        KV = kv[i2]
        ST, W2 = state[g], w2[g]
        i, zb = grab(lrn, n("z"))
        z = zb[:, 0:NB * D].rearrange("p (b d) -> p b d", b=NB)
        wait("pe", n("conv_kv"), n("state"))
        for b in range(NB):
            ins = pe.matmul(z[:, b, :], KV[0:D, b, :], ST[0:D, b, 0, :], start=True, stop=True)
        mark("pe", n("z_ps"), ins)
        wait("act", n("z_ps"), o("sig"))
        mark("act", n("t_z"), act.activation(t_z[:, :, :], z, ACT.Tanh, scale=0.5))
        wait("dve", n("t_z"), o("d_silu"))
        mark("dve", n("sig"), dve.tensor_scalar(sig[:, :, :], t_z[:, :, :], 0.5, 0.5, ALU.mult, ALU.add))
        wait("dve", n("sig"), o("ch"), o("h_ps"), o("sq_h"))
        mark("dve", n("h"), dve.tensor_tensor(h[:, :, :], z, sig[:, :, :], ALU.mult))
        lrn.freed_by(i, n("h"))
        yield
        i, bank = grab(lrn, n("h_t"))
        wait("pe", n("h"))
        M.apart("pe")
        for b in range(NB):
            ins = pe.transpose(bank[0:D, b * P:(b + 1) * P], h[:, b, :], ident[:, :])
        mark("pe", n("h_ps"), ins)
        wait("act", n("h_ps"), o2("hh_ps"))
        mark("act", n("h_t"), act.activation(flat(h_t[i2][:, :, :]), bank[0:D, :], ACT.Copy))
        lrn.freed_by(i, n("h_t"))
        wait("dve", n("h"), o("dz"))
        mark("dve", n("r"), dve.scalar_tensor_tensor(ds[:, 0], sig[:, :, :], 1.0, h[:, :, :], ALU.subtract, ALU.mult))
        wait("dve", n("r"))
        mark("dve", n("d_silu"), dve.tensor_tensor(ds[:, 1], sig[:, :, :], ds[:, 0], ALU.subtract))
        yield
        i, bank = grab(lrn, n("pred"))
        pred = bank[:, 0:NB * D].rearrange("p (b d) -> p b d", b=NB)
        wait("pe", n("h_t"))
        for b in range(NB):
            ins = pe.matmul(pred[:, b, :], h_t[i2][:, b, :], ST[0:D, b, 2, :], start=True, stop=True)
        mark("pe", n("pred_ps"), ins)
        wait("dve", n("pred_ps"), n("kv_n"), o("grad_w"), o("e_ps"), o("sq_e"))
        mark("dve", n("e2"), dve.scalar_tensor_tensor(grad[:, 1], pred, 2.0, kv_n[i2][:, 1], ALU.mult, ALU.subtract))
        lrn.freed_by(i, n("e2"))
        yield
        i, bank = grab(lrn, n("e_t"))
        wait("pe", n("e2"))
        M.apart("pe")
        for b in range(NB):
            ins = pe.transpose(bank[0:D, b * P:(b + 1) * P], grad[:, 1, b, :], ident[:, :])
        mark("pe", n("e_ps"), ins)
        wait("act", n("e_ps"), o("dh_ps"))
        mark("act", n("e_t"), act.activation(flat(e_t[:, :, :]), bank[0:D, :], ACT.Copy))
        lrn.freed_by(i, n("e_t"))
        wait("act", n("h"), o("norm_h"))
        mark("act", n("sq_h"), act.activation(sq[:, 0], h[:, :, :], ACT.Square))
        wait("act", n("e2"))
        mark("act", n("sq_e"), act.activation(sq[:, 2], grad[:, 1], ACT.Square))
        yield
        i, bank = grab(lrn, n("dh"))
        dh = bank[:, 0:NB * D].rearrange("p (b d) -> p b d", b=NB)
        wait("pe", n("e_t"), n("w2"))
        for b in range(NB):
            ins = pe.matmul(dh[:, b, :], e_t[:, b, :], W2[:, b, :], start=True, stop=True)
        mark("pe", n("dh_ps"), ins)
        wait("dve", n("dh_ps"), n("d_silu"), o("sq_z"))
        mark("dve", n("dz"), dve.tensor_tensor(grad[:, 0], dh, ds[:, 1], ALU.mult))
        lrn.freed_by(i, n("dz"))
        wait("act", n("dz"))
        mark("act", n("sq_z"), act.activation(sq[:, 1], grad[:, 0], ACT.Square))
        yield
        wait("dve", n("sq_z"), n("sq_h"), n("sq_e"), n("norm_k"))
        mark("dve", n("norm_h"), dve.tensor_reduce(norms[i2][:, 1:4, :], sq[:, :, :, :], AX.X, ALU.add))
        wait("dve", n("norm_h"))
        mark("dve", n("norm_p"), dve.tensor_tensor(small[:, 0:2, :], norms[i2][:, 0:2, :], norms[i2][:, 2:4, :], ALU.mult))
        wait("dve", n("norm_p"))
        mark("dve", n("norm_s"), dve.tensor_tensor(small[:, 2, :], small[:, 0, :], small[:, 1, :], ALU.add))
        wait("dve", n("norm_s"))
        mark("dve", n("norm_g"), dve.tensor_scalar(small[:, 3, :], small[:, 2, :], GRAD_SCALE ** 2, 1e-12, ALU.mult, ALU.max))
        wait("pool", n("norm_g"))
        mark("pool", n("inv_g"), pool.tensor_tensor(small[:, 4, :], small[:, 3, :], minus_half[:, 0:NB], ALU.pow))
        wait("pool", n("h"), o2("upd_ps"), n("ends"))
        mark("pool", n("ch"), pool.tensor_tensor(ch[i2][:, :, :, :], spread(h[:, :, :].unsqueeze(2), 2, 2), at_end(i2), ALU.mult))
        yield
        wait("dve", n("inv_g"), n("theta"))
        mark("dve", n("weight"), dve.scalar_tensor_tensor(small[:, 5, :], small[:, 4, :], 1.0, theta[i2][:, :], ALU.min, ALU.mult))
        wait("dve", n("weight"), o2("upd_ps"), o2("out_ps"), o2("zq_ps"))
        wgt = small[:, 5, :].unsqueeze(2)
        mark("dve", n("dz_w"), dve.tensor_tensor(dz_w[i2][:, :, :, :], spread(grad[:, 0].unsqueeze(2), 2, 2),
                                                 spread(spread(wgt, 2, 2).unsqueeze(3), 3, D), ALU.mult))
        mark("dve", n("grad_w"), dve.tensor_tensor(e_w[i2][:, :, :], grad[:, 1], spread(wgt, 2, D), ALU.mult))
        yield

    def retrieve(c, g):
        n, o, o2 = names(g)
        i2 = g % 2
        C = resp_c[i2][:, :, :]
        ST, W2 = state[g], w2[g]
        i, bank = grab(rtv, n("zq"))
        wait("pe", n("grad_w"), n("kq"), n("ab_q"))
        for b in range(NB):
            zq = bank[:, b * P:(b + 1) * P]
            pe.matmul(zq, ST[:, b, 0:2, :].rearrange("p w d -> p (w d)"), ab_q[i2][:, b, :], start=True, stop=False)
            ins = pe.matmul(zq, dz_w[i2][:, b].rearrange("p w d -> p (w d)"), kq[i2][:, b, :], start=False, stop=True)
        mark("pe", n("zq_ps"), ins)
        wait("act", n("zq_ps"), o("hq"))
        mark("act", n("t_q"), act.activation(flat(t_q[:, :, :]), bank[:, :], ACT.Tanh, scale=0.5))
        wait("dve", n("t_q"), o("hh_ps"), o("ab_h"))
        mark("dve", n("hq"), dve.scalar_tensor_tensor(flat(hq[:, :, :]), flat(t_q[:, :, :]), 1.0, bank[:, :], ALU.add, ALU.mult))
        rtv.freed_by(i, n("hq"))
        wait("pool", n("hq"), n("copy_a"), n("scan_b"), o("out_ps"))
        mark("pool", n("ab_h"), pool.tensor_tensor(ab_h[:, :, :], hq[:, :, :], carry[i2][:, :, :], ALU.mult))
        yield
        iu, upd = grab(new, n("upd"))
        wait("pe", n("g_dec"), n("ck"), n("ch"))
        for b in range(NB):
            ub = upd[:, b * P:(b + 1) * P]
            pe.matmul(ub, g_dec[i2][:, b].rearrange("p w d -> p (w d)"), ST[:, b, 1:3].rearrange("p w d -> p (w d)"), start=True, stop=False)
            pe.matmul(ub[:, 0:D], ck[i2][:, b].rearrange("p w d -> p (w d)"), dz_w[i2][:, b, 0, :], start=False, stop=False)
            ins = pe.matmul(ub[:, D:P], ch[i2][:, b].rearrange("p w d -> p (w d)"), e_w[i2][:, b, :], start=False, stop=True)
        mark("pe", n("upd_ps"), ins)
        yield
        i, bank = grab(rtv, n("hh"))
        wait("pe", n("hq"))
        for b in range(NB):
            ins = pe.matmul(bank[:, b * P:(b + 1) * P], h_t[i2][:, b, :], hq[0:D, b, :], start=True, stop=True)
        mark("pe", n("hh_ps"), ins)
        wait("dve", n("hh_ps"), o("out_ps"))
        mark("dve", n("p2"), dve.tensor_tensor(flat(hh[:, :, :]), bank[:, :], flat(C), ALU.mult))
        rtv.freed_by(i, n("p2"))
        yield
        i, bank = grab(rtv, n("out"))
        wait("pe", n("p2"), n("ab_h"))
        for b in range(NB):
            ob = bank[0:D, b * P:(b + 1) * P]
            pe.matmul(ob, ST[:, b, 2, :], ab_h[:, b, :], start=True, stop=False)
            ins = pe.matmul(ob, e_w[i2][:, b, :], hh[:, b, :], start=False, stop=True)
        mark("pe", n("out_ps"), ins)
        wait("act", n("out_ps"), o2("wo_ps1"))
        mark("act", n("ret"), act.activation(flat(ret[i2][:, :, :]), bank[0:D, :], ACT.Copy, scale=0.5))
        rtv.freed_by(i, n("ret"))
        wait("act", n("upd_ps"))
        u4 = upd[:, :].rearrange("p (b w d) -> p b w d", b=NB, w=2)
        act.activation(ST[:, :, 0:2, :], spread(u4[:, :, 0:1, :], 2, 2), ACT.Copy)
        mark("act", n("state"), act.activation(ST[:, :, 2, :], u4[:, :, 1, :], ACT.Copy))
        new.freed_by(iu, n("state"))
        yield
        i, bank = grab(rtv, n("w2"))
        wait("pe", n("state"))
        M.apart("pe")
        for b in range(NB):
            ins = pe.transpose(bank[0:D, b * P:(b + 1) * P], ST[:, b, 2, :], ident[:, :])
        mark("pe", n("w2_ps"), ins)
        wait("act", n("w2_ps"), n("dh_ps"))
        mark("act", n("w2"), act.activation(W2[:, :, :], bank[0:D, :].rearrange("p (b d) -> p b d", b=NB)[:, :, 0:D], ACT.Copy))
        rtv.freed_by(i, n("w2"))
        yield

    def epilogue(c, g):
        n, o, o2 = names(g)
        i2 = g % 2
        X, Y, R = x[g], y, rows[i2]
        held = []
        for j in range(2):
            i, bank = grab(epi, n(f"wo{j}"))
            held.append((i, bank))
            wait("pe", n("ret"))
            for b in (2 * j, 2 * j + 1):
                ins = pe.matmul(bank[:, (b % 2) * H:(b % 2 + 1) * H], ret[i2][:, b, :], w_o[:, :], start=True, stop=True)
            mark("pe", n(f"wo_ps{j}"), ins)
            wait("act", n(f"wo_ps{j}"), o("ms"))
            for b in (2 * j, 2 * j + 1):
                prev = n(f"ssq{b - 1}") if b else o(f"ssq{NB - 1}")
                wait("act", prev)
                mark("act", n(f"ssq{b}"), act.activation(junk[:, :], bank[:, (b % 2) * H:(b % 2 + 1) * H], ACT.Square, accum_out=ssq[:, b:b + 1]))
        yield
        wait("dve", *[n(f"ssq{b}") for b in range(NB)])
        wait("dve", o("rms"))
        mark("dve", n("ms"), dve.tensor_scalar(rms[:, 0, :], ssq[:, :], 1.0 / H, EPS_RMS, ALU.mult, ALU.add))
        wait("pool", n("ms"), o(f"gated{NB - 1}"))
        mark("pool", n("rms"), pool.tensor_tensor(rms[:, 1, :], rms[:, 0, :], minus_half[:, 0:NB], ALU.pow))
        yield
        for b in range(NB):
            i, bank = held[b // 2]
            wait("dve", n("rms"), n(f"gt{b}"), o("norm3"))
            mark("dve", n(f"gated{b}"), dve.scalar_tensor_tensor(Y[:, b, :], bank[:, (b % 2) * H:(b % 2 + 1) * H], rms[:, 1, b:b + 1],
                                                                 gt[g][:, b, 0:H], ALU.mult, ALU.mult))
            if b % 2:
                epi.freed_by(i, n(f"gated{b}"))
        yield
        wait("pool", *[n(f"gated{b}") for b in range(NB)])
        mark("pool", n("res"), pool.tensor_tensor(Y[:, :, :], Y[:, :, :], X[:, :, :], ALU.add))
        yield
        wait("dve", n("res"), o("mv3"))
        for b in range(NB):
            mark("dve", n(f"stats{b}"), dve.bn_stats(stats[:, b, :], Y[:, b, :]))
        wait("dve", o("norm3"), o("var"))
        for b in range(NB):
            wait("dve", n(f"stats{b}"))
            M.apart("dve")
            mark("dve", n(f"mv{b}"), dve.bn_aggr(mv[:, b, :], stats[:, b, :]))
        wait("dve", n("mv3"), o("rstd"))
        mark("dve", n("var"), dve.tensor_scalar(rstd[:, 0, :], mv[:, :, 1], EPS_LN, None, ALU.add))
        wait("pool", n("var"))
        mark("pool", n("rstd"), pool.tensor_tensor(rstd[:, 1, :], rstd[:, 0, :], minus_half[:, 0:NB], ALU.pow))
        yield
        dve.wait_ge(s_scatter[i2], c * (2 * NB * 16) + (g // 2) * NB * 16 + 16)
        wait("dve", n("rstd"), o2("rt_ps1"))
        for b in range(NB):
            mark("dve", n(f"norm{b}"), dve.tensor_scalar(R[:, b, 0:H], Y[:, b, :], mv[:, b, 0:1], rstd[:, 1, b:b + 1], ALU.subtract, ALU.mult))
        mark("dve", n("token"), dve.tensor_copy(R[:, :, H:H + 1], token[:, g * NB:(g + 1) * NB].unsqueeze(2)))
        wait("dve", n("token"))
        mark("dve", n("next_token"), dve.tensor_scalar(token[:, g * NB:(g + 1) * NB], token[:, g * NB:(g + 1) * NB], float(P), None, ALU.add))
        yield
        for k in range(KH):
            i, bank = grab(epi, n(f"rt{k}"))
            wait("pe", n("norm3"))
            for b in range(NB):
                ins = pe.transpose(bank[:, b * P:(b + 1) * P], R[:, b, k * P:(k + 1) * P], ident[:, :])
            mark("pe", n(f"rt_ps{k}"), ins)
            wait("act", n(f"rt_ps{k}"), o("score_ps"))
            mark("act", n(f"rt{k}"), act.activation(rows_t[:, k, :], bank[:, :], ACT.Copy))
            epi.freed_by(i, n(f"rt{k}"))
        yield
        i, bank = grab(epi, n("score"))
        score = bank[:, 0:NB * NE].rearrange("p (b e) -> p b e", b=NB)
        wait("pe", n("rt0"), n("rt1"))
        for b in range(NB):
            for k in range(KH):
                ins = pe.matmul(score[:, b, :], rows_t[:, k, b * P:(b + 1) * P], w_route[:, k, :], start=k == 0, stop=k == KH - 1)
        mark("pe", n("score_ps"), ins)
        wait("dve", n("score_ps"))
        mark("dve", n("best"), dve.tensor_reduce(best[:, 0, :], score, AX.X, ALU.max))
        wait("dve", n("best"))
        mark("dve", n("is_best"), dve.tensor_tensor(pick[:, 0], score, spread(best[:, 0, :].unsqueeze(2), 2, NE), ALU.is_ge))
        epi.freed_by(i, n("is_best"))
        wait("dve", n("is_best"))
        mark("dve", n("ranked"), dve.tensor_tensor(pick[:, 1], pick[:, 0], spread(rank[:, :].unsqueeze(1), 1, NB), ALU.mult))
        wait("dve", n("ranked"))
        mark("dve", n("top"), dve.tensor_reduce(best[:, 1, :], pick[:, 1], AX.X, ALU.max))
        wait("dve", n("top"), o("pos_ps"))
        mark("dve", n("onehot"), dve.tensor_tensor(onehot[:, :, :], spread(rank[:, :].unsqueeze(1), 1, NB),
                                                   spread(best[:, 1, :].unsqueeze(2), 2, NE), ALU.is_equal))
        yield
        i, bank = grab(epi, n("pos"))
        pos = bank[:, 0:NB * NE].rearrange("p (b e) -> p b e", b=NB)
        wait("pe", n("onehot"), o("routed"))
        pe.matmul(pos, before[:, :], onehot[:, :, :], start=True, stop=False)
        for b in range(NB - 1):
            pe.matmul(pos[:, b + 1:NB, :], ones_bf[:, :], spread(onehot[:, b:b + 1, :], 1, NB - 1 - b), start=False, stop=False)
        ins = pe.matmul(pos, ones_bf[:, :], spread(routed[:, :].unsqueeze(1), 1, NB), start=False, stop=True)
        mark("pe", n("pos_ps"), ins)
        wait("dve", n("onehot"))
        mark("dve", n("total"), dve.tensor_reduce(total[:, :], onehot[:, :, :].rearrange("p b e -> p e b"), AX.X, ALU.add))
        wait("dve", n("total"), n("pos_ps"))
        mark("dve", n("routed"), dve.tensor_tensor(routed[:, :], routed[:, :], total[:, :], ALU.add))
        mark("dve", n("where0"), dve.tensor_tensor(where[:, 0], pos, spread(region0[:, :].unsqueeze(1), 1, NB), ALU.add))
        epi.freed_by(i, n("where0"))
        wait("dve", n("where0"))
        mark("dve", n("where1"), dve.tensor_tensor(where[:, 1], where[:, 0], onehot[:, :, :], ALU.mult))
        wait("dve", n("where1"))
        mark("dve", n("where_f"), dve.tensor_reduce(where_f[:, :], where[:, 1], AX.X, ALU.add))
        wait("dve", n("where_f"))
        mark("dve", n("index"), dve.tensor_copy(index[i2][:, :], where_f[:, :]))
        wait("pool", n("index"), n("norm3"), n("token"))
        M.apart("pool")
        for b in range(NB):
            pool.indirect_dma_start(sorted_rows[:, :], bass.IndirectOffsetOnAxis(index[i2][:, b:b + 1], 0), R[:, b, :], None,
                                    bounds_check=NE * REGION - 1, oob_is_err=False).then_inc(s_scatter[i2], 16)
        yield

    s_blank = sem("s_blank")
    for r in rows:
        pool.memset(r[:, :, H:ROW], 0.0).then_inc(s_blank, 1)
    dve.wait_ge(s_blank, 2)
    for j in range(2):
        lo = NE * REGION + j * (P // 2)
        pool.dma_start(sorted_rows[lo:lo + P // 2, :], v["pad_row"][j * D:(j + 1) * D, :]).then_inc(s_scatter[j], 16)

    STAGES = dict(p=(project, 0), s=(respond, 1), l=(learn, 1), r=(retrieve, 2), e=(epilogue, 3))

    def slot(c, g, first=False, tail=False):
        stages = {}
        for letter, (make, lag) in STAGES.items():
            step = g - lag
            if tail and step >= 0:
                continue
            if first and step < 0:
                continue
            stages[letter] = make(c if step >= 0 else c - 1, step % G)
        for letter in ORDER:
            if letter in stages:
                next(stages[letter])

    M.begin(0, first=True)
    for g in range(G):
        slot(0, g, first=True)
    M.fill()
    with nc.Fori(1, NC) as c:
        M.begin(c)
        for s in rings:
            s.begin()
        for g in range(G):
            slot(c, g)
    body = dict(count=M.count, at=M.at, slots={s.name: (dict(s.last), dict(s.place)) for s in rings})
    M.begin(NC)
    wait("sp", f"conv_kv.{G - 1}", f"conv_q.{G - 1}")
    for k in range(KH):
        sp.dma_start(v["w_expert"][:, k, :, :], dram["w_expert"][:, k * P:(k + 1) * P, :].rearrange("e p f -> p e f")).then_inc(v["s_expert"], 16)
    for g in range(G - 1):
        slot(NC, g, tail=True)
    plans["loop1"] = body
    for e in (pe, act, dve, pool, sp):
        for who, s in M.sem.items():
            e.wait_ge(s, M.per_lap[who] * NC + M.count[who])
        for s in s_scatter:
            e.wait_ge(s, NC * 2 * NB * 16 + 16)


ORDER = "ppslepplspesleperelpepprprlsperepsprellpp"


def tiles(nc, ctx, sb, sem, v):
    routed, ones_bf, region0, tile_no, pad_row = (v[n] for n in ("routed", "ones_bf", "region0", "tile_no", "pad_row"))
    banks, sorted_rows = v["banks"], v["sorted_rows"]
    pe, dve, pool = nc.tensor, nc.vector, nc.gpsimd
    s_cnt, s_d, s_pad, s_io = sem("s_cnt"), sem("s_tiles"), sem("s_pad"), sem("s_iota")
    lane = sb("lane", [P, 1])
    n_tok = sb("n_tok", [P, NE])
    pad_f = sb("pad_f", [P, NE])
    pad_i = sb("pad_i", [P, NE], I32)
    nt_i = sb("nt_i", [P, 2, NE], I32)
    nt = sb("nt", [P, NE])
    cum = sb("cum", [P, NE])
    one = sb("one", [P, NE])
    past = sb("past", [P, NT, NE])
    first = sb("first", [P, NT, NE])
    e_of = sb("e_of", [P, 2, NT])
    f_of = sb("f_of", [P, 4, NT])
    tile_row = sb("tile_row", [P, NT], I32)
    tile_expert = sb("tile_expert", [P, NT], I32)
    made = [0]

    def step(instruction):
        made[0] += 1
        instruction.then_inc(s_d, 1)
        dve.wait_ge(s_d, made[0])

    pool.iota(lane[:, :], pattern=[[0, 1]], base=0, channel_multiplier=1, allow_small_or_imprecise_dtypes=True).then_inc(s_io, 1)
    pe.matmul(banks[0][:, 0:NE], ones_bf[:, :], routed[:, :], start=True, stop=True).then_inc(s_cnt, 1)
    dve.wait_ge(s_cnt, 1)
    dve.wait_ge(s_io, 1)
    step(dve.tensor_copy(n_tok[:, :], banks[0][:, 0:NE]))
    step(dve.tensor_tensor(pad_f[:, :], n_tok[:, :], region0[:, :], ALU.add))
    step(dve.tensor_scalar(pad_f[:, :], pad_f[:, :], lane[:, 0:1], None, ALU.add))
    step(dve.tensor_copy(pad_i[:, :], pad_f[:, :]))
    pad_ready = made[0]
    step(dve.tensor_scalar(n_tok[:, :], n_tok[:, :], float(P - 1), None, ALU.add))
    step(dve.tensor_copy(nt_i[:, 0, :], n_tok[:, :]))
    step(dve.tensor_scalar(nt_i[:, 1, :], nt_i[:, 0, :], 7, None, ALU.arith_shift_right))
    step(dve.tensor_copy(nt[:, :], nt_i[:, 1, :]))
    step(dve.memset(one[:, :], 1.0))
    step(dve.tensor_tensor_scan(cum[:, :], one[:, :], nt[:, :], 0.0, ALU.mult, ALU.add))
    step(dve.tensor_tensor(past[:, :, :], spread(tile_no[:, :].unsqueeze(2), 2, NE), spread(cum[:, :].unsqueeze(1), 1, NT), ALU.is_ge))
    step(dve.tensor_reduce(e_of[:, 0, :], past[:, :, :], AX.X, ALU.add))
    step(dve.tensor_tensor(first[:, :, :], past[:, :, :], spread(nt[:, :].unsqueeze(1), 1, NT), ALU.mult))
    step(dve.tensor_reduce(f_of[:, 0, :], first[:, :, :], AX.X, ALU.add))
    step(dve.tensor_tensor(f_of[:, 1, :], tile_no[:, :], f_of[:, 0, :], ALU.subtract))
    step(dve.tensor_scalar(f_of[:, 2, :], f_of[:, 1, :], float(P), None, ALU.mult))
    step(dve.scalar_tensor_tensor(f_of[:, 3, :], e_of[:, 0, :], float(REGION), f_of[:, 2, :], ALU.mult, ALU.add))
    step(dve.tensor_scalar(f_of[:, 3, :], f_of[:, 3, :], float(NE * REGION), None, ALU.min))
    step(dve.tensor_copy(tile_row[:, :], f_of[:, 3, :]))
    step(dve.tensor_scalar(e_of[:, 1, :], e_of[:, 0, :], float(NE - 1), None, ALU.min))
    step(dve.tensor_copy(tile_expert[:, :], e_of[:, 1, :]))
    pool.wait_ge(s_d, pad_ready)
    for e in range(NE):
        pool.indirect_dma_start(sorted_rows[:, :], bass.IndirectOffsetOnAxis(pad_i[:, e:e + 1], 0), pad_row[:, :], None,
                                bounds_check=NE * REGION - 1, oob_is_err=False).then_inc(s_pad, 16)
    for e in (nc.tensor, nc.scalar, nc.vector, nc.gpsimd, nc.sync):
        e.wait_ge(s_d, made[0])
        e.wait_ge(s_pad, 16 * NE)
    v["tile_row"], v["tile_expert"] = tile_row, tile_expert
    TILE_LIST.update(row=tile_row, expert=tile_expert)


TILE_LIST = {}


def loop2(nc, ctx, sb, sem, v, plan, plans):
    banks, sorted_rows, out, ident, w_expert, minus_half = (
        v[n] for n in ("banks", "sorted_rows", "out", "ident", "w_expert", "minus_half"))
    tile_row, tile_expert = TILE_LIST["row"], TILE_LIST["expert"]
    pe, act, dve, pool, sp = nc.tensor, nc.scalar, nc.vector, nc.gpsimd, nc.sync
    M = Marks(nc, ctx, "l2", plan)
    mark, wait = M.mark, M.wait
    U = UNROLL
    xs = [sb(f"xs{u}", [P, ROW]) for u in range(U)]
    xs_t = [sb(f"xs_t{u}", [P, KH, P]) for u in range(U)]
    ys = [sb(f"ys{u}", [P, H]) for u in range(U)]
    os_ = [sb(f"os{u}", [P, H]) for u in range(U)]
    st = [sb(f"st{u}", [P, 6]) for u in range(U)]
    mvs = [sb(f"mvs{u}", [P, 2]) for u in range(U)]
    rs = [sb(f"rs{u}", [P, 3]) for u in range(U)]
    tok = [sb(f"tok{u}", [P, 1], I32) for u in range(U)]
    s_row = [sem(f"s_row{u}") for u in range(U)]
    s_out = [sem(f"s_out{u}") for u in range(U)]

    for e, sm in M.sem.items():
        M.engines[e].sem_inc(sm, M.per_lap[e])
    for u in range(U):
        pool.dma_start(os_[u][:, :], sorted_rows[NE * REGION:NE * REGION + P, 0:H]).then_inc(s_out[u], 16)
    pe.wait_ge(v["s_expert"], 16 * KH)
    with nc.Fori(0, NT // U) as it:
        M.begin(it + 1)
        for u in range(U):
            n = lambda name, u_=u: f"{name}.{u_}"
            wait("sp", n("ys"), n("tok"))
            M.apart("sp")
            r0 = sp.value_load(tile_row[0:1, bass.ds(it * U + u, 1)], min_val=0, max_val=NE * REGION)
            sp.dma_start(xs[u][:, :], sorted_rows[bass.ds(r0, P), :]).then_inc(s_row[u], 16)

        def front(u):
            n = lambda name: f"{name}.{u}"
            bt = banks[u]
            pe.wait_ge(s_row[u], it * 16 + 16)
            wait("pe", n("xt"))
            for k in range(KH):
                ins = pe.transpose(bt[:, k * P:(k + 1) * P], xs[u][:, k * P:(k + 1) * P], ident[:, :])
            mark("pe", n("tr"), ins)
            wait("act", n("tr"), n("mm"))
            mark("act", n("xt"), act.activation(xs_t[u][:, :, :].rearrange("p k t -> p (k t)"), bt[:, 0:H], ACT.Copy))

        def middle(u):
            n = lambda name: f"{name}.{u}"
            bank = banks[4 + u]
            e = pe.value_load(tile_expert[0:1, bass.ds(it * U + u, 1)], min_val=0, max_val=NE - 1)
            wait("pe", n("xt"), n("ys"))
            for k in range(KH):
                ins = pe.matmul(bank[:, 0:H], xs_t[u][:, k, :], w_expert[:, k, bass.ds(e, 1), :], start=k == 0, stop=k == KH - 1)
            mark("pe", n("mm"), ins)
            dve.wait_ge(s_row[u], it * 16 + 16)
            wait("dve", n("mm"), n("os"))
            mark("dve", n("ys"), dve.scalar_tensor_tensor(ys[u][:, :], xs[u][:, 0:H], 2.0, bank[:, 0:H], ALU.mult, ALU.add))
            dve.wait_ge(s_out[u], it * 16 + 16)
            mark("dve", n("tok"), dve.tensor_copy(tok[u][:, :], xs[u][:, H:H + 1]))
            wait("dve", n("ys"))
            mark("dve", n("st"), dve.bn_stats(st[u][:, :], ys[u][:, :]))
            wait("dve", n("st"), n("os"))
            M.apart("dve")
            mark("dve", n("mv"), dve.bn_aggr(mvs[u][:, :], st[u][:, :]))
            wait("dve", n("mv"), n("rs"))
            mark("dve", n("var"), dve.tensor_scalar(rs[u][:, 0:1], mvs[u][:, 1:2], EPS_LN, None, ALU.add))
            wait("pool", n("var"), n("os"))
            mark("pool", n("rs"), pool.tensor_tensor(rs[u][:, 1:2], rs[u][:, 0:1], minus_half[:, 0:1], ALU.pow))

        def back(u):
            n = lambda name: f"{name}.{u}"
            dve.wait_ge(s_out[u], it * 16 + 16)
            wait("dve", n("rs"))
            mark("dve", n("os"), dve.tensor_scalar(os_[u][:, :], ys[u][:, :], mvs[u][:, 0:1], rs[u][:, 1:2], ALU.subtract, ALU.mult))
            wait("pool", n("os"), n("tok"))
            M.apart("pool")
            pool.indirect_dma_start(out[:, :], bass.IndirectOffsetOnAxis(tok[u][:, :], 0), os_[u][:, :], None,
                                    bounds_check=TOK - 1, oob_is_err=False).then_inc(s_out[u], 16)

        for u in range(U + 2):
            if u < U:
                front(u)
            if 0 <= u - 1 < U:
                middle(u - 1)
            if 0 <= u - 2 < U:
                back(u - 2)
    plans["loop2"] = dict(count=M.count, at=M.at, slots={})
    for s in s_out:
        sp.wait_ge(s, 16 * (NT // U) + 16)


INPUTS = dict(hidden=[B, S, H], w_kv=[H, P], w_q=[H, P], w_ae=[H, P], w_gt=[H, H + D], bias_gt=[P, H + D],
              norm_g=[P, H], w_o=[D, H], conv_w=[P, 2, 4], conv_b=[P, 2], bias_ae=[P, 1], w_route=[H, NE],
              state0=[D, NB, 3, D], w2_0=[D, NB, D], w_expert=[NE, H, H])


def program(nc, plan):
    dram = {n: nc.dram_tensor(f"in_{n}", s, F32, kind="ExternalInput").ap() for n, s in INPUTS.items()}
    dram["out"] = nc.dram_tensor("out_0", [TOK, H], F32, kind="ExternalOutput").ap()
    return build(nc, dram, plan)


def kernel(**inputs):
    import numpy as np
    import concourse.bacc as bacc
    from concourse.bass_utils import run_bass_kernel_spmd

    a = {k.split("_", 2)[2]: np.asarray(w) for k, w in inputs.items()}
    rows = lambda w: np.broadcast_to(w[None, :], (P, w.shape[0]))
    arrays = dict(
        hidden=a["hidden"],
        w_kv=np.concatenate([a["Wk"], a["Wv"]]).T,
        w_q=np.concatenate([a["Wq"], a["Wq"]]).T,
        w_ae=np.concatenate([a["aW"], a["eW"]]).T,
        w_gt=np.concatenate([a["gW"], a["tW"]]).T,
        bias_gt=rows(np.concatenate([a["gb"], a["tb"]])),
        norm_g=rows(a["norm_g"]),
        w_o=a["Wo"].T,
        conv_w=np.stack([np.concatenate([a["ckw"], a["cvw"]]), np.concatenate([a["cqw"], a["cqw"]])], 1),
        conv_b=np.stack([np.concatenate([a["ckb"], a["cvb"]]), np.concatenate([a["cqb"], a["cqb"]])], 1),
        bias_ae=np.concatenate([a["ab"], a["eb"]])[:, None],
        w_route=a["gate_w"].T,
        state0=np.broadcast_to(np.stack([a["mW1"].T, a["mW1"].T, a["mW2"].T], 1)[:, None], (D, NB, 3, D)),
        w2_0=np.broadcast_to(a["mW2"][:, None], (D, NB, D)),
        w_expert=a["expert_w"].transpose(0, 2, 1),
    )
    plan = program(bacc.Bacc("TRN2", target_bir_lowering=False, num_devices=1), None)
    nc = bacc.Bacc("TRN2", target_bir_lowering=False, num_devices=1)
    program(nc, plan)
    feed = {f"in_{n}": np.ascontiguousarray(w) for n, w in arrays.items()}
    r = run_bass_kernel_spmd(nc, [feed], core_ids=[0])
    return r.results[0]["out_0"].reshape(B, S, H)
```

```python
import concourse.bass as bass
from concourse import mybir
from contextlib import ExitStack

F32 = mybir.dt.float32
BF16 = mybir.dt.bfloat16
I32 = mybir.dt.int32
ALU = mybir.AluOpType
ACT = mybir.ActivationFunctionType
AX = mybir.AxisListType

P = 128
B = 16
S = 512
H = 256
KH = H // P
D = 64
NC = S // P
G = 4
NB = B // G
TOK = B * S
NE = 8
REGION = TOK + P
NT = TOK // P + NE
ROW = H + 4
PAIRS = 6
LAPS = NT // (2 * PAIRS)
WORDS = 2 * (LAPS + 1)
MIDDLE_LAG = 1
PAIR_BANKS = 3
LAST_TILE = NE * REGION // P
TILE_CODES = 1024
NO_TOKEN = 2.0 * TOK
EPS_RMS = 1e-6
EPS_LN = 1e-5
GRAD_SCALE = 0.1
SCALE_A, SHIFT_A = -0.5 * 0.1 / D, 1 - 0.5 * 0.1
SCALE_E, SHIFT_E = 0.5 * 0.9 / D, 0.5 * 0.9 + 0.05
LR = 0.1


def spread(ap, axis, n):
    shape = list(ap.shape)
    shape[axis] = n
    return ap.broadcast_to(shape)


class Marks:

    def __init__(self, nc, ctx, prefix, plan):
        self.engines = dict(pe=nc.tensor, act=nc.scalar, dve=nc.vector, pool=nc.gpsimd, sp=nc.sync)
        self.sem = {e: ctx.enter_context(nc.semaphore(f"{prefix}_{e}")) for e in ("pe", "act", "dve", "pool")}
        self.passed = ctx.enter_context(nc.semaphore(f"{prefix}_passed"))
        self.plan = plan
        self.per_lap = plan["count"] if plan else {e: 1 for e in self.sem}

    def begin(self, lap, first=False):
        self.lap, self.first = lap, first
        self.count = {e: 0 for e in self.sem}
        self.at = {}

    def mark(self, e, name, instruction):
        instruction.then_inc(self.sem[e], 1)
        self.count[e] += 1
        assert name not in self.at, name
        self.at[name] = (e, self.count[e])

    def wait(self, e, *names):
        need = {}
        for name in names:
            if name is None:
                continue
            if name in self.at:
                who, n = self.at[name]
            elif self.first:
                continue
            elif self.plan:
                who, n = self.plan["at"][name]
                n -= self.per_lap[who]
            else:
                who, n = "pe", 1
            need[who] = max(need.get(who, n), n)
        for who, n in need.items():
            self.engines[e].wait_ge(self.sem[who], self.lap * self.per_lap[who] + n)

    def apart(self, e):
        self.engines[e].sem_inc(self.passed, 1)

    def fill(self):
        for e, s in self.sem.items():
            missing = self.per_lap[e] - self.count[e]
            if self.plan and missing:
                self.engines[e].wait_ge(s, self.count[e])
                self.engines[e].sem_inc(s, missing)
        if self.plan:
            assert all(self.plan["at"][name][1] >= n for name, (_, n) in self.at.items())


class Slots:

    def __init__(self, name, banks, plan):
        self.name, self.banks = name, banks
        self.place = plan["slots"][name][1] if plan else {}
        self.end = plan["slots"][name][0] if plan else None
        self.last = {}
        self.held = set()

    def begin(self):
        if self.end:
            self.last = dict(self.end)
        else:
            self.place = {}

    def take(self, use):
        i = self.place.setdefault(use, len(self.place) % len(self.banks))
        assert i not in self.held, use
        self.held.add(i)
        return i, self.banks[i], self.last.get(i)

    def freed_by(self, i, name):
        self.held.remove(i)
        self.last[i] = name


def build(nc, dram, plan):
    plans = {}
    out = dram["out"]
    with ExitStack() as ctx:
        def sb(name, shape, dt=F32):
            return ctx.enter_context(nc.sbuf_tensor(name, shape, dt))

        def sem(name):
            return ctx.enter_context(nc.semaphore(name))

        sorted_rows = nc.dram_tensor("sorted_rows", [NE * REGION + P, ROW], F32).ap()

        w_kv = sb("w_kv", [P, KH, P])
        w_q = sb("w_q", [P, KH, P])
        w_ae = sb("w_ae", [P, KH, P])
        NG = H + D
        w_gt = sb("w_gt", [P, KH, NG])
        bias_gt = sb("bias_gt", [P, NG])
        norm_g = sb("norm_g", [P, H])
        w_o = sb("w_o", [D, H])
        conv_w = sb("conv_w", [P, 2, 4])
        conv_b = sb("conv_b", [P, 2])
        bias_ae = sb("bias_ae", [P, 1])
        w_route = sb("w_route", [P, KH, NE])
        ident = sb("ident", [P, P])
        ident_nb = sb("ident_nb", [P, NB, P])
        ident_g = sb("ident_g", [P, 2, D])
        ones_ae = sb("ones_ae", [P, P])
        sum_scale = sb("sum_scale", [P, 1])
        sum_shift = sb("sum_shift", [P, 1])
        ones_bf = sb("ones_bf", [P, P], BF16)
        before = sb("before", [P, P], BF16)
        rank = sb("rank", [P, NE])
        region0 = sb("region0", [P, NE])
        token = sb("token", [P, G * NB])
        minus_half = sb("minus_half", [P, 8])
        eps_ln = sb("eps_ln", [P, 1])
        tile_no = sb("tile_no", [P, NT])
        lane = sb("lane", [P, 1])
        pad_row = sb("pad_row", [P, ROW])

        state = [sb(f"state{g}", [P, NB, 3, D]) for g in range(G)]
        w2 = [sb(f"w2_{g}", [D, NB, D]) for g in range(G)]
        n_raw = 2 * NB * (P + 3)
        shared = sb("shared", [P, G * n_raw])
        raw = [shared[:, g * n_raw:(g + 1) * n_raw].rearrange("p (j b t) -> p j b t", j=2, b=NB) for g in range(G)]
        w_expert = shared[:, 0:KH * NE * H].rearrange("p (k e f) -> p k e f", k=KH, e=NE)
        routed = sb("routed", [P, NE], BF16)

        banks = [ctx.enter_context(nc.psum_tensor(f"bank{i}", [P, 512], F32)) for i in range(8)]

        s_proj, s_load, s_expert = sem("s_proj"), sem("s_load"), sem("s_expert")
        halves = lambda name: dram[name].rearrange("(k p) m -> p k m", p=P)
        loads = [
            (s_proj, w_kv[:, :, :], halves("w_kv")),
            (s_proj, w_q[:, :, :], halves("w_q")),
            (s_proj, w_ae[:, :, :], halves("w_ae")),
            (s_proj, bias_ae[:, :], dram["bias_ae"]),
            (s_proj, conv_w[:, :, :], dram["conv_w"]),
            (s_proj, conv_b[:, :], dram["conv_b"]),
            (s_load, norm_g[:, :], dram["norm_g"]),
            (s_load, w_gt[:, :, :], halves("w_gt")),
            (s_load, bias_gt[:, :], dram["bias_gt"]),
        ]
        for g in range(G):
            loads += [(s_load, state[g][0:D, :, :, :], dram["state0"]), (s_load, w2[g][:, :, :], dram["w2_0"])]
        loads += [(s_load, w_o[:, :], dram["w_o"]), (s_load, w_route[:, :, :], halves("w_route"))]
        for j, (s, dst, src) in enumerate(loads):
            (nc.sync if s is s_proj and j % 2 else nc.scalar).dma_start(dst, src).then_inc(s, 16)
        n_proj = sum(s is s_proj for s, _, _ in loads)
        n_load = len(loads) - n_proj

        s_fill, s_const = sem("s_fill"), sem("s_const")
        pool = nc.gpsimd
        fills = [(ident[:, :], 0.0), (ident_nb[:, :, :], 0.0), (ident_g[:, :, :], 0.0),
                 (ones_ae[0:D, 0:D], 1.0), (ones_ae[0:D, D:P], 0.0), (ones_ae[D:P, 0:D], 0.0), (ones_ae[D:P, D:P], 1.0),
                 (sum_scale[0:D, :], SCALE_A), (sum_scale[D:P, :], SCALE_E),
                 (sum_shift[0:D, :], SHIFT_A), (sum_shift[D:P, :], SHIFT_E),
                 (ones_bf[:, :], 1.0), (minus_half[:, :], -0.5), (eps_ln[:, :], EPS_LN),
                 (pad_row[:, 0:H], 0.0), (pad_row[:, H:H + 1], NO_TOKEN), (pad_row[:, H + 1:ROW], 0.0),
                 (routed[:, :], 0.0)]
        for g in range(G):
            fills += [(state[g][D:P, :, :, :], 0.0), (raw[g][:, :, :, P:P + 3], 0.0)]
        t_first = sb("t_first", [P, NB, P])
        fills.append((t_first[:, :, :], 0.0))
        for dst, value in fills:
            nc.vector.memset(dst, value).then_inc(s_fill, 1)
        n_const = 0
        pool.wait_ge(s_fill, len(fills))

        def pool_const(instruction):
            nonlocal n_const
            n_const += 1
            instruction.then_inc(s_const, 1)

        def diagonal(dst, base, pattern):
            return pool.affine_select(out=dst, in_=dst, compare_op=ALU.not_equal, fill=1.0, base=base,
                                      pattern=pattern, channel_multiplier=1)

        pool_const(diagonal(ident[:, :], 0, [[-1, P]]))
        pool_const(diagonal(ident_nb[:, :, :], 0, [[0, NB], [-1, P]]))
        pool_const(diagonal(ident_g[:, 0, :], 0, [[-1, D]]))
        pool.wait_ge(s_const, n_const)
        pool_const(diagonal(ident_g[:, :, :], -D, [[0, 2], [-1, D]]))
        pool_const(pool.affine_select(out=before[:, :], in_=ones_bf[:, :], compare_op=ALU.is_gt, fill=0.0,
                                      base=0, pattern=[[1, P]], channel_multiplier=-1))
        for dst, pattern, base, lanes in ((rank, [[-1, NE]], NE, 0), (region0, [[REGION, NE]], 0, 0),
                                          (token, [[S, G * NB]], 0, 1), (tile_no, [[1, NT]], 0, 0),
                                          (lane, [[0, 1]], 0, 1)):
            pool_const(pool.iota(dst[:, :], pattern=pattern, base=base, channel_multiplier=lanes,
                                 allow_small_or_imprecise_dtypes=True))

        s_prep = sem("s_prep")
        nc.vector.wait_ge(s_proj, 16 * n_proj)
        nc.vector.tensor_scalar(bias_ae[:, :], bias_ae[:, :], 0.5, None, ALU.mult).then_inc(s_prep, 1)
        n_bias = 1
        nc.vector.wait_ge(s_load, 16 * n_load)
        for k in range(KH):
            nc.vector.tensor_tensor(w_gt[:, k, 0:H], w_gt[:, k, 0:H], norm_g[:, :], ALU.mult).then_inc(s_prep, 1)
        nc.vector.tensor_tensor(bias_gt[:, 0:H], bias_gt[:, 0:H], norm_g[:, :], ALU.mult).then_inc(s_prep, 1)
        n_prep = n_bias + KH + 1

        def all_ready(e):
            e.wait_ge(s_load, 16 * n_load)
            e.wait_ge(s_fill, len(fills))
            e.wait_ge(s_const, n_const)
            e.wait_ge(s_prep, n_prep)

        for e in (nc.tensor, nc.scalar, nc.gpsimd):
            e.wait_ge(s_proj, 16 * n_proj)
        nc.scalar.wait_ge(s_prep, n_bias)
        all_ready(nc.vector)
        all_ready(nc.gpsimd)

        tile_buffers_ = tile_buffers(sb)
        s_out = [sem(f"s_out{p}") for p in range(PAIRS)]
        with ExitStack() as inner:
            sb1 = lambda name, shape, dt=F32: inner.enter_context(nc.sbuf_tensor(name, shape, dt))
            loop1(nc, ctx, sb1, sem, dict(locals()), plan and plan["loop1"], plans)
        pair_rows, lap_experts = tiles(nc, ctx, sb, sem, dict(locals()))
        loop2(nc, ctx, sb, sem, dict(locals()), plan and plan["loop2"], plans)
    return plans


def loop1(nc, ctx, sb, sem, v, plan, plans):
    dram, banks = v["dram"], v["banks"]
    w_kv, w_q, w_ae, w_gt, bias_gt, w_o = (v[n] for n in ("w_kv", "w_q", "w_ae", "w_gt", "bias_gt", "w_o"))
    conv_w, conv_b, bias_ae, w_route = (v[n] for n in ("conv_w", "conv_b", "bias_ae", "w_route"))
    ident, ident_nb, ident_g, ones_ae, sum_scale, sum_shift = (
        v[n] for n in ("ident", "ident_nb", "ident_g", "ones_ae", "sum_scale", "sum_shift"))
    ones_bf, before, rank, region0, token = (v[n] for n in ("ones_bf", "before", "rank", "region0", "token"))
    minus_half, state, w2, raw, routed = (v[n] for n in ("minus_half", "state", "w2", "raw", "routed"))
    t_first, sorted_rows, all_ready = v["t_first"], v["sorted_rows"], v["all_ready"]
    NG = H + D

    pe, act, dve, pool, sp = nc.tensor, nc.scalar, nc.vector, nc.gpsimd, nc.sync
    M = Marks(nc, ctx, "l1", plan)
    mark, wait = M.mark, M.wait

    def two(name, shape, dt=F32):
        return [sb(f"{name}{i}", shape, dt) for i in range(2)]

    x = two("x", [P, NB, H])
    s_x = [sem(f"s_x{i}") for i in range(2)]
    gt = [sb(f"gt{g}", [P, NB, NG]) for g in range(G)]
    x_t = two("x_t", [P, KH, NB * P])
    s_xt = [sem(f"s_xt{i}") for i in range(2)]
    kv = two("kv", [P, NB, P])
    q = two("q", [P, NB, P])
    tanh_ae = sb("tanh_ae", [P, NB * P])
    decay = two("decay", [P, 3, NB, P])
    soft = sb("soft", [P, 3, NB, D])
    theta = two("theta", [P, NB])
    resp_c = two("resp_c", [P, NB, P])
    resp_e = sb("resp_e", [P, NB, P])
    ends = two("ends", [P, NB, 2])
    carry = two("carry", [P, NB, P])
    carry_f = sb("carry_f", [P, NB, P])
    kv_n = two("kv_n", [P, 2, NB, D])
    kq = two("kq", [P, NB, P])
    ab_q = two("ab_q", [P, NB, P])
    g_dec = two("g_dec", [P, NB, 2, D])
    ck = two("ck", [P, NB, 2, D])
    sq_k = sb("sq_k", [P, NB, D])
    norms = two("norms", [P, 4, NB])
    t_z = sb("t_z", [P, NB, D])
    sig = sb("sig", [P, NB, D])
    h = sb("h", [P, NB, D])
    h_t = two("h_t", [D, NB, P])
    grad = sb("grad", [P, 2, NB, D])
    dz_w = two("dz_w", [P, NB, 2, D])
    e_w = two("e_w", [P, NB, D])
    e_t = sb("e_t", [D, NB, P])
    ds = sb("ds", [P, 2, NB, D])
    sq = sb("sq", [P, 3, NB, D])
    ch = two("ch", [P, NB, 2, D])
    small = sb("small", [P, 8, NB])
    t_q = sb("t_q", [P, NB, P])
    hq = sb("hq", [P, NB, P])
    hh = sb("hh", [P, NB, P])
    ab_h = sb("ab_h", [P, NB, P])
    ret = two("ret", [D, NB, P])
    junk = sb("junk", [P, H])
    ssq = sb("ssq", [P, NB])
    rms = sb("rms", [P, 2, NB])
    y = sb("y", [P, NB, H])
    stats = sb("stats", [P, NB, 6])
    mv = sb("mv", [P, NB, 2])
    rstd = sb("rstd", [P, 3, NB])
    rows = two("rows", [P, NB, ROW])
    rows_t = sb("rows_t", [P, KH, NB * P])
    best = sb("best", [P, 2, NB])
    pick = sb("pick", [P, 3, NB, NE])
    onehot = sb("onehot", [P, NB, NE], BF16)
    total = sb("total", [P, NE])
    where = sb("where", [P, 2, NB, NE])
    where_f = sb("where_f", [P, NB])
    index = two("index", [P, NB], I32)
    s_scatter = [sem(f"s_scatter{i}") for i in range(2)]

    pro = Slots("pro", banks[0:3], plan)
    lrn = Slots("lrn", banks[3:4], plan)
    rtv = Slots("rtv", banks[4:5], plan)
    new = Slots("new", banks[5:6], plan)
    epi = Slots("epi", banks[6:8], plan)
    rings = (pro, lrn, rtv, new, epi)

    def grab(slots, use):
        i, bank, last = slots.take(use)
        wait("pe", last)
        return i, bank

    flat = lambda a: a.rearrange("p b t -> p (b t)")

    def names(g):
        return tuple((lambda name, g_=(g - k) % G: f"{name}.{g_}") for k in range(3))

    def project(c, g):
        n, o, o2 = names(g)
        i2 = g % 2
        KV, Q, xt = kv[i2], q[i2], x_t[i2]
        wait("sp", o2(f"gt_ps{NB - 1}"), o2("ae_ps"))
        sp.dma_start(xt[:, :, :], dram["hidden_t"][c, g]).then_inc(s_xt[i2], 16)
        yield
        wait("dve", n("conv_kv"), n("conv_q"))
        mark("dve", n("halo"), dve.tensor_copy(raw[g][:, :, :, 0:3], raw[g][:, :, :, P:P + 3]))
        pe.wait_ge(s_xt[i2], c * 32 + (g // 2) * 16 + 16)
        for j, (name, w) in enumerate((("kv", w_kv), ("q", w_q))):
            i, bank = grab(pro, n(name))
            for k in range(KH):
                ins = pe.matmul(bank[:, :], w[:, k, :], xt[:, k, :], start=k == 0, stop=k == KH - 1)
            mark("pe", n(f"{name}_ps"), ins)
            wait("act", n(f"{name}_ps"), n("halo"))
            mark("act", n(f"{name}_raw"),
                 act.activation(raw[g][:, j, :, 3:P + 3], bank[:, :].rearrange("p (b t) -> p b t", b=NB), ACT.Copy))
            pro.freed_by(i, n(f"{name}_raw"))
            yield
        i, bank = grab(pro, n("ae"))
        for k in range(KH):
            ins = pe.matmul(bank[:, :], w_ae[:, k, :], xt[:, k, :], start=k == 0, stop=k == KH - 1)
        mark("pe", n("ae_ps"), ins)
        wait("act", n("ae_ps"), o("sum"))
        mark("act", n("tanh_ae"), act.activation(tanh_ae[:, :], bank[:, :], ACT.Tanh, bias=bias_ae[:, 0:1], scale=0.5))
        pro.freed_by(i, n("tanh_ae"))
        yield
        for j, (name, dst) in enumerate((("kv", KV), ("q", Q))):
            last = (o2("kq_ps"), o2("kv_n_ps"), o2("z_ps")) if name == "kv" else (o2("kq_ps"), o2("ab_q"))
            wait("act", n(f"{name}_raw"), n("halo"), *last)
            mark("act", n(f"conv_{name}0"),
                 act.activation(dst[:, :, :], raw[g][:, j, :, 0:P], ACT.Identity, bias=conv_b[:, j:j + 1], scale=conv_w[:, j, 0:1]))
            for tap in range(1, 4):
                wait("dve", n(f"conv_{name}{tap - 1}"))
                mark("dve", n(f"conv_{name}{tap}" if tap < 3 else f"conv_{name}"),
                     dve.scalar_tensor_tensor(dst[:, :, :], raw[g][:, j, :, tap:tap + P], conv_w[:, j, tap:tap + 1],
                                              dst[:, :, :], ALU.mult, ALU.add))
            yield
        if M.first and g == 0:
            all_ready(pe)
        wait("pe", n("tanh_ae"))
        gate_scale, gate_shift = sum_scale[:, 0:1], sum_shift[:, 0:1]
        i, bank = grab(pro, n("sum"))
        mark("pe", n("sum"), pe.matmul(bank[:, :], ones_ae[:, :], tanh_ae[:, :], start=True, stop=True))
        wait("act", n("sum"), o2("scan_b"))
        v4 = bank[:, :].rearrange("p (b t) -> p b t", b=NB)
        mark("act", n("dec_ae"), act.activation(decay[i2][:, 2, :, :], v4, ACT.Identity, bias=gate_shift, scale=gate_scale))
        for name, w, rows_, scale, shift in (("a", 0, slice(0, D), SCALE_A, SHIFT_A), ("e", 1, slice(D, P), SCALE_E, SHIFT_E)):
            act.activation(decay[i2][0:D, w, :, :], v4[rows_], ACT.Copy, bias=shift, scale=scale)
            mark("act", n(f"dec_{name}"), act.activation(decay[i2][D:P, w, :, :], v4[rows_], ACT.Copy, bias=shift, scale=scale))
        pro.freed_by(i, n("dec_e"))
        yield
        if M.first and g == 0:
            all_ready(act)
        for b in range(NB):
            i, bank = grab(pro, n(f"gt{b}"))
            for k in range(KH):
                ins = pe.matmul(bank[:, 0:NG], xt[:, k, b * P:(b + 1) * P], w_gt[:, k, :], start=k == 0, stop=k == KH - 1)
            mark("pe", n(f"gt_ps{b}"), ins)
            wait("dve", n(f"gt_ps{b}"), n(f"gated{b}"), n("soft"))
            mark("dve", n(f"gt{b}"), dve.tensor_tensor(gt[g][:, b, :], bank[:, 0:NG], bias_gt[:, :], ALU.add))
            pro.freed_by(i, n(f"gt{b}"))
            yield
        u = gt[g][:, :, H:NG]
        wait("act", n(f"gt{NB - 1}"), o("theta0"))
        mark("act", n("abs_u"), act.activation(soft[:, 0, :, :], u, ACT.Abs))
        wait("act", n("abs_u"))
        mark("act", n("exp_u"), act.activation(soft[:, 1, :, :], soft[:, 0, :, :], ACT.Exp, scale=-1.0))
        wait("act", n("exp_u"))
        mark("act", n("ln_u"), act.activation(soft[:, 2, :, :], soft[:, 1, :, :], ACT.Ln, bias=1.0))
        yield
        wait("dve", n("ln_u"))
        mark("dve", n("soft"), dve.scalar_tensor_tensor(soft[:, 0, :, :], u, 0.0, soft[:, 2, :, :], ALU.max, ALU.add))
        wait("dve", n("soft"), o2("weight"))
        mark("dve", n("theta0"), dve.tensor_reduce(theta[i2][:, :], soft[:, 0, :, :], AX.X, ALU.add))
        wait("dve", n("theta0"))
        mark("dve", n("theta"), dve.tensor_scalar(theta[i2][:, :], theta[i2][:, :], -GRAD_SCALE * LR / D, None, ALU.mult))
        yield

    def respond(c, g):
        n, o, o2 = names(g)
        i2 = g % 2
        KV, Q = kv[i2], q[i2]
        i, bank = grab(pro, n("kv_n"))
        wait("pe", n("conv_kv"))
        for b in range(NB):
            ins = pe.transpose(bank[:, b * P:(b + 1) * P], KV[:, b, :], ident[:, :])
        mark("pe", n("kv_n_ps"), ins)
        vb = bank[:, :].rearrange("p (b two d) -> p two b d", b=NB, two=2)
        wait("act", n("kv_n_ps"), o2("ck"), o2("e2"), o2("sq_k"))
        act.activation(kv_n[i2][:, 0], vb[:, 0], ACT.Copy)
        mark("act", n("kv_n"), act.activation(kv_n[i2][:, 1], vb[:, 1], ACT.Copy, scale=2.0))
        pro.freed_by(i, n("kv_n"))
        wait("dve", n("dec_a"), n("dec_e"), o("scan_f"))
        mark("dve", n("first"), dve.tensor_copy(t_first[:, :, 0:1], decay[i2][:, 2, :, 0:1]))
        wait("dve", n("first"))
        mark("dve", n("clear"), dve.memset(decay[i2][:, :, :, 0:1], 0.0))
        C, E_, AB, AF = (flat(a[:, :, :]) for a in (resp_c[i2], resp_e, carry[i2], carry_f))
        dec_a, dec_e, dec_ae = (flat(decay[i2][:, j]) for j in range(3))
        wait("pool", n("kv_n"), o("norm_k"))
        mark("pool", n("sq_k"), pool.tensor_tensor(sq_k[:, :, :], kv_n[i2][:, 0], kv_n[i2][:, 0], ALU.mult))
        yield
        wait("dve", n("clear"), o("end_e"))
        mark("dve", n("scan_e"), dve.tensor_tensor_scan(E_, dec_e, flat(ident_nb[:, :, :]), 0.0, ALU.mult, ALU.add))
        wait("dve", n("first"), o("g_dec_s"), o("copy_a"))
        mark("dve", n("scan_f"), dve.tensor_tensor_scan(AF, dec_ae, flat(t_first[:, :, :]), 0.0, ALU.mult, ALU.add))
        wait("act", n("scan_f"), o2("ab_h"), o2("g_dec"))
        mark("act", n("copy_a"), act.activation(AB[0:D], AF[0:D], ACT.Copy))
        yield
        wait("dve", n("scan_e"), o2("p2"))
        mark("dve", n("scan_c"), dve.tensor_tensor_scan(C, dec_a, E_, 0.0, ALU.mult, ALU.add))
        wait("dve", n("scan_f"), o2("ab_h"))
        mark("dve", n("scan_b"), dve.tensor_tensor_scan(AB[D:P], dec_a[D:P], AF[D:P], 0.0, ALU.mult, ALU.add))
        wait("dve", n("scan_c"), o2("ck"), o2("ch"))
        mark("dve", n("end_e"), dve.tensor_copy(ends[i2][:, :, 1:2], resp_e[:, :, P - 1:P]))
        mark("dve", n("ends"), dve.tensor_copy(ends[i2][:, :, 0:1], resp_c[i2][:, :, P - 1:P]))
        yield
        i, bank = grab(pro, n("kq"))
        wait("pe", n("conv_q"))
        for b in range(NB):
            ins = pe.matmul(bank[:, b * P:(b + 1) * P], KV[0:D, b, :], Q[0:D, b, :], start=True, stop=True)
        mark("pe", n("kq_ps"), ins)
        wait("dve", n("kq_ps"), n("scan_c"), o2("zq_ps"))
        mark("dve", n("kq"), dve.tensor_tensor(flat(kq[i2][:, :, :]), bank[:, :], C, ALU.mult))
        pro.freed_by(i, n("kq"))
        wait("pool", n("conv_q"), n("copy_a"), n("scan_b"), o2("zq_ps"))
        mark("pool", n("ab_q"), pool.tensor_tensor(ab_q[i2][:, :, :], q[i2][:, :, :], carry[i2][:, :, :], ALU.mult))
        wait("dve", n("sq_k"), o2("norm_p"))
        mark("dve", n("norm_k"), dve.tensor_reduce(norms[i2][:, 0, :], sq_k[:, :, :], AX.X, ALU.add))
        yield
        wait("dve", n("scan_b"), n("copy_a"), o2("upd_ps"))
        for w, (name, src) in enumerate((("g_dec", carry[i2]), ("g_dec_s", carry_f))):
            mark("dve", n(name), dve.tensor_tensor(g_dec[i2][:, :, w, :], spread(ident_g[:, w:w + 1, :], 1, NB),
                                                   spread(src[:, :, P - 1:P], 2, D), ALU.mult))
        wait("pool", n("kv_n"), n("ends"), o2("upd_ps"))
        mark("pool", n("ck"), pool.tensor_tensor(ck[i2][:, :, :, :], spread(kv_n[i2][:, 0].unsqueeze(2), 2, 2), at_end(i2), ALU.mult))
        yield

    def at_end(i2):
        return spread(ends[i2][:, :, :].unsqueeze(3), 3, D)

    def learn(c, g):
        n, o, o2 = names(g)
        i2 = g % 2
        KV = kv[i2]
        ST, W2 = state[g], w2[g]
        i, zb = grab(lrn, n("z"))
        z = zb[:, 0:NB * D].rearrange("p (b d) -> p b d", b=NB)
        wait("pe", n("conv_kv"), n("state"))
        for b in range(NB):
            ins = pe.matmul(z[:, b, :], KV[0:D, b, :], ST[0:D, b, 0, :], start=True, stop=True)
        mark("pe", n("z_ps"), ins)
        wait("act", n("z_ps"), o("sig"))
        mark("act", n("t_z"), act.activation(t_z[:, :, :], z, ACT.Tanh, scale=0.5))
        wait("dve", n("t_z"), o("d_silu"))
        mark("dve", n("sig"), dve.tensor_scalar(sig[:, :, :], t_z[:, :, :], 0.5, 0.5, ALU.mult, ALU.add))
        wait("dve", n("sig"), o("ch"), o("h_ps"), o("sq_h"))
        mark("dve", n("h"), dve.tensor_tensor(h[:, :, :], z, sig[:, :, :], ALU.mult))
        lrn.freed_by(i, n("h"))
        yield
        i, bank = grab(lrn, n("h_t"))
        wait("pe", n("h"))
        M.apart("pe")
        for b in range(NB):
            ins = pe.transpose(bank[0:D, b * P:(b + 1) * P], h[:, b, :], ident[:, :])
        mark("pe", n("h_ps"), ins)
        wait("act", n("h_ps"), o2("hh_ps"))
        mark("act", n("h_t"), act.activation(flat(h_t[i2][:, :, :]), bank[0:D, :], ACT.Copy))
        lrn.freed_by(i, n("h_t"))
        wait("dve", n("h"), o("dz"))
        mark("dve", n("r"), dve.scalar_tensor_tensor(ds[:, 0], sig[:, :, :], 1.0, h[:, :, :], ALU.subtract, ALU.mult))
        wait("dve", n("r"))
        mark("dve", n("d_silu"), dve.tensor_tensor(ds[:, 1], sig[:, :, :], ds[:, 0], ALU.subtract))
        yield
        i, bank = grab(lrn, n("pred"))
        pred = bank[:, 0:NB * D].rearrange("p (b d) -> p b d", b=NB)
        wait("pe", n("h_t"))
        for b in range(NB):
            ins = pe.matmul(pred[:, b, :], h_t[i2][:, b, :], ST[0:D, b, 2, :], start=True, stop=True)
        mark("pe", n("pred_ps"), ins)
        wait("dve", n("pred_ps"), n("kv_n"), o("grad_w"), o("e_ps"), o("sq_e"))
        mark("dve", n("e2"), dve.scalar_tensor_tensor(grad[:, 1], pred, 2.0, kv_n[i2][:, 1], ALU.mult, ALU.subtract))
        lrn.freed_by(i, n("e2"))
        yield
        i, bank = grab(lrn, n("e_t"))
        wait("pe", n("e2"))
        M.apart("pe")
        for b in range(NB):
            ins = pe.transpose(bank[0:D, b * P:(b + 1) * P], grad[:, 1, b, :], ident[:, :])
        mark("pe", n("e_ps"), ins)
        wait("act", n("e_ps"), o("dh_ps"))
        mark("act", n("e_t"), act.activation(flat(e_t[:, :, :]), bank[0:D, :], ACT.Copy))
        lrn.freed_by(i, n("e_t"))
        wait("act", n("h"), o("norm_h"))
        mark("act", n("sq_h"), act.activation(sq[:, 0], h[:, :, :], ACT.Square))
        wait("act", n("e2"))
        mark("act", n("sq_e"), act.activation(sq[:, 2], grad[:, 1], ACT.Square))
        yield
        i, bank = grab(lrn, n("dh"))
        dh = bank[:, 0:NB * D].rearrange("p (b d) -> p b d", b=NB)
        wait("pe", n("e_t"), n("w2"))
        for b in range(NB):
            ins = pe.matmul(dh[:, b, :], e_t[:, b, :], W2[:, b, :], start=True, stop=True)
        mark("pe", n("dh_ps"), ins)
        wait("dve", n("dh_ps"), n("d_silu"), o("sq_z"))
        mark("dve", n("dz"), dve.tensor_tensor(grad[:, 0], dh, ds[:, 1], ALU.mult))
        lrn.freed_by(i, n("dz"))
        wait("act", n("dz"))
        mark("act", n("sq_z"), act.activation(sq[:, 1], grad[:, 0], ACT.Square))
        yield
        wait("dve", n("sq_z"), n("sq_h"), n("sq_e"), n("norm_k"))
        mark("dve", n("norm_h"), dve.tensor_reduce(norms[i2][:, 1:4, :], sq[:, :, :, :], AX.X, ALU.add))
        wait("dve", n("norm_h"))
        mark("dve", n("norm_p"), dve.tensor_tensor(small[:, 0:2, :], norms[i2][:, 0:2, :], norms[i2][:, 2:4, :], ALU.mult))
        wait("dve", n("norm_p"))
        mark("dve", n("norm_s"), dve.tensor_tensor(small[:, 2, :], small[:, 0, :], small[:, 1, :], ALU.add))
        wait("dve", n("norm_s"))
        mark("dve", n("norm_g"), dve.tensor_scalar(small[:, 3, :], small[:, 2, :], GRAD_SCALE ** 2, 1e-12, ALU.mult, ALU.max))
        wait("pool", n("norm_g"))
        mark("pool", n("inv_g"), pool.tensor_tensor(small[:, 4, :], small[:, 3, :], minus_half[:, 0:NB], ALU.pow))
        wait("pool", n("h"), o2("upd_ps"), n("ends"))
        mark("pool", n("ch"), pool.tensor_tensor(ch[i2][:, :, :, :], spread(h[:, :, :].unsqueeze(2), 2, 2), at_end(i2), ALU.mult))
        yield
        wait("dve", n("inv_g"), n("theta"))
        mark("dve", n("weight"), dve.scalar_tensor_tensor(small[:, 5, :], small[:, 4, :], 1.0, theta[i2][:, :], ALU.min, ALU.mult))
        wait("dve", n("weight"), o2("upd_ps"), o2("out_ps"), o2("zq_ps"))
        wgt = small[:, 5, :].unsqueeze(2)
        mark("dve", n("dz_w"), dve.tensor_tensor(dz_w[i2][:, :, :, :], spread(grad[:, 0].unsqueeze(2), 2, 2),
                                                 spread(spread(wgt, 2, 2).unsqueeze(3), 3, D), ALU.mult))
        mark("dve", n("grad_w"), dve.tensor_tensor(e_w[i2][:, :, :], grad[:, 1], spread(wgt, 2, D), ALU.mult))
        yield

    def retrieve(c, g):
        n, o, o2 = names(g)
        i2 = g % 2
        C = resp_c[i2][:, :, :]
        ST, W2 = state[g], w2[g]
        wait("sp", o2("res"))
        sp.dma_start(x[i2][:, :, :], dram["hidden"][c, g]).then_inc(s_x[i2], 16)
        i, bank = grab(rtv, n("zq"))
        wait("pe", n("grad_w"), n("kq"), n("ab_q"))
        for b in range(NB):
            zq = bank[:, b * P:(b + 1) * P]
            pe.matmul(zq, ST[:, b, 0:2, :].rearrange("p w d -> p (w d)"), ab_q[i2][:, b, :], start=True, stop=False)
            ins = pe.matmul(zq, dz_w[i2][:, b].rearrange("p w d -> p (w d)"), kq[i2][:, b, :], start=False, stop=True)
        mark("pe", n("zq_ps"), ins)
        wait("act", n("zq_ps"), o("hq"))
        mark("act", n("t_q"), act.activation(flat(t_q[:, :, :]), bank[:, :], ACT.Tanh, scale=0.5))
        wait("dve", n("t_q"), o("hh_ps"), o("ab_h"))
        mark("dve", n("hq"), dve.scalar_tensor_tensor(flat(hq[:, :, :]), flat(t_q[:, :, :]), 1.0, bank[:, :], ALU.add, ALU.mult))
        rtv.freed_by(i, n("hq"))
        wait("pool", n("hq"), n("copy_a"), n("scan_b"), o("out_ps"))
        mark("pool", n("ab_h"), pool.tensor_tensor(ab_h[:, :, :], hq[:, :, :], carry[i2][:, :, :], ALU.mult))
        yield
        iu, upd = grab(new, n("upd"))
        wait("pe", n("g_dec_s"), n("ck"), n("ch"))
        for b in range(NB):
            ub = upd[:, b * P:(b + 1) * P]
            pe.matmul(ub, g_dec[i2][:, b].rearrange("p w d -> p (w d)"), ST[:, b, 1:3].rearrange("p w d -> p (w d)"), start=True, stop=False)
            pe.matmul(ub[:, 0:D], ck[i2][:, b].rearrange("p w d -> p (w d)"), dz_w[i2][:, b, 0, :], start=False, stop=False)
            ins = pe.matmul(ub[:, D:P], ch[i2][:, b].rearrange("p w d -> p (w d)"), e_w[i2][:, b, :], start=False, stop=True)
        mark("pe", n("upd_ps"), ins)
        yield
        i, bank = grab(rtv, n("hh"))
        wait("pe", n("hq"))
        for b in range(NB):
            ins = pe.matmul(bank[:, b * P:(b + 1) * P], h_t[i2][:, b, :], hq[0:D, b, :], start=True, stop=True)
        mark("pe", n("hh_ps"), ins)
        wait("dve", n("hh_ps"), o("out_ps"))
        mark("dve", n("p2"), dve.tensor_tensor(flat(hh[:, :, :]), bank[:, :], flat(C), ALU.mult))
        rtv.freed_by(i, n("p2"))
        yield
        i, bank = grab(rtv, n("out"))
        wait("pe", n("p2"), n("ab_h"))
        for b in range(NB):
            ob = bank[0:D, b * P:(b + 1) * P]
            pe.matmul(ob, ST[:, b, 2, :], ab_h[:, b, :], start=True, stop=False)
            ins = pe.matmul(ob, e_w[i2][:, b, :], hh[:, b, :], start=False, stop=True)
        mark("pe", n("out_ps"), ins)
        wait("act", n("out_ps"), o2("wo_ps1"))
        mark("act", n("ret"), act.activation(flat(ret[i2][:, :, :]), bank[0:D, :], ACT.Copy, scale=0.5))
        rtv.freed_by(i, n("ret"))
        wait("act", n("upd_ps"))
        u4 = upd[:, :].rearrange("p (b w d) -> p b w d", b=NB, w=2)
        act.activation(ST[:, :, 0:2, :], spread(u4[:, :, 0:1, :], 2, 2), ACT.Copy)
        mark("act", n("state"), act.activation(ST[:, :, 2, :], u4[:, :, 1, :], ACT.Copy))
        new.freed_by(iu, n("state"))
        yield
        i, bank = grab(rtv, n("w2"))
        wait("pe", n("state"))
        M.apart("pe")
        for b in range(NB):
            ins = pe.transpose(bank[0:D, b * P:(b + 1) * P], ST[:, b, 2, :], ident[:, :])
        mark("pe", n("w2_ps"), ins)
        wait("act", n("w2_ps"), n("dh_ps"))
        mark("act", n("w2"), act.activation(W2[:, :, :], bank[0:D, :].rearrange("p (b d) -> p b d", b=NB)[:, :, 0:D], ACT.Copy))
        rtv.freed_by(i, n("w2"))
        yield

    def epilogue(c, g):
        n, o, o2 = names(g)
        i2 = g % 2
        X, Y, R = x[i2], y, rows[i2]
        held = []
        for j in range(2):
            i, bank = grab(epi, n(f"wo{j}"))
            held.append((i, bank))
            wait("pe", n("ret"))
            for b in (2 * j, 2 * j + 1):
                ins = pe.matmul(bank[:, (b % 2) * H:(b % 2 + 1) * H], ret[i2][:, b, :], w_o[:, :], start=True, stop=True)
            mark("pe", n(f"wo_ps{j}"), ins)
            wait("act", n(f"wo_ps{j}"), o("ms"))
            for b in (2 * j, 2 * j + 1):
                prev = n(f"ssq{b - 1}") if b else o(f"ssq{NB - 1}")
                wait("act", prev)
                mark("act", n(f"ssq{b}"), act.activation(junk[:, :], bank[:, (b % 2) * H:(b % 2 + 1) * H], ACT.Square, accum_out=ssq[:, b:b + 1]))
        yield
        wait("dve", *[n(f"ssq{b}") for b in range(NB)])
        wait("dve", o("rms"))
        mark("dve", n("ms"), dve.tensor_scalar(rms[:, 0, :], ssq[:, :], 1.0 / H, EPS_RMS, ALU.mult, ALU.add))
        wait("pool", n("ms"), o(f"gated{NB - 1}"))
        mark("pool", n("rms"), pool.tensor_tensor(rms[:, 1, :], rms[:, 0, :], minus_half[:, 0:NB], ALU.pow))
        yield
        for b in range(NB):
            i, bank = held[b // 2]
            wait("dve", n("rms"), n(f"gt{b}"), o("norm3"))
            mark("dve", n(f"gated{b}"), dve.scalar_tensor_tensor(Y[:, b, :], bank[:, (b % 2) * H:(b % 2 + 1) * H], rms[:, 1, b:b + 1],
                                                                 gt[g][:, b, 0:H], ALU.mult, ALU.mult))
            if b % 2:
                epi.freed_by(i, n(f"gated{b}"))
        yield
        pool.wait_ge(s_x[i2], c * 32 + (g // 2) * 16 + 16)
        wait("pool", *[n(f"gated{b}") for b in range(NB)])
        mark("pool", n("res"), pool.tensor_tensor(Y[:, :, :], Y[:, :, :], X[:, :, :], ALU.add))
        yield
        wait("dve", n("res"), o("mv3"))
        for b in range(NB):
            mark("dve", n(f"stats{b}"), dve.bn_stats(stats[:, b, :], Y[:, b, :]))
        wait("dve", o("norm3"), o("var"))
        for b in range(NB):
            wait("dve", n(f"stats{b}"))
            M.apart("dve")
            mark("dve", n(f"mv{b}"), dve.bn_aggr(mv[:, b, :], stats[:, b, :]))
        wait("dve", n("mv3"), o("rstd"))
        mark("dve", n("var"), dve.tensor_scalar(rstd[:, 0, :], mv[:, :, 1], EPS_LN, None, ALU.add))
        wait("pool", n("var"))
        mark("pool", n("rstd"), pool.tensor_tensor(rstd[:, 1, :], rstd[:, 0, :], minus_half[:, 0:NB], ALU.pow))
        yield
        wait("dve", n("rstd"), o("norm3"))
        mark("dve", n("shift"), dve.scalar_tensor_tensor(rstd[:, 2, :], mv[:, :, 0], -1.0, rstd[:, 1, :], ALU.mult, ALU.mult))
        for e in (act, dve):
            e.wait_ge(s_scatter[i2], c * (2 * NB * 16) + (g // 2) * NB * 16 + 16)
        wait("act", n("shift"), o2("rt_ps1"))
        for b in range(NB):
            mark("act", n(f"norm{b}"), act.activation(R[:, b, 0:H], Y[:, b, :], ACT.Identity, bias=rstd[:, 2, b:b + 1], scale=rstd[:, 1, b:b + 1]))
        mark("dve", n("token"), dve.tensor_copy(R[:, :, H:H + 1], token[:, g * NB:(g + 1) * NB].unsqueeze(2)))
        wait("dve", n("token"))
        mark("dve", n("next_token"), dve.tensor_scalar(token[:, g * NB:(g + 1) * NB], token[:, g * NB:(g + 1) * NB], float(P), None, ALU.add))
        yield
        for k in range(KH):
            i, bank = grab(epi, n(f"rt{k}"))
            wait("pe", n("norm3"))
            for b in range(NB):
                ins = pe.transpose(bank[:, b * P:(b + 1) * P], R[:, b, k * P:(k + 1) * P], ident[:, :])
            mark("pe", n(f"rt_ps{k}"), ins)
            wait("act", n(f"rt_ps{k}"), o("score_ps"))
            mark("act", n(f"rt{k}"), act.activation(rows_t[:, k, :], bank[:, :], ACT.Copy))
            epi.freed_by(i, n(f"rt{k}"))
        yield
        i, bank = grab(epi, n("score"))
        score = bank[:, 0:NB * NE].rearrange("p (b e) -> p b e", b=NB)
        wait("pe", n("rt0"), n("rt1"))
        for b in range(NB):
            for k in range(KH):
                ins = pe.matmul(score[:, b, :], rows_t[:, k, b * P:(b + 1) * P], w_route[:, k, :], start=k == 0, stop=k == KH - 1)
        mark("pe", n("score_ps"), ins)
        wait("dve", n("score_ps"))
        mark("dve", n("best"), dve.tensor_reduce(best[:, 0, :], score, AX.X, ALU.max))
        wait("dve", n("best"))
        mark("dve", n("is_best"), dve.tensor_tensor(pick[:, 0], score, spread(best[:, 0, :].unsqueeze(2), 2, NE), ALU.is_ge))
        epi.freed_by(i, n("is_best"))
        wait("dve", n("is_best"))
        mark("dve", n("ranked"), dve.tensor_tensor(pick[:, 1], pick[:, 0], spread(rank[:, :].unsqueeze(1), 1, NB), ALU.mult))
        wait("dve", n("ranked"))
        mark("dve", n("top"), dve.tensor_reduce(best[:, 1, :], pick[:, 1], AX.X, ALU.max))
        wait("dve", n("top"), o("pos_ps"))
        mark("dve", n("onehot"), dve.tensor_tensor(onehot[:, :, :], spread(rank[:, :].unsqueeze(1), 1, NB),
                                                   spread(best[:, 1, :].unsqueeze(2), 2, NE), ALU.is_equal))
        yield
        i, bank = grab(epi, n("pos"))
        pos = bank[:, 0:NB * NE].rearrange("p (b e) -> p b e", b=NB)
        wait("pe", n("onehot"), o("routed"))
        pe.matmul(pos, before[:, :], onehot[:, :, :], start=True, stop=False)
        for b in range(NB - 1):
            pe.matmul(pos[:, b + 1:NB, :], ones_bf[:, :], spread(onehot[:, b:b + 1, :], 1, NB - 1 - b), start=False, stop=False)
        ins = pe.matmul(pos, ones_bf[:, :], spread(routed[:, :].unsqueeze(1), 1, NB), start=False, stop=True)
        mark("pe", n("pos_ps"), ins)
        wait("dve", n("onehot"))
        mark("dve", n("total"), dve.tensor_reduce(total[:, :], onehot[:, :, :].rearrange("p b e -> p e b"), AX.X, ALU.add))
        wait("dve", n("total"), n("pos_ps"))
        mark("dve", n("routed"), dve.tensor_tensor(routed[:, :], routed[:, :], total[:, :], ALU.add))
        mark("dve", n("where0"), dve.tensor_tensor(where[:, 0], pos, spread(region0[:, :].unsqueeze(1), 1, NB), ALU.add))
        epi.freed_by(i, n("where0"))
        wait("dve", n("where0"))
        mark("dve", n("where1"), dve.tensor_tensor(where[:, 1], where[:, 0], onehot[:, :, :], ALU.mult))
        wait("dve", n("where1"))
        mark("dve", n("where_f"), dve.tensor_reduce(where_f[:, :], where[:, 1], AX.X, ALU.add))
        wait("dve", n("where_f"))
        mark("dve", n("index"), dve.tensor_copy(index[i2][:, :], where_f[:, :]))
        wait("pool", n("index"), n("norm3"), n("token"))
        M.apart("pool")
        for b in range(NB):
            pool.indirect_dma_start(sorted_rows[:, :], bass.IndirectOffsetOnAxis(index[i2][:, b:b + 1], 0), R[:, b, :], None,
                                    bounds_check=NE * REGION - 1, oob_is_err=False).then_inc(s_scatter[i2], 16)
        yield

    s_blank = sem("s_blank")
    for r in rows:
        pool.memset(r[:, :, H:ROW], 0.0).then_inc(s_blank, 1)
    dve.wait_ge(s_blank, 2)
    for j in range(2):
        lo = NE * REGION + j * (P // 2)
        pool.dma_start(sorted_rows[lo:lo + P // 2, :], v["pad_row"][j * D:(j + 1) * D, :]).then_inc(s_scatter[j], 16)

    STAGES = dict(p=(project, 0), s=(respond, 1), l=(learn, 1), r=(retrieve, 2), e=(epilogue, 3))

    def slot(c, g):
        stages = {}
        for letter, (make, lag) in STAGES.items():
            step = g - lag
            stages[letter] = make(c if step >= 0 else c - 1, step % G)
        for letter in ORDER:
            next(stages[letter])

    first = dict(e=epilogue(0, 0))
    for letters, stage in (("abcd", project), ("ijk", respond), ("lmn", learn), ("rs", retrieve)):
        first.update({letter: stage(0, g) for g, letter in enumerate(letters)})
    M.begin(0, first=True)
    for letter in HEAD_ORDER:
        next(first[letter])
    M.fill()
    with nc.Fori(1, NC) as c:
        M.begin(c)
        for s in rings:
            s.begin()
        for g in range(G):
            slot(c, g)
    body = dict(count=M.count, at=M.at, slots={s.name: (dict(s.last), dict(s.place)) for s in rings})
    M.begin(NC)
    wait("sp", f"conv_kv.{G - 1}", f"conv_q.{G - 1}")
    for k in range(KH):
        sp.dma_start(v["w_expert"][:, k, :, :], dram["w_expert"][:, k * P:(k + 1) * P, :].rearrange("e p f -> p e f")).then_inc(v["s_expert"], 16)
    last = dict(s=respond(NC - 1, 3), l=learn(NC - 1, 3), r=retrieve(NC - 1, 2), R=retrieve(NC - 1, 3),
                e=epilogue(NC - 1, 1), f=epilogue(NC - 1, 2), g=epilogue(NC - 1, 3))
    for letter in TAIL_ORDER:
        next(last[letter])
    plans["loop1"] = body
    for e in (pe, act, dve, pool, sp):
        for who, s in M.sem.items():
            e.wait_ge(s, M.per_lap[who] * NC + M.count[who])
    for s in s_scatter:
        sp.wait_ge(s, NC * 2 * NB * 16 + 16)


ORDER = "lseseppplseepprlepprlepsrpllpsereplrpep"
HEAD_ORDER = "aaaabaaabbbabilaalalblbibclaiicbilcjalmjjbbcrmdrcbmrjbcmcrcmmcjmeendkdnkcedkcnedddedsncdeskncdkdnesedsedrsn"
TAIL_ORDER = "slesserrllerlselsrlelffeffRReRfeReggfgRggfgfrfggg"


def pads(p):
    return 16 * len(range(p, NE, PAIRS))


def tile_buffers(sb):
    n_tok = sb("n_tok", [P, NE])
    pad_f = sb("pad_f", [P, NE])
    pad_i = sb("pad_i", [P, NE], I32)
    nt_i = sb("nt_i", [P, 2, NE], I32)
    nt = sb("nt", [P, NE])
    cum = sb("cum", [P, NE])
    one = sb("one", [P, NE])
    past = sb("past", [P, NT, NE])
    first = sb("first", [P, NT, NE])
    e_of = sb("e_of", [P, NT])
    f_of = sb("f_of", [P, 4, NT])
    word2_f = sb("word2_f", [P, 2, NT // 2])
    pair_rows = sb("pair_rows", [P, NT // 2], I32)
    digits = sb("digits", [P, WORDS, PAIRS])
    digit_value = sb("digit_value", [P, PAIRS])
    word_f = sb("word_f", [P, WORDS])
    lap_experts = sb("lap_experts", [P, WORDS], I32)
    return dict(locals())


def tiles(nc, ctx, sb, sem, v):
    routed, ones_bf, region0, tile_no, pad_row, lane = (
        v[n] for n in ("routed", "ones_bf", "region0", "tile_no", "pad_row", "lane"))
    banks, sorted_rows = v["banks"], v["sorted_rows"]
    pe, dve, pool = nc.tensor, nc.vector, nc.gpsimd
    s_cnt, s_d = sem("s_cnt"), sem("s_tiles")
    T = v["tile_buffers_"]
    n_tok, pad_f, pad_i, nt_i, nt, cum, one = (T[n] for n in ("n_tok", "pad_f", "pad_i", "nt_i", "nt", "cum", "one"))
    past, first, e_of, f_of, word2_f, pair_rows = (T[n] for n in ("past", "first", "e_of", "f_of", "word2_f", "pair_rows"))
    digits, digit_value, word_f, lap_experts = (T[n] for n in ("digits", "digit_value", "word_f", "lap_experts"))
    made = [0]

    def step(instruction):
        made[0] += 1
        instruction.then_inc(s_d, 1)
        dve.wait_ge(s_d, made[0])

    pe.matmul(banks[0][:, 0:NE], ones_bf[:, :], routed[:, :], start=True, stop=True).then_inc(s_cnt, 1)
    dve.wait_ge(s_cnt, 1)
    step(dve.tensor_copy(n_tok[:, :], banks[0][:, 0:NE]))
    step(dve.tensor_tensor(pad_f[:, :], n_tok[:, :], region0[:, :], ALU.add))
    step(dve.tensor_scalar(pad_f[:, :], pad_f[:, :], lane[:, 0:1], None, ALU.add))
    step(dve.tensor_copy(pad_i[:, :], pad_f[:, :]))
    pad_ready = made[0]
    step(dve.tensor_scalar(n_tok[:, :], n_tok[:, :], float(P - 1), None, ALU.add))
    step(dve.tensor_copy(nt_i[:, 0, :], n_tok[:, :]))
    step(dve.tensor_scalar(nt_i[:, 1, :], nt_i[:, 0, :], 7, None, ALU.arith_shift_right))
    step(dve.tensor_copy(nt[:, :], nt_i[:, 1, :]))
    step(dve.memset(one[:, :], 1.0))
    step(dve.tensor_tensor_scan(cum[:, :], one[:, :], nt[:, :], 0.0, ALU.mult, ALU.add))
    step(dve.tensor_tensor(past[:, :, :], spread(tile_no[:, :].unsqueeze(2), 2, NE), spread(cum[:, :].unsqueeze(1), 1, NT), ALU.is_ge))
    step(dve.tensor_reduce(e_of[:, :], past[:, :, :], AX.X, ALU.add))
    step(dve.tensor_tensor(first[:, :, :], past[:, :, :], spread(nt[:, :].unsqueeze(1), 1, NT), ALU.mult))
    step(dve.tensor_reduce(f_of[:, 0, :], first[:, :, :], AX.X, ALU.add))
    step(dve.tensor_tensor(f_of[:, 1, :], tile_no[:, :], f_of[:, 0, :], ALU.subtract))
    step(dve.tensor_scalar(f_of[:, 2, :], f_of[:, 1, :], float(P), None, ALU.mult))
    step(dve.scalar_tensor_tensor(f_of[:, 3, :], e_of[:, :], float(REGION), f_of[:, 2, :], ALU.mult, ALU.add))
    step(dve.tensor_scalar(f_of[:, 3, :], f_of[:, 3, :], float(NE * REGION), None, ALU.min))
    row2 = f_of[:, 3, :].rearrange("p (j i) -> p j i", i=2)
    step(dve.tensor_scalar(word2_f[:, 0, :], row2[:, :, 0], 1.0 / P, None, ALU.mult))
    step(dve.scalar_tensor_tensor(word2_f[:, 1, :], row2[:, :, 1], float(TILE_CODES) / P, word2_f[:, 0, :], ALU.mult, ALU.add))
    step(dve.tensor_copy(pair_rows[:, :], word2_f[:, 1, :]))
    step(dve.memset(digits[:, :, :], 0.0))
    for j in range(PAIRS):
        step(dve.memset(digit_value[:, j:j + 1], float(NE ** j)))
    flat = digits[:, :, :].rearrange("p l j -> p (l j)")
    step(dve.tensor_scalar(flat[:, 2 * MIDDLE_LAG:NT + 2 * MIDDLE_LAG], e_of[:, :], float(NE - 1), None, ALU.min))
    step(dve.tensor_tensor(digits[:, :, :], digits[:, :, :], spread(digit_value[:, :].unsqueeze(1), 1, WORDS), ALU.mult))
    step(dve.tensor_reduce(word_f[:, :], digits[:, :, :], AX.X, ALU.add))
    step(dve.tensor_copy(lap_experts[:, :], word_f[:, :]))
    pool.wait_ge(s_d, pad_ready)
    for e in range(NE):
        pool.indirect_dma_start(sorted_rows[:, :], bass.IndirectOffsetOnAxis(pad_i[:, e:e + 1], 0), pad_row[:, :], None,
                                bounds_check=NE * REGION - 1, oob_is_err=False).then_inc(v["s_out"][e % PAIRS], 16)
    for e in (nc.tensor, nc.sync):
        e.wait_ge(s_d, made[0])
    for p, s in enumerate(v["s_out"]):
        nc.sync.wait_ge(s, pads(p))
    return pair_rows, lap_experts


def loop2(nc, ctx, sb, sem, v, plan, plans):
    banks, sorted_rows, out, ident, w_expert, eps_ln = (
        v[n] for n in ("banks", "sorted_rows", "out", "ident", "w_expert", "eps_ln"))
    pair_rows, lap_experts = v["pair_rows"], v["lap_experts"]
    pe, act, dve, pool, sp = nc.tensor, nc.scalar, nc.vector, nc.gpsimd, nc.sync
    M = Marks(nc, ctx, "l2", plan)
    mark, wait = M.mark, M.wait

    def pairs(name, shape, dt=F32):
        return [sb(f"{name}{p}", shape, dt) for p in range(PAIRS)]

    xs = pairs("xs", [P, 2, ROW])
    xs_t = pairs("xs_t", [P, 2, KH, P])
    ys = pairs("ys", [P, 2, H])
    os_ = pairs("os", [P, 2, H])
    st = pairs("st", [P, 2, 6])
    mvs = pairs("mvs", [P, 2, 2])
    rs = pairs("rs", [P, 3, 2])
    tok = pairs("tok", [P, 2], I32)
    s_row = [sem(f"s_row{p}") for p in range(PAIRS)]
    s_out = v["s_out"]

    act.activation(rs[0][:, 0, 0:1], eps_ln[:, :], ACT.Sqrt)
    pe.wait_ge(v["s_expert"], 16 * KH)

    def front(lap, p):
        n = lambda name: f"{name}.{p}"
        wait("sp", n("ys"), n("tok"))
        M.apart("sp")
        word = sp.value_load(pair_rows[0:1, bass.ds(lap * PAIRS + p, 1)], min_val=0, max_val=LAST_TILE * (TILE_CODES + 1))
        for i, code in enumerate((word & (TILE_CODES - 1), word >> (TILE_CODES.bit_length() - 1))):
            row = code.with_bounds(min_val=0, max_val=LAST_TILE) * P
            sp.dma_start(xs[p][:, i, :], sorted_rows[bass.ds(row, P), :]).then_inc(s_row[p], 16)
        pe.wait_ge(s_row[p], lap * 32 + 32)
        wait("pe", f"xt.{(p - PAIR_BANKS) % PAIRS}")
        bank = banks[p % PAIR_BANKS]
        for i in range(2):
            for k in range(KH):
                ins = pe.transpose(bank[:, (i * KH + k) * P:(i * KH + k + 1) * P], xs[p][:, i, k * P:(k + 1) * P], ident[:, :])
        mark("pe", n("tr"), ins)
        wait("act", n("tr"), n("mm"))
        mark("act", n("xt"), act.activation(xs_t[p][:, :, :, :].rearrange("p i k t -> p (i k t)"), bank[:, :], ACT.Copy))

    def middle(lap, p):
        n = lambda name: f"{name}.{p}"
        bank = banks[PAIR_BANKS + p % PAIR_BANKS][:, :].rearrange("p (i f) -> p i f", i=2)
        wait("pe", n("xt"), f"ys.{(p - PAIR_BANKS) % PAIRS}")
        for i in range(2):
            for k in range(KH):
                ins = pe.matmul(bank[:, i, :], xs_t[p][:, i, k, :], w_expert[:, k, bass.ds(expert[p, i], 1), :], start=k == 0, stop=k == KH - 1)
        mark("pe", n("mm"), ins)
        dve.wait_ge(s_row[p], lap * 32 + 32)
        wait("dve", n("mm"), n("os"))
        mark("dve", n("ys"), dve.scalar_tensor_tensor(ys[p][:, :, :], xs[p][:, :, 0:H], 2.0, bank, ALU.mult, ALU.add))
        dve.wait_ge(s_out[p], lap * 32 + pads(p))
        mark("dve", n("tok"), dve.tensor_copy(tok[p][:, :], xs[p][:, :, H]))
        wait("dve", n("ys"))
        for i in range(2):
            mark("dve", n(f"st{i}"), dve.bn_stats(st[p][:, i, :], ys[p][:, i, :]))
        for i in range(2):
            wait("dve", n(f"st{i}"))
            M.apart("dve")
            mark("dve", n(f"mv{i}"), dve.bn_aggr(mvs[p][:, i, :], st[p][:, i, :]))

    def scale(lap, p):
        n = lambda name: f"{name}.{p}"
        wait("act", n("mv1"), n("rs"))
        mark("act", n("dev"), act.activation(rs[p][:, 0, :], mvs[p][:, :, 1], ACT.Sqrt, bias=eps_ln[:, 0:1], scale=1.0))
        wait("dve", n("dev"), n("os"))
        mark("dve", n("rs"), dve.reciprocal(rs[p][:, 1, :], rs[p][:, 0, :]))
        wait("dve", n("rs"))
        mark("dve", n("shift"), dve.scalar_tensor_tensor(rs[p][:, 2, :], mvs[p][:, :, 0], -1.0, rs[p][:, 1, :], ALU.mult, ALU.mult))

    def back(lap, p):
        n = lambda name: f"{name}.{p}"
        act.wait_ge(s_out[p], lap * 32 + pads(p))
        wait("act", n("shift"))
        for i in range(2):
            ins = act.activation(os_[p][:, i, :], ys[p][:, i, :], ACT.Identity, bias=rs[p][:, 2, i:i + 1], scale=rs[p][:, 1, i:i + 1])
        mark("act", n("os"), ins)
        wait("pool", n("os"), n("tok"))
        M.apart("pool")
        for i in range(2):
            pool.indirect_dma_start(out[:, :], bass.IndirectOffsetOnAxis(tok[p][:, i:i + 1], 0), os_[p][:, i, :], None,
                                    bounds_check=TOK - 1, oob_is_err=False).then_inc(s_out[p], 16)

    STAGES = ((front, 0), (scale, 3), (middle, MIDDLE_LAG), (back, 3))
    expert = {}

    def experts(lap):
        words = [pe.value_load(lap_experts[0:1, bass.ds(lap * 2 + h, 1)], min_val=0, max_val=NE ** PAIRS - 1) for h in range(2)]
        for j in range(2 * PAIRS):
            expert[(j // 2 - MIDDLE_LAG) % PAIRS, j % 2] = (words[j // PAIRS] >> (3 * (j % PAIRS))) & (NE - 1)

    def slot(lap, p, first=False, tail=False):
        for stage, lag in STAGES:
            step = p - lag
            if (tail and step >= 0) or (first and step < 0):
                continue
            stage(lap if step >= 0 else lap - 1, step % PAIRS)

    M.begin(0, first=True)
    experts(0)
    for p in range(PAIRS):
        slot(0, p, first=True)
    M.fill()
    with nc.Fori(1, LAPS) as lap:
        M.begin(lap)
        experts(lap)
        for p in range(PAIRS):
            slot(lap, p)
    plans["loop2"] = dict(count=M.count, at=M.at, slots={})
    M.begin(LAPS)
    experts(LAPS)
    for p in range(max(lag for _, lag in STAGES)):
        slot(LAPS, p, tail=True)
    for p, s in enumerate(s_out):
        sp.wait_ge(s, 32 * LAPS + pads(p))


INPUTS = dict(hidden=[NC, G, P, NB, H], hidden_t=[NC, G, P, KH, NB * P], w_kv=[H, P], w_q=[H, P], w_ae=[H, P], w_gt=[H, H + D], bias_gt=[P, H + D],
              norm_g=[P, H], w_o=[D, H], conv_w=[P, 2, 4], conv_b=[P, 2], bias_ae=[P, 1], w_route=[H, NE],
              state0=[D, NB, 3, D], w2_0=[D, NB, D], w_expert=[NE, H, H])


def program(nc, plan):
    dram = {n: nc.dram_tensor(f"in_{n}", s, F32, kind="ExternalInput").ap() for n, s in INPUTS.items()}
    dram["out"] = nc.dram_tensor("out_0", [TOK, H], F32, kind="ExternalOutput").ap()
    return build(nc, dram, plan)


def kernel(**inputs):
    import numpy as np
    import concourse.bacc as bacc
    from concourse.bass_utils import run_bass_kernel_spmd

    a = {k.split("_", 2)[2]: np.asarray(w) for k, w in inputs.items()}
    rows = lambda w: np.broadcast_to(w[None, :], (P, w.shape[0]))
    arrays = dict(
        hidden=a["hidden"].reshape(G, NB, NC, P, H).transpose(2, 0, 3, 1, 4),
        hidden_t=a["hidden"].reshape(G, NB, NC, P, KH, P).transpose(2, 0, 5, 4, 1, 3).reshape(NC, G, P, KH, NB * P),
        w_kv=np.concatenate([a["Wk"], a["Wv"]]).T,
        w_q=np.concatenate([a["Wq"], a["Wq"]]).T,
        w_ae=np.concatenate([a["aW"], a["eW"]]).T,
        w_gt=np.concatenate([a["gW"], a["tW"]]).T,
        bias_gt=rows(np.concatenate([a["gb"], a["tb"]])),
        norm_g=rows(a["norm_g"]),
        w_o=a["Wo"].T,
        conv_w=np.stack([np.concatenate([a["ckw"], a["cvw"]]), np.concatenate([a["cqw"], a["cqw"]])], 1),
        conv_b=np.stack([np.concatenate([a["ckb"], a["cvb"]]), np.concatenate([a["cqb"], a["cqb"]])], 1),
        bias_ae=np.concatenate([a["ab"], a["eb"]])[:, None],
        w_route=a["gate_w"].T,
        state0=np.broadcast_to(np.stack([a["mW1"].T, a["mW1"].T, a["mW2"].T], 1)[:, None], (D, NB, 3, D)),
        w2_0=np.broadcast_to(a["mW2"][:, None], (D, NB, D)),
        w_expert=a["expert_w"].transpose(0, 2, 1),
    )
    plan = program(bacc.Bacc("TRN2", target_bir_lowering=False, num_devices=1), None)
    nc = bacc.Bacc("TRN2", target_bir_lowering=False, num_devices=1)
    program(nc, plan)
    feed = {f"in_{n}": np.ascontiguousarray(w) for n, w in arrays.items()}
    r = run_bass_kernel_spmd(nc, [feed], core_ids=[0])
    return r.results[0]["out_0"].reshape(B, S, H)
```
